# Optimizing a Trainium2 kernel written in Bass

```python
import numpy as np
import jax
import jax.numpy as jnp

def _softmax(x, axis=-1):
    return jax.nn.softmax(x, axis=axis)

def _gelu(x):
    return jax.nn.gelu(x, approximate=True)

def _silu(x):
    return jax.nn.silu(x)

def _sigmoid(x):
    return jax.nn.sigmoid(x)

def _layernorm(x, axis=-1, eps=1e-05):
    m = jnp.mean(x, axis=axis, keepdims=True)
    v = jnp.var(x, axis=axis, keepdims=True)
    return (x - m) / jnp.sqrt(v + eps)

def _scatter_add(tgt, idx, src, axis=0):
    return tgt.at[idx].add(src)

def _segment_sum(src, seg, n):
    return jax.ops.segment_sum(src, seg, n)
kernel_name = 'mk_vit_tower_d2_tok_img768_r4_a6e4ff'

def setup_inputs(seed: int=0):
    np.random.seed(seed)
    _w = jnp.asarray

    def _rec_inputs():
        import jax
        import jax.numpy as jnp
        _rk = jax.random.key(seed)
        x = -0.000356955 + 1 * jax.random.normal(jax.random.fold_in(_rk, 1), (32, 3, 96, 96), jnp.float32)
        return x
    x = _rec_inputs()

    def _L0_tok_setup():
        import jax, jax.numpy as jnp
        import numpy as np
        PATCH = 16
        key = jax.random.key(seed)
        k1, k2, k3 = jax.random.split(key, 3)
        x = jax.random.normal(k1, (128, 3, 224, 224), dtype=jnp.float32)
        W = jax.random.normal(k2, (192, 3, PATCH, PATCH), dtype=jnp.float32) * 0.02
        b = jax.random.normal(k3, (192,), dtype=jnp.float32) * 0.02
        return {'x': x, 'W': W, 'b': b}
    _L0_tok_all = _L0_tok_setup()
    _L0_tok_in = {k: v for k, v in _L0_tok_all.items() if k in ('W', 'b')}
    del _L0_tok_all

    def _L0_attn_setup():
        import jax, jax.numpy as jnp
        import numpy as np
        EMBED_DIM = 192
        NUM_HEADS = 12
        HEAD_DIM = EMBED_DIM // NUM_HEADS
        MAX_REL = 14
        TABLE_ROWS = 2 * MAX_REL + 2

        def rel_pos_indices(N, max_rel):
            L = N - 1
            s = int(L ** 0.5)
            r = np.arange(L)
            dv = r[None, :] // s - r[:, None] // s
            dh = r[None, :] % s - r[:, None] % s
            fv = np.clip(dv, -max_rel, max_rel) + max_rel + 1
            fh = np.clip(dh, -max_rel, max_rel) + max_rel + 1
            fv = np.pad(fv, ((1, 0), (1, 0)), constant_values=0)
            fh = np.pad(fh, ((1, 0), (1, 0)), constant_values=0)
            return (jnp.asarray(fv, jnp.int32), jnp.asarray(fh, jnp.int32))
        key = jax.random.key(seed)
        ks = jax.random.split(key, 8)
        C = EMBED_DIM
        x = jax.random.normal(ks[0], (64, 197, C), dtype=jnp.float32)
        w_qkv = jax.random.normal(ks[1], (C, 3 * C), dtype=jnp.float32) * 0.02
        tab_vk = jax.random.normal(ks[2], (TABLE_ROWS, HEAD_DIM), dtype=jnp.float32) * 0.02
        tab_hk = jax.random.normal(ks[3], (TABLE_ROWS, HEAD_DIM), dtype=jnp.float32) * 0.02
        tab_vv = jax.random.normal(ks[4], (TABLE_ROWS, HEAD_DIM), dtype=jnp.float32) * 0.02
        tab_hv = jax.random.normal(ks[5], (TABLE_ROWS, HEAD_DIM), dtype=jnp.float32) * 0.02
        w_proj = jax.random.normal(ks[6], (C, C), dtype=jnp.float32) * 0.02
        b_proj = jnp.zeros((C,), dtype=jnp.float32)
        return {'x': x, 'w_qkv': w_qkv, 'tab_vk': tab_vk, 'tab_hk': tab_hk, 'tab_vv': tab_vv, 'tab_hv': tab_hv, 'w_proj': w_proj, 'b_proj': b_proj}
    _L0_attn_all = _L0_attn_setup()
    _L0_attn_in = {k: v for k, v in _L0_attn_all.items() if k in ('w_qkv', 'tab_vk', 'tab_hk', 'tab_vv', 'tab_hv', 'w_proj', 'b_proj')}
    del _L0_attn_all

    def _L0_ffn_setup():
        import jax, jax.numpy as jnp
        import numpy as np
        B, T, D = (2, 512, 192)
        S, R, M, K = (8, 16, 64, 4)
        H, G = (32, 64)

        def _ssinf3(x, P, C, W1, b1, W2, b2, G1, g1b, G2, g2b):
            shp = x.shape
            xf = x.reshape(-1, shp[-1])
            z = jnp.einsum('nd,sdr->nsr', xf, P)
            scores = jnp.einsum('nsr,smr->nsm', z, C)
            topv, topi = jax.lax.top_k(scores, K)
            w = jax.nn.softmax(topv, axis=-1)
            sidx = jnp.arange(S)[None, :, None]
            W1g = W1[sidx, topi]
            b1g = b1[sidx, topi]
            W2g = W2[sidx, topi]
            b2g = b2[sidx, topi]
            h = jax.nn.gelu(jnp.einsum('nsr,nskrh->nskh', z, W1g) + b1g)
            yl = jnp.einsum('nskh,nskhr->nskr', h, W2g) + b2g
            comb = jnp.einsum('nskr,nsk->nsr', yl, w)
            comb = comb.reshape(xf.shape[0], S * R)
            out = jax.nn.gelu(comb @ G1 + g1b) @ G2 + g2b
            return out.reshape(shp)
        key = jax.random.key(seed)
        k = jax.random.split(key, 8)
        rn = lambda kk, shape, s: jax.random.normal(kk, shape, dtype=jnp.float32) * s
        return {'x': rn(k[0], (B, T, D), 1.0), 'P': rn(k[1], (S, D, R), D ** (-0.5)), 'C': rn(k[2], (S, M, R), R ** (-0.5)), 'W1': rn(k[3], (S, M, R, H), R ** (-0.5)), 'b1': jnp.zeros((S, M, H), jnp.float32), 'W2': rn(k[4], (S, M, H, R), H ** (-0.5)), 'b2': jnp.zeros((S, M, R), jnp.float32), 'G1': rn(k[5], (S * R, G), (S * R) ** (-0.5)), 'g1b': jnp.zeros((G,), jnp.float32), 'G2': rn(k[6], (G, D), G ** (-0.5)), 'g2b': jnp.zeros((D,), jnp.float32)}
    _L0_ffn_all = _L0_ffn_setup()
    _L0_ffn_in = {k: v for k, v in _L0_ffn_all.items() if k in ('P', 'C', 'W1', 'b1', 'W2', 'b2', 'G1', 'g1b', 'G2', 'g2b')}
    del _L0_ffn_all

    def _L1_attn_setup():
        import jax, jax.numpy as jnp
        import numpy as np
        N_HEAD = 12
        N_EMBD = 192
        BLOCK = 512
        THETA = 10000.0

        def _rope_tables(head_dim, end, theta=THETA):
            half = head_dim // 2
            freqs = 1.0 / theta ** (jnp.arange(0, head_dim, 2, dtype=jnp.float32) / head_dim)
            t = jnp.arange(end, dtype=jnp.float32)
            ang = jnp.outer(t, freqs)
            return (jnp.cos(ang), jnp.sin(ang))

        def _apply_rope(x, cos, sin):
            B, H, T, hd = x.shape
            xr = x.reshape(B, H, T, hd // 2, 2)
            x0, x1 = (xr[..., 0], xr[..., 1])
            c = cos[None, None, :T, :]
            s = sin[None, None, :T, :]
            o0 = x0 * c - x1 * s
            o1 = x0 * s + x1 * c
            return jnp.stack([o0, o1], axis=-1).reshape(B, H, T, hd)
        key = jax.random.key(seed)
        ks = jax.random.split(key, 9)
        B, T, C = (2, 512, N_EMBD)
        std = 0.02
        return {'x': jax.random.normal(ks[0], (B, T, C), jnp.float32), 'norm_scale': jnp.ones((C,), jnp.float32), 'norm_bias': jnp.zeros((C,), jnp.float32), 'W_attn': jax.random.normal(ks[1], (C, 3 * C), jnp.float32) * std, 'b_attn': jax.random.normal(ks[2], (3 * C,), jnp.float32) * std, 'W_proj': jax.random.normal(ks[3], (C, C), jnp.float32) * std, 'b_proj': jax.random.normal(ks[4], (C,), jnp.float32) * std, 'sinks': jax.random.normal(ks[5], (N_HEAD,), jnp.float32) * 0.5, 'rezero': jax.random.normal(ks[6], (1,), jnp.float32) * 0.1}
    _L1_attn_all = _L1_attn_setup()
    _L1_attn_in = {k: v for k, v in _L1_attn_all.items() if k in ('norm_scale', 'norm_bias', 'W_attn', 'b_attn', 'W_proj', 'b_proj', 'sinks', 'rezero')}
    del _L1_attn_all

    def _L1_ffn_setup():
        import jax, jax.numpy as jnp
        import numpy as np
        EPS_NORM = 1e-06
        EPS_Q = 1e-05

        def rmsnorm(x, g):
            return x * jax.lax.rsqrt(jnp.mean(x * x, axis=-1, keepdims=True) + EPS_NORM) * g

        def activation_quant(x):
            scale = 127.0 / jnp.maximum(jnp.max(jnp.abs(x), axis=-1, keepdims=True), EPS_Q)
            return jnp.clip(jnp.round(x * scale), -128, 127) / scale

        def weight_quant(w):
            scale = 1.0 / jnp.maximum(jnp.mean(jnp.abs(w)), EPS_Q)
            return jnp.clip(jnp.round(w * scale), -1, 1) / scale

        def bitlinear(x, w, g):
            x_norm = rmsnorm(x, g)
            x_q = x_norm + jax.lax.stop_gradient(activation_quant(x_norm) - x_norm)
            w_q = w + jax.lax.stop_gradient(weight_quant(w) - w)
            return jnp.einsum('bsd,od->bso', x_q, w_q)
        key = jax.random.key(seed)
        k1, k2, k3 = jax.random.split(key, 3)
        B, S, D, H = (8, 1024, 192, 512)
        x = jax.random.normal(k1, (B, S, D), dtype=jnp.float32)
        w_in = jax.random.normal(k2, (2 * H, D), dtype=jnp.float32) * 0.002
        w_out = jax.random.normal(k3, (D, H), dtype=jnp.float32) * 0.002
        g_in = jnp.ones((D,), dtype=jnp.float32)
        g_out = jnp.ones((H,), dtype=jnp.float32)
        return {'x': x, 'w_in': w_in, 'g_in': g_in, 'w_out': w_out, 'g_out': g_out}
    _L1_ffn_all = _L1_ffn_setup()
    _L1_ffn_in = {k: v for k, v in _L1_ffn_all.items() if k in ('w_in', 'g_in', 'w_out', 'g_out')}
    del _L1_ffn_all
    return {'x': x, 'L0_tok_W': _L0_tok_in['W'], 'L0_tok_b': _L0_tok_in['b'], 'L0_attn_w_qkv': _L0_attn_in['w_qkv'], 'L0_attn_tab_vk': _L0_attn_in['tab_vk'], 'L0_attn_tab_hk': _L0_attn_in['tab_hk'], 'L0_attn_tab_vv': _L0_attn_in['tab_vv'], 'L0_attn_tab_hv': _L0_attn_in['tab_hv'], 'L0_attn_w_proj': _L0_attn_in['w_proj'], 'L0_attn_b_proj': _L0_attn_in['b_proj'], 'L0_ffn_P': _L0_ffn_in['P'], 'L0_ffn_C': _L0_ffn_in['C'], 'L0_ffn_W1': _L0_ffn_in['W1'], 'L0_ffn_b1': _L0_ffn_in['b1'], 'L0_ffn_W2': _L0_ffn_in['W2'], 'L0_ffn_b2': _L0_ffn_in['b2'], 'L0_ffn_G1': _L0_ffn_in['G1'], 'L0_ffn_g1b': _L0_ffn_in['g1b'], 'L0_ffn_G2': _L0_ffn_in['G2'], 'L0_ffn_g2b': _L0_ffn_in['g2b'], 'L1_attn_norm_scale': _L1_attn_in['norm_scale'], 'L1_attn_norm_bias': _L1_attn_in['norm_bias'], 'L1_attn_W_attn': _L1_attn_in['W_attn'], 'L1_attn_b_attn': _L1_attn_in['b_attn'], 'L1_attn_W_proj': _L1_attn_in['W_proj'], 'L1_attn_b_proj': _L1_attn_in['b_proj'], 'L1_attn_sinks': _L1_attn_in['sinks'], 'L1_attn_rezero': _L1_attn_in['rezero'], 'L1_ffn_w_in': _L1_ffn_in['w_in'], 'L1_ffn_g_in': _L1_ffn_in['g_in'], 'L1_ffn_w_out': _L1_ffn_in['w_out'], 'L1_ffn_g_out': _L1_ffn_in['g_out']}

def reference(x, L0_tok_W, L0_tok_b, L0_attn_w_qkv, L0_attn_tab_vk, L0_attn_tab_hk, L0_attn_tab_vv, L0_attn_tab_hv, L0_attn_w_proj, L0_attn_b_proj, L0_ffn_P, L0_ffn_C, L0_ffn_W1, L0_ffn_b1, L0_ffn_W2, L0_ffn_b2, L0_ffn_G1, L0_ffn_g1b, L0_ffn_G2, L0_ffn_g2b, L1_attn_norm_scale, L1_attn_norm_bias, L1_attn_W_attn, L1_attn_b_attn, L1_attn_W_proj, L1_attn_b_proj, L1_attn_sinks, L1_attn_rezero, L1_ffn_w_in, L1_ffn_g_in, L1_ffn_w_out, L1_ffn_g_out):
    import jax
    import jax.numpy as jnp

    def _L0_tok_ref(x, W, b):
        import jax, jax.numpy as jnp
        import numpy as np
        PATCH = 16
        B, C, H, Wd = x.shape
        E = W.shape[0]
        p = PATCH
        xp = x.reshape(B, C, H // p, p, Wd // p, p)
        out = jnp.einsum('bchpwq,ecpq->bhwe', xp, W) + b
        return out.reshape(B, H // p * (Wd // p), E)

    def _L0_attn_ref(x, w_qkv, tab_vk, tab_hk, tab_vv, tab_hv, w_proj, b_proj):
        import jax, jax.numpy as jnp
        import numpy as np
        EMBED_DIM = 192
        NUM_HEADS = 12
        HEAD_DIM = EMBED_DIM // NUM_HEADS
        MAX_REL = 14
        TABLE_ROWS = 2 * MAX_REL + 2

        def rel_pos_indices(N, max_rel):
            L = N - 1
            s = int(L ** 0.5)
            r = np.arange(L)
            dv = r[None, :] // s - r[:, None] // s
            dh = r[None, :] % s - r[:, None] % s
            fv = np.clip(dv, -max_rel, max_rel) + max_rel + 1
            fh = np.clip(dh, -max_rel, max_rel) + max_rel + 1
            fv = np.pad(fv, ((1, 0), (1, 0)), constant_values=0)
            fh = np.pad(fh, ((1, 0), (1, 0)), constant_values=0)
            return (jnp.asarray(fv, jnp.int32), jnp.asarray(fh, jnp.int32))
        B, N, C = x.shape
        H, hd = (NUM_HEADS, C // NUM_HEADS)
        scale = hd ** (-0.5)
        idx_v, idx_h = rel_pos_indices(N, MAX_REL)
        emb_k = tab_vk[idx_v] + tab_hk[idx_h]
        emb_v = tab_vv[idx_v] + tab_hv[idx_h]
        qkv = (x @ w_qkv).reshape(B, N, 3, H, hd)
        q = qkv[:, :, 0].transpose(0, 2, 1, 3)
        k = qkv[:, :, 1].transpose(0, 2, 1, 3)
        v = qkv[:, :, 2].transpose(0, 2, 1, 3)
        attn = jnp.einsum('bhqd,bhkd->bhqk', q, k) * scale
        attn = attn + jnp.einsum('bhqd,qkd->bhqk', q, emb_k) * scale
        attn = jax.nn.softmax(attn, axis=-1)
        out = jnp.einsum('bhqk,bhkd->bhqd', attn, v)
        out = out + jnp.einsum('bhqk,qkd->bhqd', attn, emb_v)
        out = out.transpose(0, 2, 1, 3).reshape(B, N, C)
        return out @ w_proj + b_proj

    def _L0_ffn_ref(x, P, C, W1, b1, W2, b2, G1, g1b, G2, g2b):
        import jax, jax.numpy as jnp
        import numpy as np
        B, T, D = (2, 512, 192)
        S, R, M, K = (8, 16, 64, 4)
        H, G = (32, 64)

        def _ssinf3(x, P, C, W1, b1, W2, b2, G1, g1b, G2, g2b):
            shp = x.shape
            xf = x.reshape(-1, shp[-1])
            z = jnp.einsum('nd,sdr->nsr', xf, P)
            scores = jnp.einsum('nsr,smr->nsm', z, C)
            topv, topi = jax.lax.top_k(scores, K)
            w = jax.nn.softmax(topv, axis=-1)
            sidx = jnp.arange(S)[None, :, None]
            W1g = W1[sidx, topi]
            b1g = b1[sidx, topi]
            W2g = W2[sidx, topi]
            b2g = b2[sidx, topi]
            h = jax.nn.gelu(jnp.einsum('nsr,nskrh->nskh', z, W1g) + b1g)
            yl = jnp.einsum('nskh,nskhr->nskr', h, W2g) + b2g
            comb = jnp.einsum('nskr,nsk->nsr', yl, w)
            comb = comb.reshape(xf.shape[0], S * R)
            out = jax.nn.gelu(comb @ G1 + g1b) @ G2 + g2b
            return out.reshape(shp)
        return _ssinf3(x, P, C, W1, b1, W2, b2, G1, g1b, G2, g2b)

    def _L1_attn_ref(x, norm_scale, norm_bias, W_attn, b_attn, W_proj, b_proj, sinks, rezero):
        import jax, jax.numpy as jnp
        import numpy as np
        N_HEAD = 12
        N_EMBD = 192
        BLOCK = 512
        THETA = 10000.0

        def _rope_tables(head_dim, end, theta=THETA):
            half = head_dim // 2
            freqs = 1.0 / theta ** (jnp.arange(0, head_dim, 2, dtype=jnp.float32) / head_dim)
            t = jnp.arange(end, dtype=jnp.float32)
            ang = jnp.outer(t, freqs)
            return (jnp.cos(ang), jnp.sin(ang))

        def _apply_rope(x, cos, sin):
            B, H, T, hd = x.shape
            xr = x.reshape(B, H, T, hd // 2, 2)
            x0, x1 = (xr[..., 0], xr[..., 1])
            c = cos[None, None, :T, :]
            s = sin[None, None, :T, :]
            o0 = x0 * c - x1 * s
            o1 = x0 * s + x1 * c
            return jnp.stack([o0, o1], axis=-1).reshape(B, H, T, hd)
        B, T, C = x.shape
        H = N_HEAD
        hd = C // H
        xn = norm_scale * x + norm_bias
        qkv = xn @ W_attn + b_attn
        q, k, v = jnp.split(qkv, 3, axis=-1)
        q = q.reshape(B, T, H, hd).transpose(0, 2, 1, 3)
        k = k.reshape(B, T, H, hd).transpose(0, 2, 1, 3)
        v = v.reshape(B, T, H, hd).transpose(0, 2, 1, 3)
        cos, sin = _rope_tables(hd, T)
        q = _apply_rope(q, cos, sin)
        k = _apply_rope(k, cos, sin)
        scale = 1.0 / jnp.sqrt(jnp.float32(hd))
        att = jnp.einsum('bhqd,bhkd->bhqk', q, k) * scale
        causal = jnp.tril(jnp.ones((T, T), dtype=bool))
        att = jnp.where(causal[None, None], att, -jnp.inf)
        sink_col = jnp.broadcast_to(sinks.reshape(1, H, 1, 1), (B, H, T, 1))
        att = jnp.concatenate([sink_col, att], axis=-1)
        att = jax.nn.softmax(att, axis=-1)[..., 1:]
        y = jnp.einsum('bhqk,bhkd->bhqd', att, v)
        y = y.transpose(0, 2, 1, 3).reshape(B, T, C)
        y = (y @ W_proj + b_proj) * rezero
        return y

    def _L1_ffn_ref(x, w_in, g_in, w_out, g_out):
        import jax, jax.numpy as jnp
        import numpy as np
        EPS_NORM = 1e-06
        EPS_Q = 1e-05

        def rmsnorm(x, g):
            return x * jax.lax.rsqrt(jnp.mean(x * x, axis=-1, keepdims=True) + EPS_NORM) * g

        def activation_quant(x):
            scale = 127.0 / jnp.maximum(jnp.max(jnp.abs(x), axis=-1, keepdims=True), EPS_Q)
            return jnp.clip(jnp.round(x * scale), -128, 127) / scale

        def weight_quant(w):
            scale = 1.0 / jnp.maximum(jnp.mean(jnp.abs(w)), EPS_Q)
            return jnp.clip(jnp.round(w * scale), -1, 1) / scale

        def bitlinear(x, w, g):
            x_norm = rmsnorm(x, g)
            x_q = x_norm + jax.lax.stop_gradient(activation_quant(x_norm) - x_norm)
            w_q = w + jax.lax.stop_gradient(weight_quant(w) - w)
            return jnp.einsum('bsd,od->bso', x_q, w_q)
        h = bitlinear(x, w_in, g_in)
        up, gate = jnp.split(h, 2, axis=-1)
        y = jax.nn.silu(gate) * up
        return bitlinear(y, w_out, g_out)
    h = _L0_tok_ref(x, L0_tok_W, L0_tok_b)
    h = h + _L0_attn_ref(_layernorm(h, axis=-1), L0_attn_w_qkv, L0_attn_tab_vk, L0_attn_tab_hk, L0_attn_tab_vv, L0_attn_tab_hv, L0_attn_w_proj, L0_attn_b_proj)
    h = h + _L0_ffn_ref(_layernorm(h, axis=-1), L0_ffn_P, L0_ffn_C, L0_ffn_W1, L0_ffn_b1, L0_ffn_W2, L0_ffn_b2, L0_ffn_G1, L0_ffn_g1b, L0_ffn_G2, L0_ffn_g2b)
    h = h + _L1_attn_ref(_layernorm(h, axis=-1), L1_attn_norm_scale, L1_attn_norm_bias, L1_attn_W_attn, L1_attn_b_attn, L1_attn_W_proj, L1_attn_b_proj, L1_attn_sinks, L1_attn_rezero)
    h = h + _L1_ffn_ref(_layernorm(h, axis=-1), L1_ffn_w_in, L1_ffn_g_in, L1_ffn_w_out, L1_ffn_g_out)
    return h

_drawn_inputs = setup_inputs


def setup_inputs(seed=0):
    import zlib

    import numpy as np

    out = dict(_drawn_inputs(seed))
    spreads = {'L0_attn_b_proj': (0.0, 0.1),
     'L0_ffn_b1': (0.0, 0.1),
     'L0_ffn_b2': (0.0, 0.1),
     'L0_ffn_g1b': (0.0, 0.1),
     'L0_ffn_g2b': (0.0, 0.1),
     'L1_attn_norm_scale': (1.0, 0.6),
     'L1_attn_norm_bias': (0.0, 0.8),
     'L1_ffn_g_in': (1.0, 0.6),
     'L1_ffn_g_out': (1.0, 0.6)}
    factors = {'L0_attn_tab_vk': 24.944,
     'L0_attn_tab_hk': 23.335,
     'L0_attn_tab_vv': 3.593,
     'L0_attn_tab_hv': 3.272,
     'L1_attn_W_attn': 8.0,
     'L1_attn_b_attn': 8.0,
     'L1_attn_W_proj': 8.0,
     'L1_attn_b_proj': 25.654,
     'L1_attn_sinks': 8.0,
     'L1_ffn_w_in': 6.088,
     'L1_ffn_w_out': 6.086}
    for name, (base, spread) in spreads.items():
        noise = np.random.default_rng([zlib.crc32(name.encode()), seed]).standard_normal(out[name].shape)
        drawn = base * np.exp(spread * noise) if base else spread * noise
        out[name] = jnp.asarray(drawn.astype(out[name].dtype))
    for name, factor in factors.items():
        out[name] = (out[name] * factor).astype(out[name].dtype)
    return out
```

```python
import concourse.bass as bass
from concourse import mybir
from contextlib import ExitStack

F32, BF16 = mybir.dt.float32, mybir.dt.bfloat16
ACT, ALU, AX = mybir.ActivationFunctionType, mybir.AluOpType, mybir.AxisListType

IMAGES, SIDE, PATCH = 32, 96, 16
GRID = SIDE // PATCH
TOK = GRID * GRID
E = 192
EC = E // 2
HEADS, HD = 12, 16
HG = HEADS // 4
PER = 3
GROUPS = -(-IMAGES // PER)
GT = PER * TOK
IMG_P = GROUPS * PER
NT = IMG_P * TOK
BL = 3
BN = NT // BL
BIMG = BN // TOK
PK = 3 * PATCH * PATCH // 128
ROWS, COLS = 7, 5
S_, R_, M_, H_, TOPK, G_ = 8, 16, 64, 32, 4, 64
CH = M_ * H_ // 128
FF = 512
LN_EPS, RMS_EPS, Q_EPS = 1e-5, 1e-6, 1e-5
NEG, TAKEN, SENTINEL = -1e30, -1e38, -3e38
ROUND = 1.5 * 2.0 ** 23


def spread(ap, axis, n):
    ap = ap.unsqueeze(axis)
    shape = list(ap.shape)
    shape[axis] = n
    return ap.to_broadcast(shape)


def over_groups(eng, step):
    step(0, 0)
    step(1, 1)
    with eng.Fori(1, GROUPS // 2) as pair:
        step(pair * 2, 0)
        step(pair * 2 + 1, 1)
    if GROUPS % 2:
        step(GROUPS - 1, 0)


def is_early(i):
    return isinstance(i, int) and i < 2


def is_last(i):
    return isinstance(i, int) and i == GROUPS - 1


def pass_gate(eng, gate):
    eng.sem_inc(gate, 1)


def layer_norm(nc, tag, sem, ps, src, dst, centred, squared, rstd, ones, eps, scale=None, bias=None):
    mean_ready, centred_ready, squared_ready = sem(f"{tag}_mean"), sem(f"{tag}_centred"), sem(f"{tag}_squared")
    var_ready, std_ready, rstd_ready = sem(f"{tag}_var"), sem(f"{tag}_std"), sem(f"{tag}_rstd")
    normed = sem(f"{tag}_normed")
    blocks = [slice(b * BN, (b + 1) * BN) for b in range(BL)]

    with nc.Block() as block:
        @block.tensor
        def _(pe):
            for b, cols in enumerate(blocks):
                for a in range(2):
                    last = nc.tensor.matmul(ps[0:EC, b, 0:BN], ones[:, :], src[:, a, cols], start=a == 0, stop=a == 1)
                last.then_inc(mean_ready, 1)
            for b, cols in enumerate(blocks):
                pe.wait_ge(squared_ready, b + 1)
                for a in range(2):
                    last = nc.tensor.matmul(ps[0:EC, BL + b, 0:BN], ones[:, :], squared[:, a, cols], start=a == 0,
                                            stop=a == 1)
                last.then_inc(var_ready, 1)

        @block.scalar
        def _(act):
            for b, cols in enumerate(blocks):
                act.wait_ge(centred_ready, b + 1)
                nc.scalar.activation(squared[:, :, cols], centred[:, :, cols], ACT.Square).then_inc(squared_ready, 1)
            for b, cols in enumerate(blocks):
                act.wait_ge(var_ready, b + 1)
                nc.scalar.activation(rstd[:, cols], ps[0:EC, BL + b, 0:BN], ACT.Sqrt, bias=eps).then_inc(std_ready, 1)

        @block.vector
        def _(dve):
            for b, cols in enumerate(blocks):
                dve.wait_ge(mean_ready, b + 1)
                nc.vector.tensor_tensor(centred[:, :, cols], src[:, :, cols], spread(ps[0:EC, b, 0:BN], 1, 2),
                                        ALU.subtract).then_inc(centred_ready, 1)
            for b, cols in enumerate(blocks):
                dve.wait_ge(std_ready, b + 1)
                nc.vector.reciprocal(rstd[:, cols], rstd[:, cols]).then_inc(rstd_ready, 1)
                dve.wait_ge(rstd_ready, b + 1)
                nc.vector.tensor_tensor(dst[:, :, cols], centred[:, :, cols], spread(rstd[:, cols], 1, 2),
                                        ALU.mult).then_inc(normed, 1)
            if scale is not None:
                dve.wait_ge(normed, BL)
                for a in range(2):
                    nc.vector.tensor_scalar(dst[:, a, :], dst[:, a, :], scale[:, a:a + 1], bias[:, a:a + 1],
                                            ALU.mult, ALU.add)


def attention(nc, tag, sem, sb, ps, QT, KT, UT, xnT, wv, v_bias, v_start, mask, blocks4, ident, identb, sink=None):
    KW = GT + (sink is not None)
    qs = [sb(f"{tag}_queries{p}", [128, HG, GT]) for p in range(2)]
    xs = [sb(f"{tag}_tokens{p}", [EC, 2, GT]) for p in range(2)]
    kd = [sb(f"{tag}_keys_by_head{p}", [128, HG, 4, KW]) for p in range(2)]
    va = [sb(f"{tag}_values{p}", [KW, HEADS, 32]) for p in range(2)]
    probs = [sb(f"{tag}_probs{p}", [GT, HEADS, KW]) for p in range(2)]
    pt = [sb(f"{tag}_probs_by_key{p}", [KW, HEADS, GT]) for p in range(2)]
    top = sb(f"{tag}_row_max", [GT, HEADS])
    scores = ps[0:GT, 0:HG, 0:4 * KW].rearrange("q g (h k) -> q g h k", h=4)
    probs_ps = ps[0:KW, HG:2 * HG, 0:4 * GT]
    v_ps = ps[0:GT, 6, 0:E]
    u_ps = ps[:, 7, 0:HG * GT]

    filled = sem(f"{tag}_constant_parts_filled")
    sliced, keys_ready, v_done = sem(f"{tag}_sliced"), sem(f"{tag}_keys"), sem(f"{tag}_v_product")
    values_ready, scored = sem(f"{tag}_values_ready"), sem(f"{tag}_scored")
    max_ready, shifted, exp_ready = sem(f"{tag}_max"), sem(f"{tag}_shifted"), sem(f"{tag}_exp")
    turned, turned_copied = sem(f"{tag}_turned"), sem(f"{tag}_turned_copied")
    summed, summed_copied = sem(f"{tag}_summed"), sem(f"{tag}_summed_copied")

    def cols(i):
        return bass.ds(i * GT, GT)

    with nc.Block() as block:
        @block.gpsimd
        def _(pool):
            for p in range(2):
                nc.gpsimd.tensor_copy(va[p][:, :, :], v_start[:, :, :]).then_inc(filled, 1)
            if sink is not None:
                for p in range(2):
                    nc.gpsimd.tensor_copy(kd[p][:, :, :, GT], sink[:, :, :]).then_inc(filled, 1)

            def step(i, p):
                if not is_early(i):
                    pool.wait_ge(scored, i - 1)
                pool.wait_ge(filled, 2)
                nc.gpsimd.tensor_copy(qs[p][:, :, :], QT[:, :, cols(i)]).then_inc(sliced, 1)
                nc.gpsimd.tensor_copy(xs[p][:, :, :], xnT[:, :, cols(i)]).then_inc(sliced, 1)
            over_groups(pool, step)

        @block.tensor
        def _(pe):
            def values_and_scores(i, p):
                pe.wait_ge(sliced, 2 * i + 2)
                if not (isinstance(i, int) and i < 1):
                    pe.wait_ge(values_ready, i)
                for a in range(2):
                    last = nc.tensor.matmul(v_ps, xs[p][:, a, :], wv[:, a, :], start=a == 0, stop=a == 1)
                last.then_inc(v_done, 1)
                pe.wait_ge(keys_ready, i + 1)
                if not (isinstance(i, int) and i < 1):
                    pe.wait_ge(shifted, i)
                for g in range(HG):
                    out = ps[0:GT, g, 0:4 * KW]
                    nc.tensor.matmul(out, identb[0:GT, 0:GT], mask[:, :], start=True, stop=False)
                    last = nc.tensor.matmul(out, qs[p][:, g, :], kd[p][:, g, :, :].rearrange("p h k -> p (h k)"),
                                            start=False, stop=True)
                last.then_inc(scored, 1)

            def weighted_sums(i, p):
                pe.wait_ge(exp_ready, i + 1)
                for g in range(HG):
                    if not (isinstance(i, int) and i < 1):
                        pe.wait_ge(turned_copied, 3 * i + g - 2)
                    for h in range(4):
                        last = nc.tensor.transpose(ps[0:KW, HG + g, h * GT:(h + 1) * GT], probs[p][:, 4 * g + h, :],
                                                   ident[0:GT, 0:GT])
                    last.then_inc(turned, 1)
                pe.wait_ge(values_ready, i + 1)
                if not (isinstance(i, int) and i < 1):
                    pe.wait_ge(summed_copied, i)
                for g in range(HG):
                    pe.wait_ge(turned_copied, 3 * i + g + 1)
                    for h in range(4):
                        last = nc.tensor.matmul(ps[32 * h:32 * h + 32, 7, g * GT:(g + 1) * GT], va[p][:, 4 * g + h, :],
                                                pt[p][:, 4 * g + h, :], start=True, stop=True)
                last.then_inc(summed, 1)

            values_and_scores(0, 0)

            def step(i, p):
                if not is_last(i):
                    values_and_scores(i + 1, 1 - p)
                weighted_sums(i, p)
            over_groups(pe, step)

        @block.vector
        def _(dve):
            def keys(i, p):
                if not is_early(i):
                    dve.wait_ge(scored, i - 1)
                for g in range(HG):
                    last = nc.vector.tensor_tensor(kd[p][:, g, :, 0:GT], spread(KT[:, g, cols(i)], 1, 4),
                                                   spread(blocks4[:, :], 2, GT), ALU.mult)
                last.then_inc(keys_ready, 1)

            if sink is not None:
                dve.wait_ge(filled, 4)
            keys(0, 0)

            def step(i, p):
                if not is_last(i):
                    keys(i + 1, 1 - p)
                if not is_early(i):
                    dve.wait_ge(summed, i - 1)
                dve.wait_ge(filled, 2)
                dve.wait_ge(v_done, i + 1)
                out = va[p][0:GT, :, 0:HD]
                v = v_ps.rearrange("k (h d) -> k h d", h=HEADS)
                if v_bias is None:
                    nc.vector.tensor_copy(out, v).then_inc(values_ready, 1)
                else:
                    nc.vector.tensor_tensor(out, v, v_bias[:, :, :], ALU.add).then_inc(values_ready, 1)
                dve.wait_ge(scored, i + 1)
                nc.vector.reduce_max(top[:, :].rearrange("q (g h) -> q g h", g=HG), scores, AX.X).then_inc(max_ready, 1)
                dve.wait_ge(max_ready, i + 1)
                if not is_early(i):
                    dve.wait_ge(turned, 3 * i - 3)
                out = probs[p][:, :, :].rearrange("q (g h) k -> q g h k", g=HG)
                nc.vector.tensor_tensor(out, scores, spread(top[:, :].rearrange("q (g h) -> q g h", g=HG), 3, KW),
                                        ALU.subtract).then_inc(shifted, 1)
            over_groups(dve, step)

        @block.scalar
        def _(act):
            def exponentials(i, p):
                act.wait_ge(shifted, i + 1)
                nc.scalar.activation(probs[p][:, :, :], probs[p][:, :, :], ACT.Exp).then_inc(exp_ready, 1)

            exponentials(0, 0)

            def step(i, p):
                for g in range(HG):
                    if not is_early(i) and g == 0:
                        act.wait_ge(summed, i - 1)
                    act.wait_ge(turned, 3 * i + g + 1)
                    nc.scalar.copy(pt[p][:, 4 * g:4 * g + 4, :].rearrange("k h q -> k (h q)"),
                                   probs_ps[:, g, :]).then_inc(turned_copied, 1)
                if not is_last(i):
                    exponentials(i + 1, 1 - p)
                act.wait_ge(summed, i + 1)
                act.wait_ge(filled, 2)
                nc.scalar.copy(UT[:, :, cols(i)], u_ps.rearrange("p (g q) -> p g q", g=HG)).then_inc(summed_copied, 1)
            over_groups(act, step)


def program(nc, ins, out):
    with ExitStack() as ctx:
        def sem(name):
            return ctx.enter_context(nc.semaphore(name))

        def allocator(stack):
            return lambda name, shape, dt=F32: stack.enter_context(nc.sbuf_tensor(name, shape, dt))

        sb = allocator(ctx)
        ps = ctx.enter_context(nc.psum_tensor("banks", [128, 8, 512], F32))

        held, loaded = {}, {}
        def hold(stack, names):
            arrived = sem(f"loaded_with_{names[-1]}")
            for n in names:
                held[n] = allocator(stack)(f"in_{n}", list(ins[n].shape), ins[n].dtype)
                loaded[n] = arrived
            return names

        hold(ctx, ("vec",))
        rest = hold(ctx, ("ones", "ident", "identb", "blocks4", "den", "P", "C", "sel", "b2", "G1", "G2"))
        hT = sb("hT", [EC, 2, NT])
        xnT = sb("xnT", [EC, 2, NT])
        w_stack = sb("w1_parts_by_row", [128, S_, M_ * H_], BF16)
        w1_loaded, b1_loaded = sem("loaded_W1"), sem("loaded_b1")
        stacked_w = sem("w1_parts_stacked")
        vec = held["vec"]
        V = {}
        for i, (n, k) in enumerate(VEC):
            V[n] = vec[0:VROWS[n], sum(k for _, k in VEC[:i]):sum(k for _, k in VEC[:i + 1])]

        with ExitStack() as mem:
            hold(mem, ("tok_w",))
            rest0 = hold(mem, ("wq0", "wk0", "av", "ah", "kconst", "mask0", "wv0", "v_start0", "bv", "bh", "wp0"))
            embed(nc, sem, allocator, ps, ins, held, loaded, (rest, rest0), hT, V, w_stack, w1_loaded, b1_loaded, stacked_w)
            s = allocator(mem)
            with ExitStack() as mem2:
                s2 = allocator(mem2)
                layer_norm(nc, "ln0", sem, ps, hT, xnT, s2("centred0", [EC, 2, NT]), s2("squared0", [EC, 2, NT]),
                           s2("rstd0", [EC, NT]), held["ones"], V["ln_eps"])
            QT, KT, UT = s("QT0", [128, HG, NT]), s("KT0", [128, HG, NT]), s("UT0", [128, HG, NT])
            project_qk0(nc, sem, ps, held, loaded, xnT, UT, QT, KT)
            with ExitStack() as mem2:
                attention(nc, "a0", sem, allocator(mem2), ps, QT, KT, UT, xnT, held["wv0"], None, held["v_start0"],
                          held["mask0"], held["blocks4"], held["ident"], held["identb"])
            project_out0(nc, sem, ps, held, UT, QT, KT, hT, V)

        attention1 = ("wq1", "wk1", "rot", "cosq", "sinq", "cosk", "sink_", "mask1", "wv1", "vb1", "v_start1",
                      "sinkcol", "wp1")
        hold(ctx, attention1)
        with ExitStack() as mem:
            s = allocator(mem)
            with ExitStack() as mem2:
                s2 = allocator(mem2)
                layer_norm(nc, "ln1", sem, ps, hT, xnT, s2("centred1", [EC, 2, NT]), s2("squared1", [EC, 2, NT]),
                           s2("rstd1", [EC, NT]), held["ones"], V["ln_eps"])
            experts(nc, sem, s, allocator, ps, ins, held, loaded, attention1, xnT, hT, w_stack, stacked_w, V)

        feed_forward1 = ("gb_in", "gb_out", "w_in", "w_out", "all_ones")
        hold(ctx, feed_forward1)
        with ExitStack() as mem:
            s = allocator(mem)
            with ExitStack() as mem2:
                s2 = allocator(mem2)
                layer_norm(nc, "ln2", sem, ps, hT, xnT, s2("centred2", [EC, 2, NT]), s2("squared2", [EC, 2, NT]),
                           s2("rstd2", [EC, NT]), held["ones"], V["ln_eps"], V["norm_scale"], V["norm_bias"])
            QT, KT, UT = s("QT1", [128, HG, NT]), s("KT1", [128, HG, NT]), s("UT1", [128, HG, NT])
            with ExitStack() as mem2:
                project_qk1(nc, sem, allocator(mem2), ps, ins, held, loaded, feed_forward1, xnT, QT, KT, V)
            with ExitStack() as mem2:
                attention(nc, "a1", sem, allocator(mem2), ps, QT, KT, UT, xnT, held["wv1"], held["vb1"],
                          held["v_start1"], held["mask1"], held["blocks4"], held["ident"], held["identb"],
                          held["sinkcol"])
            project_out1(nc, sem, ps, held, UT, QT, hT, V)

        with ExitStack() as mem:
            quantised(nc, sem, allocator(mem), ps, held, hT, out, V)


VEC = [("tok_b", 2), ("ln_eps", 1), ("bp0", 2), ("g2b", 2), ("g1b", 1), ("norm_scale", 2), ("norm_bias", 2),
       ("bq1", 3), ("bk1", 3), ("bp1", 2), ("rezero", 1), ("rms_eps", 1), ("rms_ln", 1)]
VROWS = {"tok_b": 96, "ln_eps": 96, "bp0": 96, "g2b": 96, "g1b": 64, "norm_scale": 96, "norm_bias": 96,
         "bq1": 128, "bk1": 128, "bp1": 96, "rezero": 96, "rms_eps": 128, "rms_ln": 128}


def embed(nc, sem, allocator, ps, ins, held, loaded, rest, hT, V, w_stack, w1_loaded, b1_loaded, stacked_w):
    with ExitStack() as mem:
        sb = allocator(mem)
        xt = sb("xt", [128, PK, NT])
        w1 = sb("w1", [S_ * R_, M_ * H_])
        b1 = sb("b1", [S_, M_ * H_])
        w_part = [sb(f"w1_part{n}", [S_ * R_, M_ * H_], BF16) for n in range(3)]
        b_part = [sb(f"b1_part{n}", [S_, M_ * H_], BF16) for n in range(3)]
        x_loaded = [sem(f"loaded_x{k}") for k in range(PK)]
        tok_done, w_split, b_split, cleared = sem("tok_done"), sem("w1_split"), sem("b1_split"), sem("w_stack_cleared")
        embedded = sem("embedded")

        with nc.Block() as block:
            @block.sync
            def _(sp):
                sp.dma_start(held["tok_w"][:], ins["tok_w"]).then_inc(loaded["tok_w"], 16)
                sp.dma_start(held["vec"][:], ins["vec"]).then_inc(loaded["vec"], 16)
                for k in range(PK):
                    sp.dma_start(xt[:, k, :], ins["xt"][:, k, :]).then_inc(x_loaded[k], 16)
                sp.dma_start(w1[:], ins["W1"]).then_inc(w1_loaded, 16)
                sp.dma_start(b1[:], ins["b1"]).then_inc(b1_loaded, 16)
                for names in rest:
                    for n in names:
                        sp.dma_start(held[n][:], ins[n]).then_inc(loaded[n], 16)
                sp.wait_ge(cleared, 2)
                sp.wait_ge(w_split, 5)
                for s in range(S_):
                    for row, part in W_ROWS:
                        sp.dma_start(w_stack[row:row + R_, s, :], w_part[part][s * R_:(s + 1) * R_, :]).then_inc(
                            stacked_w, 16)
                sp.wait_ge(b_split, 5)
                for n in range(3):
                    sp.dma_start(w_stack[BIAS_ROW + n:BIAS_ROW + n + 1, :, :], b_part[n][:, :]).then_inc(stacked_w, 16)
                sp.wait_ge(stacked_w, 16 * (S_ * len(W_ROWS) + 3))
                for names in rest:
                    sp.wait_ge(loaded[names[0]], 16 * len(names))

            @block.gpsimd
            def _(pool):
                nc.gpsimd.memset(w_stack[64:96, :, :], 0.0).then_inc(cleared, 1)
                nc.gpsimd.memset(w_stack[96:128, :, :], 0.0).then_inc(cleared, 1)
                pool.wait_ge(cleared, 2)

            @block.vector
            def _(dve):
                for x, part, ready, split in ((w1, w_part, w1_loaded, w_split), (b1, b_part, b1_loaded, b_split)):
                    dve.wait_ge(ready, 16)
                    nc.vector.tensor_copy(part[0][:], x[:]).then_inc(split, 1)
                    for n in (1, 2):
                        dve.wait_ge(split, 2 * n - 1)
                        nc.vector.tensor_tensor(x[:], x[:], part[n - 1][:], ALU.subtract).then_inc(split, 1)
                        dve.wait_ge(split, 2 * n)
                        nc.vector.tensor_copy(part[n][:], x[:]).then_inc(split, 1)

            @block.tensor
            def _(pe):
                pe.wait_ge(loaded["tok_w"], 16)
                for k in range(PK):
                    pe.wait_ge(x_loaded[k], 16)
                    for b in range(BL):
                        for a in range(2):
                            last = nc.tensor.matmul(ps[0:EC, 2 * b + a, 0:BN], held["tok_w"][:, k, a * EC:(a + 1) * EC],
                                                    xt[:, k, b * BN:(b + 1) * BN], start=k == 0, stop=k == PK - 1)
                            if k == PK - 1:
                                last.then_inc(tok_done, 1)

            @block.scalar
            def _(act):
                act.wait_ge(loaded["vec"], 16)
                for b in range(BL):
                    for a in range(2):
                        act.wait_ge(tok_done, 2 * b + a + 1)
                        nc.scalar.activation(hT[:, a, b * BN:(b + 1) * BN], ps[0:EC, 2 * b + a, 0:BN], ACT.Identity,
                                             bias=V["tok_b"][:, a:a + 1]).then_inc(embedded, 1)


W_ROWS = [(0, 0), (16, 1), (32, 0), (48, 1), (64, 0), (96, 2)]
Z_ROWS = [(0, 0), (16, 0), (32, 1), (48, 1), (64, 2), (96, 0)]
BIAS_ROW = 112


def images(ap):
    return ap.rearrange("p (b t) -> p b t", t=TOK)


def class_units():
    rows = [(r, ("row", r)) for r in range(ROWS)] + [(ROWS, ("first", 0))]
    cols = [(c, ("col", c)) for c in range(COLS)] + [(COLS, ("first", 0))]
    return [(0, rows[0:3]), (0, rows[3:6]), (0, rows[6:7]), (0, rows[7:8]),
            (1, cols[0:2]), (1, cols[2:4]), (1, cols[4:5]), (1, cols[5:6])]


def positions(ap, kinds):
    v = images(ap)
    kind, first = kinds[0]
    if kind == "first":
        return v[:, :, 0:1]
    grid = v[:, :, 1:TOK].rearrange("p b (r c) -> p b r c", c=COLS)
    n = len(kinds)
    if kind == "row":
        t = grid[:, :, first:first + n, :].rearrange("p b r c -> p r b c")
    else:
        t = grid[:, :, :, first:first + n].rearrange("p b r c -> p c b r")
    return t if n > 1 else t[:, 0]


def class_pass(nc, sem, tag, pe_wait, ps, by_row, by_col, srcs, dsts):
    done, copied = sem(f"{tag}_product"), sem(f"{tag}_copied")
    units = [(n, u) for n in range(len(srcs)) for u in class_units()]

    def view(bank, kinds, size):
        n = len(kinds)
        flat = ps[:, bank, 0:n * size * IMG_P]
        if n > 1:
            return flat.rearrange("p (k b t) -> p k b t", k=n, b=IMG_P)
        return flat.rearrange("p (b t) -> p b t", b=IMG_P)

    def size(kinds):
        return {"first": 1, "row": COLS, "col": ROWS}[kinds[0][0]]

    with nc.Block() as block:
        @block.tensor
        def _(pe):
            for w in pe_wait:
                pe.wait_ge(*w)
            for i, (n, (which, classes)) in enumerate(units):
                if i >= 8:
                    pe.wait_ge(copied, i - 7)
                m = (by_row, by_col)[which]
                for j, (c, kind) in enumerate(classes):
                    k = size([kind])
                    last = nc.tensor.matmul(ps[:, i % 8, j * k * IMG_P:(j + 1) * k * IMG_P].rearrange(
                        "p (b t) -> p b t", b=IMG_P), m[:, c, :], positions(srcs[n], [kind]), start=True, stop=True)
                last.then_inc(done, 1)

        @block.vector
        def _(dve):
            for i, (n, (which, classes)) in enumerate(units):
                dve.wait_ge(done, i + 1)
                kinds = [k for _, k in classes]
                got, dst = view(i % 8, kinds, size(kinds)), positions(dsts[n], kinds)
                if which == 0:
                    nc.vector.tensor_copy(dst, got).then_inc(copied, 1)
                else:
                    if i % 8 == 4:
                        dve.wait_ge(copied, i)
                    nc.vector.tensor_tensor(dst, dst, got, ALU.add).then_inc(copied, 1)


def project_qk0(nc, sem, ps, held, loaded, xnT, base, QT, KT):
    done, q_copied, k_copied = sem("qk0_product"), sem("q0_copied"), sem("k0_copied")
    units = [(w, g, b) for w in ("wq0", "wk0") for g in range(HG) for b in range(BL)]
    nq = HG * BL
    with nc.Block() as block:
        @block.tensor
        def _(pe):
            for i, (w, g, b) in enumerate(units):
                if i >= 8:
                    j = i - 8
                    pe.wait_ge(q_copied if j < nq else k_copied, (j if j < nq else j - nq) + 1)
                for a in range(2):
                    last = nc.tensor.matmul(ps[:, i % 8, 0:BN], held[w][:, a, g, :], xnT[:, a, b * BN:(b + 1) * BN],
                                            start=a == 0, stop=a == 1)
                last.then_inc(done, 1)

        @block.scalar
        def _(act):
            for i, (w, g, b) in enumerate(units[:nq]):
                act.wait_ge(done, i + 1)
                nc.scalar.mul(base[:, g, b * BN:(b + 1) * BN], ps[:, i % 8, 0:BN], HD ** -0.5).then_inc(q_copied, 1)

        @block.vector
        def _(dve):
            for i, (w, g, b) in enumerate(units[nq:], nq):
                dve.wait_ge(done, i + 1)
                nc.vector.tensor_tensor(images(KT[:, g, b * BN:(b + 1) * BN]), images(ps[:, i % 8, 0:BN]),
                                        spread(held["kconst"][:, :], 1, BIMG), ALU.add).then_inc(k_copied, 1)
    class_pass(nc, sem, "q0_classes", [], ps, held["av"], held["ah"], [base[:, g, :] for g in range(HG)],
               [QT[:, g, :] for g in range(HG)])


def denominators(nc, sem, tag, ps, held, UT, target):
    done, inv, used = sem(f"{tag}_den"), sem(f"{tag}_inverted"), sem(f"{tag}_divided")
    units = [(g, b) for g in range(HG) for b in range(BL)]
    with nc.Block() as block:
        @block.tensor
        def _(pe):
            for i, (g, b) in enumerate(units):
                if i >= 8:
                    pe.wait_ge(used, i - 7)
                nc.tensor.matmul(ps[:, i % 8, 0:BN], held["den"][:, :], UT[:, g, b * BN:(b + 1) * BN], start=True,
                                 stop=True).then_inc(done, 1)

        @block.vector
        def _(dve):
            for i, (g, b) in enumerate(units):
                dve.wait_ge(done, i + 1)
                nc.vector.reciprocal(ps[:, i % 8, 0:BN], ps[:, i % 8, 0:BN]).then_inc(inv, 1)
                dve.wait_ge(inv, i + 1)
                t = target[:, g, b * BN:(b + 1) * BN]
                nc.vector.tensor_tensor(t, t, ps[:, i % 8, 0:BN], ALU.mult).then_inc(used, 1)


def project_out0(nc, sem, ps, held, UT, OT, _KT, hT, V):
    class_pass(nc, sem, "u0_classes", [], ps, held["bv"], held["bh"], [UT[:, g, :] for g in range(HG)],
               [OT[:, g, :] for g in range(HG)])
    denominators(nc, sem, "a0", ps, held, UT, OT)
    done = sem("out0_product")
    units = [(b, m) for b in range(BL) for m in range(2)]
    with nc.Block() as block:
        @block.tensor
        def _(pe):
            for i, (b, m) in enumerate(units):
                for g in range(HG):
                    last = nc.tensor.matmul(ps[0:EC, i, 0:BN], held["wp0"][:, g, m * EC:(m + 1) * EC],
                                            OT[:, g, b * BN:(b + 1) * BN], start=g == 0, stop=g == HG - 1)
                last.then_inc(done, 1)

        @block.vector
        def _(dve):
            for i, (b, m) in enumerate(units):
                dve.wait_ge(done, i + 1)
                h = hT[:, m, b * BN:(b + 1) * BN]
                nc.vector.scalar_tensor_tensor(h, ps[0:EC, i, 0:BN], V["bp0"][:, m:m + 1], h, ALU.add, ALU.add)


def project_qk1(nc, sem, sb, ps, ins, held, loaded, to_load, xnT, QT, KT, V):
    base = sb("qk1_base", [128, BN]), sb("qk1_base_b", [128, BN])
    turned = sb("qk1_sin", [128, BN]), sb("qk1_sin_b", [128, BN])
    done, biased, rotated = sem("qk1_product"), sem("qk1_biased"), sem("qk1_rotated")
    cos_part, sin_part, ready = sem("qk1_cos_part"), sem("qk1_sin_part"), sem("qk1_ready")
    units = [(w, g, b) for w in range(2) for g in range(HG) for b in range(BL)]
    with nc.Block() as block:
        @block.sync
        def _(sp):
            for n in to_load:
                sp.dma_start(held[n][:], ins[n]).then_inc(loaded[n], 16)
            sp.wait_ge(loaded[to_load[0]], 16 * len(to_load))

        @block.tensor
        def _(pe):
            def product(i):
                w, g, b = units[i]
                if i >= 4:
                    pe.wait_ge(biased, i - 3)
                for a in range(2):
                    last = nc.tensor.matmul(ps[:, i % 4, 0:BN], held[("wq1", "wk1")[w]][:, a, g, :],
                                            xnT[:, a, b * BN:(b + 1) * BN], start=a == 0, stop=a == 1)
                last.then_inc(done, 1)

            product(0)
            for i in range(len(units)):
                if i + 1 < len(units):
                    product(i + 1)
                pe.wait_ge(biased, i + 1)
                if i >= 4:
                    pe.wait_ge(sin_part, i - 3)
                nc.tensor.matmul(ps[:, 4 + i % 4, 0:BN], held["rot"][:, :], base[i % 2][:, :], start=True,
                                 stop=True).then_inc(rotated, 1)

        @block.scalar
        def _(act):
            for i, (w, g, b) in enumerate(units):
                act.wait_ge(done, i + 1)
                if i >= 2:
                    act.wait_ge(rotated, i - 1)
                    act.wait_ge(cos_part, i - 1)
                bias = V[("bq1", "bk1")[w]][:, g:g + 1]
                nc.scalar.activation(base[i % 2][:, :], ps[:, i % 4, 0:BN], ACT.Identity, bias=bias).then_inc(biased, 1)

        @block.vector
        def _(dve):
            for i, (w, g, b) in enumerate(units):
                cos, sin = (held["cosq"], held["sinq"]) if w == 0 else (held["cosk"], held["sink_"])
                dst = (QT, KT)[w][:, g, b * BN:(b + 1) * BN]
                dve.wait_ge(biased, i + 1)
                nc.vector.tensor_tensor(images(dst), images(base[i % 2][:, :]), spread(cos[:, :], 1, BIMG),
                                        ALU.mult).then_inc(cos_part, 1)
                dve.wait_ge(rotated, i + 1)
                nc.vector.tensor_tensor(images(turned[i % 2][:, :]), images(ps[:, 4 + i % 4, 0:BN]),
                                        spread(sin[:, :], 1, BIMG), ALU.mult).then_inc(sin_part, 1)
                dve.wait_ge(cos_part, i + 1)
                dve.wait_ge(sin_part, i + 1)
                nc.vector.tensor_tensor(dst, dst, turned[i % 2][:, :], ALU.add).then_inc(ready, 1)


def project_out1(nc, sem, ps, held, UT, scaled, hT, V):
    denominators(nc, sem, "a1", ps, held, UT, UT)
    done, biased = sem("out1_product"), sem("out1_biased")
    units = [(b, m) for b in range(BL) for m in range(2)]
    with nc.Block() as block:
        @block.tensor
        def _(pe):
            for i, (b, m) in enumerate(units):
                for g in range(HG):
                    last = nc.tensor.matmul(ps[0:EC, i, 0:BN], held["wp1"][:, g, m * EC:(m + 1) * EC],
                                            UT[:, g, b * BN:(b + 1) * BN], start=g == 0, stop=g == HG - 1)
                last.then_inc(done, 1)

        @block.vector
        def _(dve):
            for i, (b, m) in enumerate(units):
                dve.wait_ge(done, i + 1)
                h = hT[:, m, b * BN:(b + 1) * BN]
                t = scaled[0:EC, m, b * BN:(b + 1) * BN]
                nc.vector.tensor_scalar(t, ps[0:EC, i, 0:BN], V["bp1"][:, m:m + 1], V["rezero"], ALU.add,
                                        ALU.mult).then_inc(biased, 1)
                dve.wait_ge(biased, i + 1)
                nc.vector.tensor_tensor(h, h, t, ALU.add)


def experts(nc, sem, sb, allocator, ps, ins, held, loaded, to_load, xnT, hT, w_stack, stacked_w, V):
    z_stack = sb("z_parts_by_row", [128, S_, NT], BF16)
    wt = sb("weights_by_expert", [128, S_ // 2, NT])
    g_stack = sb("weight_parts_by_row", [96, S_, 2, NT], BF16)
    stacked_z, stacked_g = sem("z_parts_stacked"), [sem("weight_parts_stacked_even"), sem("weight_parts_stacked_odd")]
    w2_loaded = sem("loaded_W2")

    with ExitStack() as mem:
        s2 = allocator(mem)
        zT = s2("zT", [128, NT])
        rest = s2("z_rest", [128, NT])
        z_part = [s2(f"z_part{n}", [128, NT], BF16) for n in range(3)]
        z_done, z_copied, z_split, cleared = sem("z_done"), sem("z_copied"), sem("z_split"), sem("z_stack_cleared")
        with nc.Block() as block:
            @block.gpsimd
            def _(pool):
                nc.gpsimd.memset(z_stack[64:96, :, :], 0.0).then_inc(cleared, 1)
                nc.gpsimd.memset(z_stack[96:128, :, :], 1.0).then_inc(cleared, 1)

            @block.tensor
            def _(pe):
                for b in range(BL):
                    for a in range(2):
                        last = nc.tensor.matmul(ps[:, b, 0:BN], held["P"][:, a, :], xnT[:, a, b * BN:(b + 1) * BN],
                                                start=a == 0, stop=a == 1)
                    last.then_inc(z_done, 1)

            @block.scalar
            def _(act):
                for b in range(BL):
                    act.wait_ge(z_done, b + 1)
                    nc.scalar.copy(zT[:, b * BN:(b + 1) * BN], ps[:, b, 0:BN]).then_inc(z_copied, 1)

            @block.vector
            def _(dve):
                dve.wait_ge(z_copied, BL)
                nc.vector.tensor_copy(z_part[0][:], zT[:]).then_inc(z_split, 1)
                for n in (1, 2):
                    dve.wait_ge(z_split, 2 * n - 1)
                    nc.vector.tensor_tensor(rest[:], (zT if n == 1 else rest)[:], z_part[n - 1][:],
                                            ALU.subtract).then_inc(z_split, 1)
                    dve.wait_ge(z_split, 2 * n)
                    nc.vector.tensor_copy(z_part[n][:], rest[:]).then_inc(z_split, 1)

            @block.sync
            def _(sp):
                for n in to_load:
                    sp.dma_start(held[n][:], ins[n]).then_inc(loaded[n], 16)
                sp.wait_ge(cleared, 2)
                sp.wait_ge(z_split, 5)
                for s in range(S_):
                    for row, part in Z_ROWS:
                        sp.dma_start(z_stack[row:row + R_, s, :], z_part[part][s * R_:(s + 1) * R_, :]).then_inc(
                            stacked_z, 16)

        choose_experts(nc, sem, s2, ps, held, zT, wt, g_stack, stacked_g)
    comb = sb("combined", [128, 2, NT])
    held["W2"] = sb("in_W2", list(ins["W2"].shape))
    with nc.Block() as block:
        @block.sync
        def _(sp):
            sp.dma_start(held["W2"][:], ins["W2"]).then_inc(w2_loaded, 16)
            sp.wait_ge(stacked_z, 16 * S_ * len(Z_ROWS))
            sp.wait_ge(stacked_g[0], 16 * 12 * ((GROUPS + 1) // 2))
            sp.wait_ge(stacked_g[1], 16 * 12 * (GROUPS // 2))
            sp.wait_ge(w2_loaded, 16)
            sp.wait_ge(loaded[to_load[0]], 16 * len(to_load))
    with ExitStack() as mem:
        run_experts(nc, sem, allocator(mem), ps, held, z_stack, g_stack, wt, w_stack, comb)

    gated = sb("gated", [G_, NT])
    g1_done, gated_ready, g2_done = sem("g1_done"), sem("gated_ready"), sem("g2_done")
    with nc.Block() as block:
        @block.tensor
        def _(pe):
            for b in range(BL):
                for j in range(2):
                    last = nc.tensor.matmul(ps[0:G_, b, 0:BN], held["G1"][:, j, :], comb[:, j, b * BN:(b + 1) * BN],
                                            start=j == 0, stop=j == 1)
                last.then_inc(g1_done, 1)
            for b in range(BL):
                pe.wait_ge(gated_ready, b + 1)
                if b == 2:
                    pe.wait_ge(gated_ready, 3)
                for m in range(2):
                    bank = 3 + (2 * b + m) if 2 * b + m < 5 else 0
                    nc.tensor.matmul(ps[0:EC, bank, 0:BN], held["G2"][:, m * EC:(m + 1) * EC],
                                     gated[:, b * BN:(b + 1) * BN], start=True, stop=True).then_inc(g2_done, 1)

        @block.scalar
        def _(act):
            for b in range(BL):
                act.wait_ge(g1_done, b + 1)
                nc.scalar.activation(gated[:, b * BN:(b + 1) * BN], ps[0:G_, b, 0:BN], ACT.Gelu_apprx_tanh,
                                     bias=V["g1b"]).then_inc(gated_ready, 1)

        @block.vector
        def _(dve):
            for i in range(2 * BL):
                b, m = divmod(i, 2)
                dve.wait_ge(g2_done, i + 1)
                h = hT[:, m, b * BN:(b + 1) * BN]
                nc.vector.scalar_tensor_tensor(h, ps[0:EC, 3 + i if i < 5 else 0, 0:BN], V["g2b"][:, m:m + 1], h,
                                               ALU.add, ALU.add)


def choose_experts(nc, sem, sb, ps, held, zT, wt, g_stack, stacked_g):
    W = M_ + TOPK
    zs = [sb(f"z_slice{p}", [128, GT]) for p in range(2)]
    sc = [sb(f"expert_scores{p}", [GT, S_, W]) for p in range(2)]
    marked = sb("scores_marked", [GT, S_, W])
    best = sb("best", [GT, S_, 8])
    wanted = sb("wanted", [GT, S_, 8])
    ex = [sb(f"expert_exp{p}", [GT, S_, M_]) for p in range(2)]
    total = sb("exp_total", [GT, S_])
    wn = [sb(f"expert_weights{p}", [GT, S_ * M_]) for p in range(2)]
    left = [sb(f"weight_rest{p}", [128, S_ // 2, GT]) for p in range(2)]
    p0s = [sb(f"weight_first{p}", [128, S_ // 2, GT], BF16) for p in range(2)]
    p1s = [sb(f"weight_second{p}", [128, S_ // 2, GT], BF16) for p in range(2)]
    p2s = [sb(f"weight_third{p}", [128, S_ // 2, GT], BF16) for p in range(2)]

    sentinels, sliced, scored, score_copied = (sem("sentinels"), sem("z_sliced"), sem("expert_scored"),
                                               sem("expert_score_copied"))
    best_ready, wanted_ready, marked_ready = sem("best_ready"), sem("wanted_ready"), sem("marked_ready")
    centred, exp_ready, picked, total_ready, inverted = (sem("escore_centred"), sem("eexp_ready"), sem("picked"),
                                                         sem("etotal_ready"), sem("etotal_inverted"))
    weighed, turned, first_ready, wt_ready = (sem("eweighed"), sem("eweight_turned"), sem("first_ready"),
                                              sem("wt_ready"))
    gate = sem("choice_gate")
    left_ready, second_ready, third_ready = sem("eleft_ready"), sem("second_ready"), sem("third_ready")

    def cols(i):
        return bass.ds(i * GT, GT)

    def wps(p):
        return ps[:, 2 + p, 0:4 * GT].rearrange("p (s t) -> p s t", s=4)

    with nc.Block() as block:
        @block.gpsimd
        def _(pool):
            for p in range(2):
                nc.gpsimd.memset(sc[p][:, :, M_:W], SENTINEL).then_inc(sentinels, 1)
            nc.gpsimd.memset(wanted[:, :, TOPK:8], SENTINEL).then_inc(sentinels, 1)

            def step(i, p):
                if not is_early(i):
                    pool.wait_ge(scored, i - 1)
                pool.wait_ge(sentinels, 3)
                nc.gpsimd.tensor_copy(zs[p][:, :], zT[:, cols(i)]).then_inc(sliced, 1)
            over_groups(pool, step)

        @block.tensor
        def _(pe):
            def turn(i, p):
                pe.wait_ge(weighed, i + 1)
                if not is_early(i):
                    pe.wait_ge(first_ready, i - 1)
                    pe.wait_ge(wt_ready, i - 1)
                for q in range(4):
                    last = nc.tensor.transpose(ps[:, 2 + p, q * GT:(q + 1) * GT], wn[p][:, q * 128:(q + 1) * 128],
                                               held["ident"][0:GT, 0:GT])
                last.then_inc(turned, 1)

            def score(i, p):
                pe.wait_ge(sliced, i + 1)
                if not is_early(i):
                    pe.wait_ge(score_copied, i - 1)
                nc.tensor.matmul(ps[0:GT, p, 0:S_ * M_], zs[p][:, :], held["C"][:, :], start=True,
                                 stop=True).then_inc(scored, 1)

            def step(i, p):
                score(i, p)
                turn(i, p)
            over_groups(pe, step)

        @block.scalar
        def _(act):
            def step(i, p):
                act.wait_ge(scored, i + 1)
                if not is_early(i):
                    act.wait_ge(centred, i - 1)
                nc.scalar.copy(sc[p][:, :, 0:M_], ps[0:GT, p, :].rearrange("t (s m) -> t s m", s=S_)).then_inc(
                    score_copied, 1)
                act.wait_ge(centred, i + 1)
                nc.scalar.activation(ex[p][:, :, :], ex[p][:, :, :], ACT.Exp).then_inc(exp_ready, 1)
                act.wait_ge(turned, i + 1)
                if not is_early(i):
                    act.wait_ge(stacked_g[p], (i - p) * 96)
                nc.scalar.copy(p0s[p][:, :, :], wps(p)).then_inc(first_ready, 1)
                act.wait_ge(sentinels, 3)
                nc.scalar.copy(wt[:, :, cols(i)], wps(p)).then_inc(wt_ready, 1)
                act.wait_ge(left_ready, i + 1)
                nc.scalar.copy(p1s[p][:, :, :], left[p][:, :, :]).then_inc(second_ready, 1)
            over_groups(act, step)

        @block.vector
        def _(dve):
            dve.wait_ge(sentinels, 3)

            def step(i, p):
                dve.wait_ge(score_copied, i + 1)
                pass_gate(dve, gate)
                for s in range(S_):
                    last = nc.vector.max(best[:, s, :], sc[p][:, s, 0:M_])
                last.then_inc(best_ready, 1)
                dve.wait_ge(best_ready, i + 1)
                nc.vector.tensor_copy(wanted[:, :, 0:TOPK], best[:, :, 0:TOPK]).then_inc(wanted_ready, 1)
                if not is_early(i):
                    dve.wait_ge(weighed, i - 1)
                nc.vector.tensor_tensor(ex[p][:, :, :], sc[p][:, :, 0:M_],
                                        spread(best[:, :, 0], 2, M_), ALU.subtract).then_inc(centred, 1)
                dve.wait_ge(wanted_ready, i + 1)
                pass_gate(dve, gate)
                for s in range(S_):
                    last = nc.vector.match_replace(marked[:, s, :], wanted[:, s, :], sc[p][:, s, :], 2 * TAKEN)
                last.then_inc(marked_ready, 1)
                dve.wait_ge(marked_ready, i + 1)
                dve.wait_ge(exp_ready, i + 1)
                nc.vector.scalar_tensor_tensor(ex[p][:, :, :], marked[:, :, 0:M_], TAKEN, ex[p][:, :, :], ALU.is_lt,
                                               ALU.mult).then_inc(picked, 1)
                dve.wait_ge(picked, i + 1)
                nc.vector.reduce_sum(total[:, :], ex[p][:, :, :], AX.X).then_inc(total_ready, 1)
                dve.wait_ge(total_ready, i + 1)
                nc.vector.reciprocal(total[:, :], total[:, :]).then_inc(inverted, 1)
                dve.wait_ge(inverted, i + 1)
                if not is_early(i):
                    dve.wait_ge(turned, i - 1)
                nc.vector.tensor_tensor(wn[p][:, :].rearrange("t (s m) -> t s m", s=S_), ex[p][:, :, :],
                                        spread(total[:, :], 2, M_), ALU.mult).then_inc(weighed, 1)
                dve.wait_ge(first_ready, i + 1)
                dve.wait_ge(wt_ready, i + 1)
                nc.vector.tensor_tensor(left[p][:, :, :], wt[:, :, cols(i)], p0s[p][:, :, :], ALU.subtract).then_inc(left_ready, 1)
                dve.wait_ge(second_ready, i + 1)
                nc.vector.tensor_tensor(p2s[p][:, :, :], left[p][:, :, :], p1s[p][:, :, :],
                                        ALU.subtract).then_inc(third_ready, 1)
            over_groups(dve, step)

        @block.sync
        def _(sp):
            def step(i, p):
                sp.wait_ge(first_ready, i + 1)
                sp.wait_ge(second_ready, i + 1)
                sp.wait_ge(third_ready, i + 1)
                for n, part in enumerate((p0s, p1s, p2s)):
                    for odd in range(2):
                        for half in range(2):
                            row = 64 * odd + 32 * half
                            sp.dma_start(g_stack[32 * n:32 * n + 32, odd:S_:2, half, cols(i)],
                                         part[p][row:row + 32, :, :]).then_inc(stacked_g[p], 16)
            over_groups(sp, step)


def run_experts(nc, sem, sb, ps, held, z_stack, g_stack, wt, w_stack, comb):
    act_out = [sb(f"hidden{p}", [128, 2, BN]) for p in range(2)]
    weighted = [sb(f"hidden_weighted{p}", [128, 2, BN]) for p in range(2)]
    w2s = [sb(f"w2_chunk{p}", [128, 2, 32]) for p in range(2)]
    h_done, gelu_done, w_done, mult_done, y_done = (sem("hidden_product"), sem("hidden_gelu"), sem("weight_spread"),
                                                    sem("hidden_weighted"), sem("second_product"))
    w2_ready, comb_done, comb_copied = sem("w2_chunk_ready"), sem("comb_done"), sem("comb_copied")
    gate = sem("w2_gate")
    PAIRS = 2 * CH

    def start(eng, *counted):
        for s in counted:
            eng.sem_inc(s, 1)

    def pair_index(b, sh, c, jj):
        return b * (2 * PAIRS) + sh * PAIRS + c * 2 + jj

    def walk(eng, step):
        with eng.Fori(0, BL) as b:
            for sh in range(2):
                step(b, sh, 0, 0)
                step(b, sh, 0, 1)
                with eng.Fori(1, CH - 1) as c:
                    step(b, sh, c, 0)
                    step(b, sh, c, 1)
                step(b, sh, CH - 1, 0)
                step(b, sh, CH - 1, 1)

    with nc.Block() as block:
        @block.tensor
        def _(pe):
            def first(b, sh, c, jj):
                n = pair_index(b, sh, c, jj)
                if not (isinstance(c, int) and c == 0 and sh == 0):
                    pe.wait_ge(gelu_done, n)
                for k in range(2):
                    s = 4 * sh + 2 * jj + k
                    last = nc.tensor.matmul(ps[:, 2 * jj + k, 0:BN], w_stack[:, s, bass.ds(c * 128, 128)],
                                            z_stack[:, s, bass.ds(b * BN, BN)], start=True, stop=True)
                last.then_inc(h_done, 1)

            def spread_weights(b, sh, c, jj):
                n = pair_index(b, sh, c, jj)
                pe.wait_ge(mult_done, n + 1)
                half, cc = (c // 8, c % 8)
                for k in range(2):
                    s = 4 * sh + 2 * jj + k
                    rows = g_stack[:, s, :, :].rearrange("p h n -> p (h n)")
                    last = nc.tensor.matmul(ps[:, 4 + k, 0:BN], held["sel"][:, bass.ds(cc * 128, 128)],
                                            rows[:, bass.ds(half * NT + b * BN, BN)], start=True, stop=True)
                last.then_inc(w_done, 1)

            def second(b, sh, c, jj):
                n = pair_index(b, sh, c, jj)
                pe.wait_ge(mult_done, n + 2)
                pe.wait_ge(w2_ready, n + 1)
                for k in range(2):
                    j = 2 * jj + k
                    last = nc.tensor.matmul(ps[32 * j:32 * j + 32, 6 + sh, 0:BN], w2s[jj][:, k, :],
                                            weighted[jj][:, k, :], start=False, stop=False, skip_group_check=True)
                last.then_inc(y_done, 1)

            start(pe, y_done)
            with pe.Fori(0, BL) as b:
                for sh in range(2):
                    pe.wait_ge(comb_copied, b * 2 + 1)
                    for jj in range(2):
                        nc.tensor.matmul(ps[:, 6 + sh, 0:BN], held["b2"][:, 2 * sh + jj, :],
                                         wt[:, 2 * sh + jj, bass.ds(b * BN, BN)], start=jj == 0, stop=False,
                                         skip_group_check=True)
                    if sh == 0:
                        pe.wait_ge(gelu_done, b * (2 * PAIRS) + 1)
                    first(b, sh, 0, 0)
                    first(b, sh, 0, 1)
                    spread_weights(b, sh, 0, 0)
                    first(b, sh, 1, 0)
                    spread_weights(b, sh, 0, 1)
                    second(b, sh, 0, 0)
                    with pe.Fori(1, CH - 1) as c:
                        first(b, sh, c, 1)
                        spread_weights(b, sh, c, 0)
                        second(b, sh, c - 1, 1)
                        first(b, sh, c + 1, 0)
                        spread_weights(b, sh, c, 1)
                        second(b, sh, c, 0)
                    first(b, sh, CH - 1, 1)
                    spread_weights(b, sh, CH - 1, 0)
                    second(b, sh, CH - 2, 1)
                    spread_weights(b, sh, CH - 1, 1)
                    second(b, sh, CH - 1, 0)
                    second(b, sh, CH - 1, 1)

        @block.scalar
        def _(act):
            def step(b, sh, c, jj):
                n = pair_index(b, sh, c, jj)
                act.wait_ge(h_done, n + 1)
                if not (isinstance(c, int) and c == 0 and sh == 0):
                    act.wait_ge(mult_done, n)
                else:
                    act.wait_ge(mult_done, b * (2 * PAIRS) + 1)
                nc.scalar.activation(act_out[jj][:, :, :], ps[:, 2 * jj:2 * jj + 2, 0:BN],
                                     ACT.Gelu_apprx_tanh).then_inc(gelu_done, 1)
            start(act, gelu_done)
            walk(act, step)

        @block.vector
        def _(dve):
            def step(b, sh, c, jj):
                n = pair_index(b, sh, c, jj)
                dve.wait_ge(gelu_done, n + 2)
                dve.wait_ge(w_done, n + 1)
                if not (isinstance(c, int) and c == 0 and sh == 0):
                    dve.wait_ge(y_done, n)
                else:
                    dve.wait_ge(y_done, b * (2 * PAIRS) + 1)
                nc.vector.tensor_tensor(weighted[jj][:, :, :], act_out[jj][:, :, :], ps[:, 4:6, 0:BN],
                                        ALU.mult).then_inc(mult_done, 1)
                if isinstance(c, int) and c == CH - 1 and jj == 1:
                    dve.wait_ge(y_done, n + 2)
                    nc.vector.tensor_scalar(comb[:, sh, bass.ds(b * BN, BN)], ps[:, 6 + sh, 0:BN], 0.0, None,
                                            ALU.add).then_inc(comb_copied, 1)
            start(dve, mult_done, comb_copied)
            walk(dve, step)

        @block.gpsimd
        def _(pool):
            w2 = held["W2"][:, :].rearrange("p (c j r) -> p c j r", j=4, r=32)

            def step(b, sh, c, jj):
                n = pair_index(b, sh, c, jj)
                if not (isinstance(c, int) and c == 0 and sh == 0):
                    pool.wait_ge(y_done, n)
                else:
                    pool.wait_ge(y_done, b * (2 * PAIRS) + 1)
                pass_gate(pool, gate)
                nc.gpsimd.tensor_copy(w2s[jj][:, :, :].rearrange("p k r -> p (k r)"),
                                      held["W2"][:, bass.ds((sh * CH + c) * 128 + jj * 64, 64)]).then_inc(w2_ready, 1)
            walk(pool, step)


def quantised(nc, sem, sb, ps, held, hT, out, V):
    win = sb("w_in_t", [EC, 2, 2 * FF], BF16)
    wout = sb("w_out_t", [128, 4, E], BF16)
    wsum = sb("w_sums", [128, 2])
    wscale = sb("w_scales", [128, 2])
    winv = sb("w_inv", [128, 2])
    ones128 = held["den"]

    prep, summed, inv_ready, rounded = sem("wq_sums"), sem("wq_summed"), sem("wq_inverted"), sem("wq_rounded")
    sizes = (E * 2 * FF, E * FF)
    with nc.Block() as block:
        @block.vector
        def _(dve):
            nc.vector.memset(wsum[:, :], 0.0).then_inc(prep, 1)
            dve.wait_ge(prep, 1)
            nc.vector.tensor_reduce(wsum[0:EC, 0:1], held["w_in"][:, :, :], AX.XY, ALU.add,
                                    apply_absolute_value=True).then_inc(prep, 1)
            nc.vector.tensor_reduce(wsum[:, 1:2], held["w_out"][:, :, :], AX.XY, ALU.add,
                                    apply_absolute_value=True).then_inc(prep, 1)
            for k in range(2):
                dve.wait_ge(summed, 1)
                nc.vector.tensor_scalar(wscale[:, k:k + 1], ps[:, 0, k:k + 1], 1.0 / sizes[k], Q_EPS, ALU.mult,
                                        ALU.max).then_inc(inv_ready, 1)
            dve.wait_ge(inv_ready, 2)
            nc.vector.reciprocal(winv[:, :], wscale[:, :]).then_inc(inv_ready, 1)
            dve.wait_ge(inv_ready, 3)
            n = 0
            for w, q, k in ((held["w_in"], win, 0), (held["w_out"], wout, 1)):
                rows = w.shape[0]
                nc.vector.tensor_scalar(w[:], w[:], winv[0:rows, k:k + 1], ROUND, ALU.mult,
                                        ALU.add).then_inc(rounded, 1)
                n += 1
                dve.wait_ge(rounded, n)
                nc.vector.tensor_scalar(w[:], w[:], ROUND, -1.0, ALU.subtract, ALU.max).then_inc(rounded, 1)
                n += 1
                dve.wait_ge(rounded, n)
                nc.vector.tensor_scalar(q[:], w[:], 1.0, None, ALU.min).then_inc(rounded, 1)
                n += 1

        @block.tensor
        def _(pe):
            pe.wait_ge(prep, 3)
            nc.tensor.matmul(ps[:, 0, 0:2], held["all_ones"][:, :], wsum[:, :], start=True, stop=True).then_inc(
                summed, 1)

    hs = [sb(f"h_slice{p}", [EC, 2, GT]) for p in range(2)]
    ht = [sb(f"h_tokens{p}", [GT, E]) for p in range(2)]
    stats = sb("bn_stats", [GT, 6])
    mv = sb("mean_var", [GT, 2])
    xn = sb("x_normed", [GT, E])
    junk = sb("squares", [GT, FF])
    col = sb("token_scalars", [GT, 16])
    qx = sb("x_rounded", [GT, E])
    qb = sb("x_quantised", [GT, E], BF16)
    qt = sb("x_quantised_t", [EC, 2, GT], BF16)
    sil = sb("silu_gate", [GT, FF])
    y = sb("y", [GT, FF])
    yb = sb("y_quantised", [GT, FF], BF16)
    yt = sb("y_quantised_t", [128, 4, GT], BF16)
    res = [sb(f"result{p}", [GT, E]) for p in range(2)]
    (RSTD, SS, RMS, AMAX, QS, DQ, SS2, RMS2, AMAX2, QS2, DQ2) = range(11)

    def c(k):
        return col[:, k:k + 1]

    steps = {
        "pool": "sliced",
        "pe": "turned qt_ps h_ps yt_ps o_ps",
        "act": "std ss rms qt_sb sil ss2 rms2 yt_sb",
        "dve": "tokens stats mv rstd xn rrms scaled amax amaxc qinv dq qs q1 q2 q3 y rrms2 scaled2 amax2 amax2c qinv2 "
               "dq2 qs2 y1 y2 y3 res",
    }
    done = {e: sem(f"f1_{e}_steps") for e in steps}
    place = {name: (e, k, len(v.split())) for e, v in steps.items() for k, name in enumerate(v.split())}

    def wait(eng, name, i):
        e, k, n = place[name]
        eng.wait_ge(done[e], i * n + (k + 1))

    sm = {name: done[e] for name, (e, _, _) in place.items()}
    stored = [sem("stored_even"), sem("stored_odd")]
    gate = sem("f1_gate")

    with nc.Block() as block:
        @block.gpsimd
        def _(pool):
            def step(i, p):
                if not is_early(i):
                    wait(pool, "turned", i - 2)
                pool.wait_ge(rounded, 6)
                nc.gpsimd.tensor_copy(hs[p][:, :, :], hT[:, :, bass.ds(i * GT, GT)]).then_inc(sm["sliced"], 1)
            over_groups(pool, step)

        @block.tensor
        def _(pe):
            def step(i, p):
                first = isinstance(i, int) and i == 0
                wait(pe, "sliced", i)
                if not first:
                    wait(pe, "tokens", i - 1)
                for a in range(2):
                    last = nc.tensor.transpose(ps[0:GT, 0, a * EC:(a + 1) * EC], hs[p][:, a, :],
                                               held["ident"][0:EC, 0:EC])
                last.then_inc(sm["turned"], 1)
                wait(pe, "q3", i)
                for a in range(2):
                    last = nc.tensor.transpose(ps[0:EC, 1, :].bitcast(BF16)[:, a * GT:(a + 1) * GT],
                                               qb[:, a * EC:(a + 1) * EC], held["identb"][0:GT, 0:GT])
                last.then_inc(sm["qt_ps"], 1)
                wait(pe, "qt_sb", i)
                if not first:
                    wait(pe, "y", i - 1)
                for n in range(2):
                    for a in range(2):
                        last = nc.tensor.matmul(ps[0:GT, 2 + n, :], qt[:, a, :], win[:, a, n * FF:(n + 1) * FF],
                                                start=a == 0, stop=a == 1)
                last.then_inc(sm["h_ps"], 1)
                wait(pe, "y3", i)
                for a in range(4):
                    last = nc.tensor.transpose(ps[:, 4, :].bitcast(BF16)[:, a * GT:(a + 1) * GT],
                                               yb[:, a * 128:(a + 1) * 128], held["identb"][0:GT, 0:GT])
                last.then_inc(sm["yt_ps"], 1)
                wait(pe, "yt_sb", i)
                if not first:
                    wait(pe, "res", i - 1)
                for a in range(4):
                    last = nc.tensor.matmul(ps[0:GT, 5, 0:E], yt[:, a, :], wout[:, a, :], start=a == 0, stop=a == 3)
                last.then_inc(sm["o_ps"], 1)
            over_groups(pe, step)

        @block.scalar
        def _(act):
            def step(i, p):
                wait(act, "mv", i)
                nc.scalar.activation(c(RSTD), mv[:, 1:2], ACT.Sqrt, bias=V["rms_ln"][0:GT]).then_inc(sm["std"], 1)
                wait(act, "xn", i)
                nc.scalar.activation(junk[:, 0:E], xn[:, :], ACT.Square, accum_out=c(SS)).then_inc(sm["ss"], 1)
                wait(act, "ss", i)
                nc.scalar.activation(c(RMS), c(SS), ACT.Sqrt, bias=V["rms_eps"][0:GT], scale=1.0 / E).then_inc(
                    sm["rms"], 1)
                wait(act, "qt_ps", i)
                nc.scalar.copy(qt[:, :, :].rearrange("p a t -> p (a t)"),
                               ps[0:EC, 1, :].bitcast(BF16)[:, 0:2 * GT]).then_inc(sm["qt_sb"], 1)
                wait(act, "h_ps", i)
                wait(act, "dq", i)
                nc.scalar.activation(sil[:, :], ps[0:GT, 3, :], ACT.Silu, scale=c(DQ)).then_inc(sm["sil"], 1)
                wait(act, "y", i)
                nc.scalar.activation(junk[:, :], y[:, :], ACT.Square, accum_out=c(SS2)).then_inc(sm["ss2"], 1)
                wait(act, "ss2", i)
                nc.scalar.activation(c(RMS2), c(SS2), ACT.Sqrt, bias=V["rms_eps"][0:GT], scale=1.0 / FF).then_inc(
                    sm["rms2"], 1)
                wait(act, "yt_ps", i)
                nc.scalar.copy(yt[:, :, :].rearrange("p a t -> p (a t)"),
                               ps[:, 4, :].bitcast(BF16)[:, 0:4 * GT]).then_inc(sm["yt_sb"], 1)
            over_groups(act, step)

        @block.vector
        def _(dve):
            def step(i, p):
                n = i + 1

                def quantise(x, width, gain, amax, qs, dq, k, q1, q2, q3, qout, t):
                    nc.vector.tensor_reduce(c(amax), x, AX.X, ALU.max, apply_absolute_value=True).then_inc(
                        sm["amax" + t], 1)
                    wait(dve, "amax" + t, i)
                    nc.vector.tensor_scalar(c(amax), c(amax), Q_EPS, None, ALU.max).then_inc(sm[f"amax{t}c"], 1)
                    wait(dve, f"amax{t}c", i)
                    nc.vector.reciprocal(c(qs), c(amax)).then_inc(sm["qinv" + t], 1)
                    nc.vector.tensor_scalar(c(dq), c(amax), wscale[0:GT, k:k + 1], 1.0 / 127.0, ALU.mult,
                                            ALU.mult).then_inc(sm["dq" + t], 1)
                    wait(dve, "qinv" + t, i)
                    nc.vector.tensor_scalar(c(qs), c(qs), 127.0, None, ALU.mult).then_inc(sm["qs" + t], 1)
                    wait(dve, "qs" + t, i)
                    nc.vector.tensor_scalar(x, x, c(qs), ROUND, ALU.mult, ALU.add).then_inc(sm[q1], 1)
                    wait(dve, q1, i)
                    nc.vector.tensor_scalar(x, x, ROUND, 127.0, ALU.subtract, ALU.min).then_inc(sm[q2], 1)
                    wait(dve, q2, i)
                    nc.vector.tensor_scalar(qout, x, -128.0, None, ALU.max).then_inc(sm[q3], 1)

                wait(dve, "turned", i)
                nc.vector.tensor_copy(ht[p][:, :], ps[0:GT, 0, 0:E]).then_inc(sm["tokens"], 1)
                wait(dve, "tokens", i)
                nc.vector.bn_stats(stats[:, :], ht[p][:, :]).then_inc(sm["stats"], 1)
                wait(dve, "stats", i)
                pass_gate(dve, gate)
                nc.vector.bn_aggr(mv[:, :], stats[:, :]).then_inc(sm["mv"], 1)
                wait(dve, "std", i)
                nc.vector.reciprocal(c(RSTD), c(RSTD)).then_inc(sm["rstd"], 1)
                wait(dve, "rstd", i)
                nc.vector.tensor_scalar(xn[:, :], ht[p][:, :], mv[:, 0:1], c(RSTD), ALU.subtract,
                                        ALU.mult).then_inc(sm["xn"], 1)
                wait(dve, "rms", i)
                nc.vector.reciprocal(c(RMS), c(RMS)).then_inc(sm["rrms"], 1)
                wait(dve, "rrms", i)
                nc.vector.scalar_tensor_tensor(qx[:, :], xn[:, :], c(RMS), held["gb_in"][0:GT, :], ALU.mult,
                                               ALU.mult).then_inc(sm["scaled"], 1)
                wait(dve, "scaled", i)
                quantise(qx[:, :], E, None, AMAX, QS, DQ, 0, "q1", "q2", "q3", qb[:, :], "")
                wait(dve, "sil", i)
                nc.vector.scalar_tensor_tensor(y[:, :], ps[0:GT, 2, :], c(DQ), sil[:, :], ALU.mult,
                                               ALU.mult).then_inc(sm["y"], 1)
                wait(dve, "rms2", i)
                nc.vector.reciprocal(c(RMS2), c(RMS2)).then_inc(sm["rrms2"], 1)
                wait(dve, "rrms2", i)
                nc.vector.scalar_tensor_tensor(y[:, :], y[:, :], c(RMS2), held["gb_out"][0:GT, :], ALU.mult,
                                               ALU.mult).then_inc(sm["scaled2"], 1)
                wait(dve, "scaled2", i)
                quantise(y[:, :], FF, None, AMAX2, QS2, DQ2, 1, "y1", "y2", "y3", yb[:, :], "2")
                wait(dve, "o_ps", i)
                if not is_early(i):
                    dve.wait_ge(stored[p], (i - p) * 8)
                nc.vector.scalar_tensor_tensor(res[p][:, :], ps[0:GT, 5, 0:E], c(DQ2), ht[p][:, :], ALU.mult,
                                               ALU.add).then_inc(sm["res"], 1)
            over_groups(dve, step)

        @block.sync
        def _(sp):
            def step(i, p):
                wait(sp, "res", i)
                rows = GT if not is_last(i) else IMAGES * TOK - (GROUPS - 1) * GT
                sp.dma_start(out[bass.ds(i * GT, rows), :], res[p][0:rows, :]).then_inc(stored[p], 16)
            over_groups(sp, step)
            sp.wait_ge(stored[0], 16 * ((GROUPS + 1) // 2))
            sp.wait_ge(stored[1], 16 * (GROUPS // 2))



def laid_out(x, np, bf16):
    f = np.float32
    a = {k: np.asarray(v) for k, v in x.items()}
    out = {}
    z = lambda *s: np.zeros(s, f)
    xt = z(PK * 128, NT)
    xt[:, :IMAGES * TOK] = a["x"].reshape(IMAGES, 3, GRID, PATCH, GRID, PATCH).transpose(1, 3, 5, 0, 2, 4).reshape(
        PK * 128, IMAGES * TOK)
    out["xt"] = xt.reshape(PK, 128, NT).transpose(1, 0, 2)
    out["tok_w"] = a["L0_tok_W"].reshape(E, PK, 128).transpose(2, 1, 0)

    def rows(w):
        return w.reshape(2, EC, -1).transpose(1, 0, 2)

    def by_head(w):
        p = z(w.shape[0], HEADS, 32)
        p[:, :, :HD] = w.reshape(w.shape[0], HEADS, HD)
        return rows(p.reshape(w.shape[0], -1)).reshape(EC, 2, HG, 128)

    def by_head_rows(w):
        p = z(HG, 4, 32, E)
        p[:, :, :HD] = w.reshape(HG, 4, HD, E)
        return p.transpose(1, 2, 0, 3).reshape(128, HG, E)

    qkv = a["L0_attn_w_qkv"]
    out["wq0"], out["wk0"], out["wv0"] = by_head(qkv[:, :E]), by_head(qkv[:, E:2 * E]), rows(qkv[:, 2 * E:])
    out["wp0"] = by_head_rows(a["L0_attn_w_proj"])
    R0, C0, ONE, MAXREL = HD, HD + ROWS + 1, 30, 14
    kc = z(4, 32, TOK)
    kc[:, R0 + ROWS, 0] = kc[:, C0 + COLS, 0] = 1
    for t in range(TOK - 1):
        kc[:, R0 + t // COLS, 1 + t] = kc[:, C0 + t % COLS, 1 + t] = 1
    out["kconst"] = kc.reshape(128, TOK)

    def classes(tab, n, base, value_side, identity):
        m = z(n + 1, 4, 32, 4, 32)
        for k in range(n + 1):
            idx = [0 if k == n or j == n else min(max(j - k, -MAXREL), MAXREL) + MAXREL + 1 for j in range(n + 1)]
            for h in range(4):
                blk = tab[idx]
                if value_side:
                    m[k, h, base:base + n + 1, h, :HD] = blk
                else:
                    m[k, h, :HD, h, base:base + n + 1] = blk.T
                if identity:
                    m[k, h, range(HD), h, range(HD)] = 1
        return m.reshape(n + 1, 128, 128).transpose(1, 0, 2)

    out["av"] = classes(a["L0_attn_tab_vk"], ROWS, R0, False, True)
    out["ah"] = classes(a["L0_attn_tab_hk"], COLS, C0, False, False)
    out["bv"] = classes(a["L0_attn_tab_vv"], ROWS, R0, True, True)
    out["bh"] = classes(a["L0_attn_tab_hv"], COLS, C0, True, False)
    den = z(4, 32, 4, 32)
    for h in range(4):
        den[h, ONE, h, :] = 1
    out["den"] = den.reshape(128, 128)
    out["blocks4"] = np.repeat(np.eye(4, dtype=f), 32, axis=0)
    img = np.arange(GT) // TOK
    same = img[:, None] == img[None, :]
    causal = same & (np.arange(GT)[None, :] <= np.arange(GT)[:, None])
    out["mask0"] = np.tile(np.where(same, 0, NEG).astype(f), (1, 4)).astype(bf16)
    m1 = np.where(causal, 0, NEG).astype(f)
    m1 = np.concatenate([m1, z(GT, 1)], axis=1)
    out["mask1"] = np.tile(m1, (1, 4)).astype(bf16)
    v0 = z(GT, HEADS, 32)
    for t in range(GT):
        p = t % TOK
        v0[t, :, R0 + (ROWS if p == 0 else (p - 1) // COLS)] = 1
        v0[t, :, C0 + (COLS if p == 0 else (p - 1) % COLS)] = 1
    v0[:, :, ONE] = 1
    out["v_start0"] = v0
    v1 = z(GT + 1, HEADS, 32)
    v1[:, :, ONE] = 1
    out["v_start1"] = v1
    out["ones"] = np.full((EC, EC), 1.0 / E, f)
    out["all_ones"] = np.ones((128, 128), f)
    out["ident"] = np.eye(128, dtype=f)
    out["identb"] = np.eye(128, dtype=f).astype(bf16)
    out["P"] = rows(a["L0_ffn_P"].transpose(1, 0, 2).reshape(E, S_ * R_))
    C = z(S_, R_, S_, M_)
    b2 = z(2, M_, S_ // 2, 4, 32)
    for s in range(S_):
        C[s, :, s, :] = a["L0_ffn_C"][s].T
        b2[s % 2, :, s // 2, s % 4, :R_] = a["L0_ffn_b2"][s]
    out["C"] = C.reshape(128, S_ * M_)
    out["b2"] = b2.reshape(128, S_ // 2, 128)
    out["W1"] = a["L0_ffn_W1"].transpose(0, 2, 1, 3).reshape(S_ * R_, M_ * H_)
    out["b1"] = a["L0_ffn_b1"].reshape(S_, M_ * H_)
    w2 = z(S_, CH, 128, 32)
    w2[..., :R_] = a["L0_ffn_W2"].reshape(S_, CH, 128, R_)
    out["W2"] = w2.reshape(2, 4, CH, 128, 32).transpose(3, 0, 2, 1, 4).reshape(128, -1)
    sel = z(3, 32, 8, 4, H_)
    for c in range(8):
        for m in range(4):
            sel[:, 4 * c + m, c, m, :] = 1
    out["sel"] = sel.reshape(96, 8 * 128).astype(bf16)
    g1 = z(4, 32, 2, G_)
    g1[:, :R_] = a["L0_ffn_G1"].reshape(2, 4, R_, G_).transpose(1, 2, 0, 3)
    out["G1"] = g1.reshape(128, 2, G_)
    out["G2"] = a["L0_ffn_G2"]
    w, bq = a["L1_attn_W_attn"], a["L1_attn_b_attn"]
    out["wq1"], out["wk1"], out["wv1"] = by_head(w[:, :E]), by_head(w[:, E:2 * E]), rows(w[:, 2 * E:])
    out["wp1"] = by_head_rows(a["L1_attn_W_proj"])
    out["vb1"] = np.broadcast_to(bq[2 * E:].reshape(1, HEADS, HD), (GT, HEADS, HD))
    rot = z(4, 32, 4, 32)
    cos, sin = z(4, 32, TOK), z(4, 32, TOK)
    freqs = (1.0 / np.float32(10000.0) ** (np.arange(0, HD, 2, dtype=f) / np.float32(HD))).astype(f)
    ang = np.outer(np.arange(TOK, dtype=f), freqs).astype(f)
    for d in range(HD):
        cos[:, d, :] = np.cos(ang[:, d // 2])
        sin[:, d, :] = np.sin(ang[:, d // 2])
    for h in range(4):
        for d in range(0, HD, 2):
            rot[h, d + 1, h, d] = -1
            rot[h, d, h, d + 1] = 1
    out["rot"] = rot.reshape(128, 128)
    cq = cos * f(HD ** -0.5)
    cq[:, 31] = 1
    out["cosq"], out["sinq"] = cq.reshape(128, TOK), (sin * f(HD ** -0.5)).reshape(128, TOK)
    out["cosk"], out["sink_"] = cos.reshape(128, TOK), sin.reshape(128, TOK)
    sk = z(4, 32, HG, 4)
    for h in range(4):
        sk[h, 31, :, h] = a["L1_attn_sinks"].reshape(HG, 4)[:, h]
    out["sinkcol"] = sk.reshape(128, HG, 4)
    out["gb_in"] = np.broadcast_to(a["L1_ffn_g_in"], (128, E))
    out["gb_out"] = np.broadcast_to(a["L1_ffn_g_out"], (128, FF))
    out["w_in"] = rows(a["L1_ffn_w_in"].T)
    out["w_out"] = a["L1_ffn_w_out"].T.reshape(4, 128, E).transpose(1, 0, 2)

    def by_head_vec(v, one=0):
        p = z(HG, 4, 32)
        p[..., :HD] = v.reshape(HG, 4, HD)
        p[..., 31] = one
        return p.reshape(HG, 128).T

    cols = {"tok_b": a["L0_tok_b"].reshape(2, EC).T, "ln_eps": np.full((128, 1), LN_EPS, f),
            "bp0": a["L0_attn_b_proj"].reshape(2, EC).T, "g2b": a["L0_ffn_g2b"].reshape(2, EC).T,
            "g1b": a["L0_ffn_g1b"].reshape(G_, 1), "norm_scale": a["L1_attn_norm_scale"].reshape(2, EC).T,
            "norm_bias": a["L1_attn_norm_bias"].reshape(2, EC).T, "bq1": by_head_vec(bq[:E], 1),
            "bk1": by_head_vec(bq[E:2 * E]), "bp1": a["L1_attn_b_proj"].reshape(2, EC).T,
            "rezero": np.broadcast_to(a["L1_attn_rezero"].reshape(1, 1), (128, 1)),
            "rms_eps": np.full((128, 1), RMS_EPS, f), "rms_ln": np.full((128, 1), LN_EPS, f)}
    vec = z(128, sum(k for _, k in VEC))
    at = 0
    for n, k in VEC:
        vec[:cols[n].shape[0], at:at + k] = cols[n]
        at += k
    out["vec"] = vec
    return {k: np.ascontiguousarray(v) for k, v in out.items()}



def kernel(**inputs):
    import numpy as _np
    import ml_dtypes as _ml
    import concourse.bacc as _bacc
    from concourse import mybir as _mybir
    from concourse.bass_utils import run_bass_kernel_spmd as _run

    nc = _bacc.Bacc("TRN2", target_bir_lowering=False, num_devices=1)
    arrays, args = {}, {}
    for name, a in laid_out(inputs, _np, _ml.bfloat16).items():
        arrays[f"in_{name}_dram"] = a
        args[name] = nc.dram_tensor(f"in_{name}_dram", a.shape, _mybir.dt.from_np(a.dtype), kind="ExternalInput").ap()
    out = nc.dram_tensor("out_0_dram", (IMAGES * TOK, E), F32, kind="ExternalOutput").ap()
    program(nc, args, out)
    r = _run(nc, [arrays], core_ids=[0])
    return r.results[0]["out_0_dram"].reshape(IMAGES, TOK, E)
```

```python
import concourse.bass as bass
from concourse import mybir
from contextlib import ExitStack

F32, BF16 = mybir.dt.float32, mybir.dt.bfloat16
ACT, ALU, AX = mybir.ActivationFunctionType, mybir.AluOpType, mybir.AxisListType

IMAGES, SIDE, PATCH = 32, 96, 16
GRID = SIDE // PATCH
TOK = GRID * GRID
E = 192
EC = E // 2
HEADS, HD = 12, 16
HG = HEADS // 4
PER = 3
GROUPS = -(-IMAGES // PER)
GT = PER * TOK
IMG_P = GROUPS * PER
NT = IMG_P * TOK
BL = 3
BN = NT // BL
BIMG = BN // TOK
EB = IMAGES * TOK // BL
PK = 3 * PATCH * PATCH // 128
ROWS, COLS = 7, 5
S_, R_, M_, H_, TOPK, G_ = 8, 16, 64, 32, 4, 64
CH = M_ * H_ // 128
FF = 512
LN_EPS, RMS_EPS, Q_EPS = 1e-5, 1e-6, 1e-5
NEG, TAKEN, SENTINEL = -1e30, -1e38, -3e38
ROUND = 1.5 * 2.0 ** 23


def spread(ap, axis, n):
    ap = ap.unsqueeze(axis)
    shape = list(ap.shape)
    shape[axis] = n
    return ap.to_broadcast(shape)


def over_groups(eng, step):
    step(0, 0)
    step(1, 1)
    with eng.Fori(1, GROUPS // 2) as pair:
        step(pair * 2, 0)
        step(pair * 2 + 1, 1)
    if GROUPS % 2:
        step(GROUPS - 1, 0)


def pipeline(eng, step, length, lead=4):
    full = lead + (GROUPS - lead) // 2 * 2
    for k in range(lead):
        step(k, k % 2)
    with eng.Fori(lead // 2, full // 2) as pair:
        step(pair * 2, 0)
        step(pair * 2 + 1, 1)
    for k in range(full, length):
        step(k, k % 2)


def is_group(i):
    return not isinstance(i, int) or 0 <= i < GROUPS


def is_early(i):
    return isinstance(i, int) and i < 2


def is_last(i):
    return isinstance(i, int) and i == GROUPS - 1


def pass_gate(eng, gate):
    eng.sem_inc(gate, 1)


def layer_norm(nc, tag, sem, ps, src, dst, centred, squared, rstd, ones, eps, scale=None, bias=None):
    mean_ready, centred_ready, squared_ready = sem(f"{tag}_mean"), sem(f"{tag}_centred"), sem(f"{tag}_squared")
    var_ready, std_ready, rstd_ready = sem(f"{tag}_var"), sem(f"{tag}_std"), sem(f"{tag}_rstd")
    normed = sem(f"{tag}_normed")
    blocks = [slice(b * BN, (b + 1) * BN) for b in range(BL)]

    with nc.Block() as block:
        @block.tensor
        def _(pe):
            for b, cols in enumerate(blocks):
                for a in range(2):
                    last = nc.tensor.matmul(ps[0:EC, b, 0:BN], ones[:, :], src[:, a, cols], start=a == 0, stop=a == 1)
                last.then_inc(mean_ready, 1)
            for b, cols in enumerate(blocks):
                pe.wait_ge(squared_ready, b + 1)
                for a in range(2):
                    last = nc.tensor.matmul(ps[0:EC, BL + b, 0:BN], ones[:, :], squared[:, a, cols], start=a == 0,
                                            stop=a == 1)
                last.then_inc(var_ready, 1)

        @block.scalar
        def _(act):
            for b, cols in enumerate(blocks):
                act.wait_ge(centred_ready, b + 1)
                nc.scalar.activation(squared[:, :, cols], centred[:, :, cols], ACT.Square).then_inc(squared_ready, 1)
            for b, cols in enumerate(blocks):
                act.wait_ge(var_ready, b + 1)
                nc.scalar.activation(rstd[:, cols], ps[0:EC, BL + b, 0:BN], ACT.Sqrt, bias=eps).then_inc(std_ready, 1)

        @block.vector
        def _(dve):
            for b, cols in enumerate(blocks):
                dve.wait_ge(mean_ready, b + 1)
                nc.vector.tensor_tensor(centred[:, :, cols], src[:, :, cols], spread(ps[0:EC, b, 0:BN], 1, 2),
                                        ALU.subtract).then_inc(centred_ready, 1)
            for b, cols in enumerate(blocks):
                dve.wait_ge(std_ready, b + 1)
                nc.vector.reciprocal(rstd[:, cols], rstd[:, cols]).then_inc(rstd_ready, 1)
                dve.wait_ge(rstd_ready, b + 1)
                nc.vector.tensor_tensor(dst[:, :, cols], centred[:, :, cols], spread(rstd[:, cols], 1, 2),
                                        ALU.mult).then_inc(normed, 1)
            if scale is not None:
                dve.wait_ge(normed, BL)
                for a in range(2):
                    nc.vector.tensor_scalar(dst[:, a, :], dst[:, a, :], scale[:, a:a + 1], bias[:, a:a + 1],
                                            ALU.mult, ALU.add)


def attention(nc, tag, sem, sb, ps, QT, KT, UT, xnT, wv, v_bias, v_start, mask, blocks4, ident, identb, sink=None):
    KW = GT + (sink is not None)
    qs = [sb(f"{tag}_queries{p}", [128, HG, GT]) for p in range(2)]
    xs = [sb(f"{tag}_tokens{p}", [EC, 2, GT]) for p in range(2)]
    kd = [sb(f"{tag}_keys_by_head{p}", [128, HG, 4, KW]) for p in range(2)]
    va = [sb(f"{tag}_values{p}", [KW, HEADS, 32]) for p in range(2)]
    probs = [sb(f"{tag}_probs{p}", [GT, HEADS, KW]) for p in range(2)]
    pt = [sb(f"{tag}_probs_by_key{p}", [KW, HEADS, GT]) for p in range(2)]
    top = sb(f"{tag}_row_max", [GT, HEADS])
    scores = ps[0:GT, 0:HG, 0:4 * KW].rearrange("q g (h k) -> q g h k", h=4)
    probs_ps = ps[0:KW, HG:2 * HG, 0:4 * GT]
    v_ps = ps[0:GT, 6, 0:E]
    u_ps = ps[:, 7, 0:HG * GT]

    filled = sem(f"{tag}_constant_parts_filled")
    sliced, keys_ready, v_done = sem(f"{tag}_sliced"), sem(f"{tag}_keys"), sem(f"{tag}_v_product")
    values_ready, scored = sem(f"{tag}_values_ready"), sem(f"{tag}_scored")
    max_ready, shifted, exp_ready = sem(f"{tag}_max"), sem(f"{tag}_shifted"), sem(f"{tag}_exp")
    turned, turned_copied = sem(f"{tag}_turned"), sem(f"{tag}_turned_copied")
    summed, summed_copied = sem(f"{tag}_summed"), sem(f"{tag}_summed_copied")

    def cols(i):
        return bass.ds(i * GT, GT)

    with nc.Block() as block:
        @block.gpsimd
        def _(pool):
            for p in range(2):
                nc.gpsimd.tensor_copy(va[p][:, :, :], v_start[:, :, :]).then_inc(filled, 1)
            if sink is not None:
                for p in range(2):
                    nc.gpsimd.tensor_copy(kd[p][:, :, :, GT], sink[:, :, :]).then_inc(filled, 1)

            def step(i, p):
                if not is_early(i):
                    pool.wait_ge(scored, i - 1)
                pool.wait_ge(filled, 2)
                nc.gpsimd.tensor_copy(qs[p][:, :, :], QT[:, :, cols(i)]).then_inc(sliced, 1)
                nc.gpsimd.tensor_copy(xs[p][:, :, :], xnT[:, :, cols(i)]).then_inc(sliced, 1)
            over_groups(pool, step)

        @block.tensor
        def _(pe):
            def values_and_scores(i, p):
                pe.wait_ge(sliced, 2 * i + 2)
                if not (isinstance(i, int) and i < 1):
                    pe.wait_ge(values_ready, i)
                for a in range(2):
                    last = nc.tensor.matmul(v_ps, xs[p][:, a, :], wv[:, a, :], start=a == 0, stop=a == 1)
                last.then_inc(v_done, 1)
                pe.wait_ge(keys_ready, i + 1)
                if not (isinstance(i, int) and i < 1):
                    pe.wait_ge(shifted, i)
                for g in range(HG):
                    out = ps[0:GT, g, 0:4 * KW]
                    nc.tensor.matmul(out, identb[0:GT, 0:GT], mask[:, :], start=True, stop=False)
                    last = nc.tensor.matmul(out, qs[p][:, g, :], kd[p][:, g, :, :].rearrange("p h k -> p (h k)"),
                                            start=False, stop=True)
                last.then_inc(scored, 1)

            def weighted_sums(i, p):
                pe.wait_ge(exp_ready, i + 1)
                for g in range(HG):
                    if not (isinstance(i, int) and i < 1):
                        pe.wait_ge(turned_copied, 3 * i + g - 2)
                    for h in range(4):
                        last = nc.tensor.transpose(ps[0:KW, HG + g, h * GT:(h + 1) * GT], probs[p][:, 4 * g + h, :],
                                                   ident[0:GT, 0:GT])
                    last.then_inc(turned, 1)
                pe.wait_ge(values_ready, i + 1)
                if not (isinstance(i, int) and i < 1):
                    pe.wait_ge(summed_copied, i)
                for g in range(HG):
                    pe.wait_ge(turned_copied, 3 * i + g + 1)
                    for h in range(4):
                        last = nc.tensor.matmul(ps[32 * h:32 * h + 32, 7, g * GT:(g + 1) * GT], va[p][:, 4 * g + h, :],
                                                pt[p][:, 4 * g + h, :], start=True, stop=True)
                last.then_inc(summed, 1)

            values_and_scores(0, 0)

            def step(i, p):
                if not is_last(i):
                    values_and_scores(i + 1, 1 - p)
                weighted_sums(i, p)
            over_groups(pe, step)

        @block.vector
        def _(dve):
            def keys(i, p):
                if not is_early(i):
                    dve.wait_ge(scored, i - 1)
                for g in range(HG):
                    last = nc.vector.tensor_tensor(kd[p][:, g, :, 0:GT], spread(KT[:, g, cols(i)], 1, 4),
                                                   spread(blocks4[:, :], 2, GT), ALU.mult)
                last.then_inc(keys_ready, 1)

            if sink is not None:
                dve.wait_ge(filled, 4)
            keys(0, 0)

            def step(i, p):
                if not is_last(i):
                    keys(i + 1, 1 - p)
                if not is_early(i):
                    dve.wait_ge(summed, i - 1)
                dve.wait_ge(filled, 2)
                dve.wait_ge(v_done, i + 1)
                out = va[p][0:GT, :, 0:HD]
                v = v_ps.rearrange("k (h d) -> k h d", h=HEADS)
                if v_bias is None:
                    nc.vector.tensor_copy(out, v).then_inc(values_ready, 1)
                else:
                    nc.vector.tensor_tensor(out, v, v_bias[:, :, :], ALU.add).then_inc(values_ready, 1)
                dve.wait_ge(scored, i + 1)
                nc.vector.reduce_max(top[:, :].rearrange("q (g h) -> q g h", g=HG), scores, AX.X).then_inc(max_ready, 1)
                dve.wait_ge(max_ready, i + 1)
                if not is_early(i):
                    dve.wait_ge(turned, 3 * i - 3)
                out = probs[p][:, :, :].rearrange("q (g h) k -> q g h k", g=HG)
                nc.vector.tensor_tensor(out, scores, spread(top[:, :].rearrange("q (g h) -> q g h", g=HG), 3, KW),
                                        ALU.subtract).then_inc(shifted, 1)
            over_groups(dve, step)

        @block.scalar
        def _(act):
            def exponentials(i, p):
                act.wait_ge(shifted, i + 1)
                nc.scalar.activation(probs[p][:, :, :], probs[p][:, :, :], ACT.Exp).then_inc(exp_ready, 1)

            exponentials(0, 0)

            def step(i, p):
                for g in range(HG):
                    if not is_early(i) and g == 0:
                        act.wait_ge(summed, i - 1)
                    act.wait_ge(turned, 3 * i + g + 1)
                    nc.scalar.copy(pt[p][:, 4 * g:4 * g + 4, :].rearrange("k h q -> k (h q)"),
                                   probs_ps[:, g, :]).then_inc(turned_copied, 1)
                if not is_last(i):
                    exponentials(i + 1, 1 - p)
                act.wait_ge(summed, i + 1)
                act.wait_ge(filled, 2)
                nc.scalar.copy(UT[:, :, cols(i)], u_ps.rearrange("p (g q) -> p g q", g=HG)).then_inc(summed_copied, 1)
            over_groups(act, step)


def free_size(shape):
    n = 1
    for k in shape[1:]:
        n *= k
    return n


PACKS = {
    "first": ("tok_w", "vec"),
    "kept": ("ones", "ident", "identb", "blocks4", "den_rows", "den_back", "P", "C", "sel", "b2", "G1", "G2"),
    "attention0": ("wq0", "wk0", "av", "ah", "kconst", "mask0", "wv0", "v_start0", "bv", "bh", "wp0"),
    "attention1": ("wq1", "wk1", "rot", "cosq", "sinq", "cosk", "sink_", "mask1", "wv1", "vb1", "v_start1", "sinkcol",
                   "wp1"),
    "feed_forward1": ("gb_in", "gb_out", "w_in", "w_out", "all_ones"),
}


def program(nc, ins, shapes, ins_types, out):
    with ExitStack() as ctx:
        def sem(name):
            return ctx.enter_context(nc.semaphore(name))

        def allocator(stack):
            return lambda name, shape, dt=F32: stack.enter_context(nc.sbuf_tensor(name, shape, dt))

        gate = sem("gate")
        sb = allocator(ctx)
        ps = ctx.enter_context(nc.psum_tensor("banks", [128, 8, 512], F32))

        held = {}
        def hold(stack, pack):
            for dt, tail in ((F32, "f"), (BF16, "b")):
                names = [n for n in PACKS[pack] if ins_types[n] == dt]
                if names:
                    width = sum(free_size(shapes[n]) for n in names)
                    tile = allocator(stack)(f"pack_{pack}_{tail}", [128, width], dt)
                    packs[pack].append((tile, ins[f"pack_{pack}_{tail}"]))
                    at = 0
                    for n in names:
                        shape, size = shapes[n], free_size(shapes[n])
                        view = tile[0:shape[0], at:at + size]
                        if len(shape) == 3:
                            view = view.rearrange("p (a n) -> p a n", a=shape[1])
                        elif len(shape) == 4:
                            view = view.rearrange("p (a b n) -> p a b n", a=shape[1], b=shape[2])
                        held[n] = view
                        at += size

        packs = {pack: [] for pack in PACKS}
        loaded = {pack: sem(f"loaded_{pack}") for pack in PACKS}

        def load(eng, pack):
            for tile, src in packs[pack]:
                eng.dma_start(tile[:], src).then_inc(loaded[pack], 16)

        def await_pack(eng, pack):
            eng.wait_ge(loaded[pack], 16 * len(packs[pack]))

        hold(ctx, "first")
        hold(ctx, "kept")
        hT = sb("hT", [EC, 2, NT])
        xnT = sb("xnT", [EC, 2, NT])
        w_stack = sb("w1_parts_by_row", [128, S_, M_ * H_], BF16)
        w1_loaded, b1_loaded = sem("loaded_W1"), sem("loaded_b1")
        stacked_w = sem("w1_parts_stacked")
        vec = held["vec"]
        scratch = {"w1": nc.dram_tensor("scratch_w1", (3, S_ * R_, M_ * H_), BF16, kind="Internal").ap(),
                   "b1": nc.dram_tensor("scratch_b1", (3, S_, M_ * H_), BF16, kind="Internal").ap(),
                   "z": nc.dram_tensor("scratch_z", (3, S_ * R_, NT), BF16, kind="Internal").ap()}
        V = {}
        for i, (n, k) in enumerate(VEC):
            V[n] = vec[0:VROWS[n], sum(k for _, k in VEC[:i]):sum(k for _, k in VEC[:i + 1])]

        with ExitStack() as mem:
            hold(mem, "attention0")
            sb2 = allocator(mem)
            w1_parts = [sb2(f"w1_part{n}", [S_ * R_, M_ * H_], BF16) for n in range(3)]
            b1_parts = [sb2(f"b1_part{n}", [S_, M_ * H_], BF16) for n in range(3)]
            embed(nc, sem, allocator, ps, ins, held, load, await_pack, hT, V, w_stack, w1_loaded, b1_loaded,
                  w1_parts, b1_parts)
            s = allocator(mem)
            with ExitStack() as mem2:
                s2 = allocator(mem2)
                layer_norm(nc, "ln0", sem, ps, hT, xnT, s2("centred0", [EC, 2, NT]), s2("squared0", [EC, 2, NT]),
                           s2("rstd0", [EC, NT]), held["ones"], V["ln_eps"])
            QT, KT, UT = s("QT0", [128, HG, NT]), s("KT0", [128, HG, NT]), s("UT0", [128, HG, NT])
            project_qk0(nc, sem, ps, held, xnT, UT, QT, KT,
                        lambda sp: stack_w1(sp, w1_parts, b1_parts, scratch, sem("w1_parts_out"), w_stack, stacked_w))
            with ExitStack() as mem2:
                attention(nc, "a0", sem, allocator(mem2), ps, QT, KT, UT, xnT, held["wv0"], None, held["v_start0"],
                          held["mask0"], held["blocks4"], held["ident"], held["identb"])
            project_out0(nc, sem, s, ps, held, UT, QT, KT, hT, V)

        hold(ctx, "attention1")
        with ExitStack() as mem:
            s = allocator(mem)
            with ExitStack() as mem2:
                s2 = allocator(mem2)
                layer_norm(nc, "ln1", sem, ps, hT, xnT, s2("centred1", [EC, 2, NT]), s2("squared1", [EC, 2, NT]),
                           s2("rstd1", [EC, NT]), held["ones"], V["ln_eps"])
            experts(nc, sem, gate, s, allocator, ps, ins, held, load, await_pack, scratch, xnT, hT, w_stack, stacked_w, V)

        hold(ctx, "feed_forward1")
        with ExitStack() as mem:
            s = allocator(mem)
            with ExitStack() as mem2:
                s2 = allocator(mem2)
                layer_norm(nc, "ln2", sem, ps, hT, xnT, s2("centred2", [EC, 2, NT]), s2("squared2", [EC, 2, NT]),
                           s2("rstd2", [EC, NT]), held["ones"], V["ln_eps"], V["norm_scale"], V["norm_bias"])
            QT, KT, UT = s("QT1", [128, HG, NT]), s("KT1", [128, HG, NT]), s("UT1", [128, HG, NT])
            with ExitStack() as mem2:
                project_qk1(nc, sem, allocator(mem2), ps, held, load, await_pack, xnT, QT, KT, V)
            with ExitStack() as mem2:
                attention(nc, "a1", sem, allocator(mem2), ps, QT, KT, UT, xnT, held["wv1"], held["vb1"],
                          held["v_start1"], held["mask1"], held["blocks4"], held["ident"], held["identb"],
                          held["sinkcol"])
            project_out1(nc, sem, s, ps, held, UT, QT, hT, V)

        with ExitStack() as mem:
            quantised(nc, sem, gate, allocator(mem), ps, held, hT, out, V)


VEC = [("tok_b", 2), ("ln_eps", 1), ("bp0", 2), ("g2b", 2), ("g1b", 1), ("norm_scale", 2), ("norm_bias", 2),
       ("bq1", 3), ("bk1", 3), ("bp1", 2), ("rezero", 1), ("rms_eps", 1), ("rms_ln", 1)]
VROWS = {"tok_b": 96, "ln_eps": 96, "bp0": 96, "g2b": 96, "g1b": 64, "norm_scale": 96, "norm_bias": 96,
         "bq1": 128, "bk1": 128, "bp1": 96, "rezero": 96, "rms_eps": 128, "rms_ln": 128}


def embed(nc, sem, allocator, ps, ins, held, load, await_pack, hT, V, w_stack, w1_loaded, b1_loaded,
          w_part, b_part):
    with ExitStack() as mem:
        sb = allocator(mem)
        xt = sb("xt", [128, PK, NT])
        w1 = sb("w1", [S_ * R_, M_ * H_])
        b1 = sb("b1", [S_, M_ * H_])
        x_loaded = [sem(f"loaded_x{k}") for k in range(PK // 2)]
        tok_done, w_split, b_split, cleared = sem("tok_done"), sem("w1_split"), sem("b1_split"), sem("w_stack_cleared")

        with nc.Block() as block:
            @block.sync
            def _(sp):
                load(sp, "first")
                for k in range(PK // 2):
                    sp.dma_start(xt[:, 2 * k:2 * k + 2, :], ins["xt"][:, 2 * k:2 * k + 2, :]).then_inc(x_loaded[k], 16)
                load(sp, "kept")
                load(sp, "attention0")
                sp.dma_start(w1[:], ins["W1"]).then_inc(w1_loaded, 16)
                sp.dma_start(b1[:], ins["b1"]).then_inc(b1_loaded, 16)
                await_pack(sp, "kept")
                await_pack(sp, "attention0")

            @block.gpsimd
            def _(pool):
                rows = w_stack[64:128, :, :].rearrange("p s n -> p (s n)").bitcast(F32)
                nc.gpsimd.memset(rows, 0.0).then_inc(cleared, 1)
                pool.wait_ge(cleared, 1)

            @block.vector
            def _(dve):
                for x, part, ready, split in ((w1, w_part, w1_loaded, w_split), (b1, b_part, b1_loaded, b_split)):
                    dve.wait_ge(ready, 16)
                    nc.vector.tensor_copy(part[0][:], x[:]).then_inc(split, 1)
                    for n in (1, 2):
                        dve.wait_ge(split, 2 * n - 1)
                        nc.vector.tensor_tensor(x[:], x[:], part[n - 1][:], ALU.subtract).then_inc(split, 1)
                        dve.wait_ge(split, 2 * n)
                        nc.vector.tensor_copy(part[n][:], x[:]).then_inc(split, 1)

            @block.tensor
            def _(pe):
                await_pack(pe, "first")
                for k in range(PK):
                    pe.wait_ge(x_loaded[k // 2], 16)
                    for b in range(BL):
                        for a in range(2):
                            last = nc.tensor.matmul(ps[0:EC, 2 * b + a, 0:BN], held["tok_w"][:, k, a * EC:(a + 1) * EC],
                                                    xt[:, k, b * BN:(b + 1) * BN], start=k == 0, stop=k == PK - 1)
                            if k == PK - 1:
                                last.then_inc(tok_done, 1)

            @block.scalar
            def _(act):
                await_pack(act, "first")
                for b in range(BL):
                    for a in range(2):
                        act.wait_ge(tok_done, 2 * b + a + 1)
                        nc.scalar.activation(hT[:, a, b * BN:(b + 1) * BN], ps[0:EC, 2 * b + a, 0:BN], ACT.Identity,
                                             bias=V["tok_b"][:, a:a + 1])


W_ROWS = [(0, 0), (16, 1), (32, 0), (48, 1), (64, 0), (96, 2)]
Z_ROWS = [(0, 0), (16, 0), (32, 1), (48, 1), (64, 2), (96, 0)]
BIAS_ROW = 112


def stack_w1(sp, w_part, b_part, scratch, parts_out, w_stack, stacked_w):
    for n in range(3):
        sp.dma_start(scratch["w1"][n], w_part[n][:, :]).then_inc(parts_out, 16)
        sp.dma_start(scratch["b1"][n], b_part[n][:, :]).then_inc(parts_out, 16)
    sp.wait_ge(parts_out, 6 * 16)
    for row, part in W_ROWS:
        sp.dma_start(w_stack[row:row + R_, :, :],
                     scratch["w1"][part].rearrange("(s r) n -> r s n", r=R_)).then_inc(stacked_w, 16)
    sp.dma_start(w_stack[BIAS_ROW:BIAS_ROW + 3, :, :], scratch["b1"]).then_inc(stacked_w, 16)
    sp.wait_ge(stacked_w, 16 * (len(W_ROWS) + 1))


def images(ap):
    return ap.rearrange("p (b t) -> p b t", t=TOK)


def class_units():
    rows = [(r, ("row", r)) for r in range(ROWS)] + [(ROWS, ("first", 0))]
    cols = [(c, ("col", c)) for c in range(COLS)] + [(COLS, ("first", 0))]
    return [(0, rows[0:3]), (0, rows[3:6]), (0, rows[6:7]), (0, rows[7:8]),
            (1, cols[0:2]), (1, cols[2:4]), (1, cols[4:5]), (1, cols[5:6])]


def positions(ap, kinds):
    v = images(ap)
    kind, first = kinds[0]
    if kind == "first":
        return v[:, :, 0:1]
    grid = v[:, :, 1:TOK].rearrange("p b (r c) -> p b r c", c=COLS)
    n = len(kinds)
    if kind == "row":
        t = grid[:, :, first:first + n, :].rearrange("p b r c -> p r b c")
    else:
        t = grid[:, :, :, first:first + n].rearrange("p b r c -> p c b r")
    return t if n > 1 else t[:, 0]


def class_pass(nc, sem, tag, pe_wait, ps, by_row, by_col, srcs, dsts):
    done, copied = sem(f"{tag}_product"), sem(f"{tag}_copied")
    units = [(n, u) for n in range(len(srcs)) for u in class_units()]

    def view(bank, kinds, size):
        n = len(kinds)
        flat = ps[:, bank, 0:n * size * IMG_P]
        if n > 1:
            return flat.rearrange("p (k b t) -> p k b t", k=n, b=IMG_P)
        return flat.rearrange("p (b t) -> p b t", b=IMG_P)

    def size(kinds):
        return {"first": 1, "row": COLS, "col": ROWS}[kinds[0][0]]

    with nc.Block() as block:
        @block.tensor
        def _(pe):
            for w in pe_wait:
                pe.wait_ge(*w)
            for i, (n, (which, classes)) in enumerate(units):
                if i >= 8:
                    pe.wait_ge(copied, i - 7)
                m = (by_row, by_col)[which]
                for j, (c, kind) in enumerate(classes):
                    k = size([kind])
                    last = nc.tensor.matmul(ps[:, i % 8, j * k * IMG_P:(j + 1) * k * IMG_P].rearrange(
                        "p (b t) -> p b t", b=IMG_P), m[:, c, :], positions(srcs[n], [kind]), start=True, stop=True)
                last.then_inc(done, 1)

        @block.vector
        def _(dve):
            for i, (n, (which, classes)) in enumerate(units):
                dve.wait_ge(done, i + 1)
                kinds = [k for _, k in classes]
                got, dst = view(i % 8, kinds, size(kinds)), positions(dsts[n], kinds)
                if which == 0:
                    nc.vector.tensor_copy(dst, got).then_inc(copied, 1)
                else:
                    if i % 8 == 4:
                        dve.wait_ge(copied, i)
                    nc.vector.tensor_tensor(dst, dst, got, ALU.add).then_inc(copied, 1)


def project_qk0(nc, sem, ps, held, xnT, base, QT, KT, meanwhile):
    done, q_copied, k_copied = sem("qk0_product"), sem("q0_copied"), sem("k0_copied")
    units = [(w, g, b) for w in ("wq0", "wk0") for g in range(HG) for b in range(BL)]
    nq = HG * BL
    with nc.Block() as block:
        @block.sync
        def _(sp):
            meanwhile(sp)

        @block.tensor
        def _(pe):
            for i, (w, g, b) in enumerate(units):
                if i >= 8:
                    j = i - 8
                    pe.wait_ge(q_copied if j < nq else k_copied, (j if j < nq else j - nq) + 1)
                for a in range(2):
                    last = nc.tensor.matmul(ps[:, i % 8, 0:BN], held[w][:, a, g, :], xnT[:, a, b * BN:(b + 1) * BN],
                                            start=a == 0, stop=a == 1)
                last.then_inc(done, 1)

        @block.scalar
        def _(act):
            for i, (w, g, b) in enumerate(units[:nq]):
                act.wait_ge(done, i + 1)
                nc.scalar.mul(base[:, g, b * BN:(b + 1) * BN], ps[:, i % 8, 0:BN], HD ** -0.5).then_inc(q_copied, 1)

        @block.vector
        def _(dve):
            for i, (w, g, b) in enumerate(units[nq:], nq):
                dve.wait_ge(done, i + 1)
                nc.vector.tensor_tensor(images(KT[:, g, b * BN:(b + 1) * BN]), images(ps[:, i % 8, 0:BN]),
                                        spread(held["kconst"][:, :], 1, BIMG), ALU.add).then_inc(k_copied, 1)
    class_pass(nc, sem, "q0_classes", [], ps, held["av"], held["ah"], [base[:, g, :] for g in range(HG)],
               [QT[:, g, :] for g in range(HG)])


def denominators(nc, sem, tag, sb, ps, held, UT, target):
    done, inv, back, used = sem(f"{tag}_den"), sem(f"{tag}_inverted"), sem(f"{tag}_spread"), sem(f"{tag}_divided")
    inverse = sb(f"{tag}_inverse", [32 * BL, BN])
    units = [(b, g) for b in range(BL) for g in range(HG)]
    with nc.Block() as block:
        @block.tensor
        def _(pe):
            for b, g in units:
                last = nc.tensor.matmul(ps[32 * b:32 * b + 32, 0, 0:BN], held["den_rows"][:, g, :],
                                        UT[:, g, b * BN:(b + 1) * BN], start=g == 0, stop=g == HG - 1)
            last.then_inc(done, 1)
            pe.wait_ge(inv, 1)
            for i, (b, g) in enumerate(units):
                if i >= 7:
                    pe.wait_ge(used, i - 6)
                nc.tensor.matmul(ps[:, 1 + i % 7, 0:BN], held["den_back"][32 * b:32 * b + 32, g, :],
                                 inverse[32 * b:32 * b + 32, :], start=True, stop=True).then_inc(back, 1)

        @block.vector
        def _(dve):
            dve.wait_ge(done, 1)
            nc.vector.reciprocal(inverse[:, :], ps[0:32 * BL, 0, 0:BN]).then_inc(inv, 1)
            for i, (b, g) in enumerate(units):
                dve.wait_ge(back, i + 1)
                t = target[:, g, b * BN:(b + 1) * BN]
                nc.vector.tensor_tensor(t, t, ps[:, 1 + i % 7, 0:BN], ALU.mult).then_inc(used, 1)


def project_out0(nc, sem, sb, ps, held, UT, OT, _KT, hT, V):
    class_pass(nc, sem, "u0_classes", [], ps, held["bv"], held["bh"], [UT[:, g, :] for g in range(HG)],
               [OT[:, g, :] for g in range(HG)])
    denominators(nc, sem, "a0", sb, ps, held, UT, OT)
    done = sem("out0_product")
    units = [(b, m) for b in range(BL) for m in range(2)]
    with nc.Block() as block:
        @block.tensor
        def _(pe):
            for i, (b, m) in enumerate(units):
                for g in range(HG):
                    last = nc.tensor.matmul(ps[0:EC, i, 0:BN], held["wp0"][:, g, m * EC:(m + 1) * EC],
                                            OT[:, g, b * BN:(b + 1) * BN], start=g == 0, stop=g == HG - 1)
                last.then_inc(done, 1)

        @block.vector
        def _(dve):
            for i, (b, m) in enumerate(units):
                dve.wait_ge(done, i + 1)
                h = hT[:, m, b * BN:(b + 1) * BN]
                nc.vector.scalar_tensor_tensor(h, ps[0:EC, i, 0:BN], V["bp0"][:, m:m + 1], h, ALU.add, ALU.add)


def project_qk1(nc, sem, sb, ps, held, load, await_pack, xnT, QT, KT, V):
    base = sb("qk1_base", [128, BN]), sb("qk1_base_b", [128, BN])
    turned = sb("qk1_sin", [128, BN]), sb("qk1_sin_b", [128, BN])
    done, biased, rotated = sem("qk1_product"), sem("qk1_biased"), sem("qk1_rotated")
    cos_part, sin_part = sem("qk1_cos_part"), sem("qk1_sin_part")
    units = [(w, g, b) for w in range(2) for g in range(HG) for b in range(BL)]
    with nc.Block() as block:
        @block.sync
        def _(sp):
            load(sp, "feed_forward1")
            await_pack(sp, "feed_forward1")

        @block.tensor
        def _(pe):
            def product(i):
                w, g, b = units[i]
                if i >= 4:
                    pe.wait_ge(biased, i - 3)
                for a in range(2):
                    last = nc.tensor.matmul(ps[:, i % 4, 0:BN], held[("wq1", "wk1")[w]][:, a, g, :],
                                            xnT[:, a, b * BN:(b + 1) * BN], start=a == 0, stop=a == 1)
                last.then_inc(done, 1)

            product(0)
            for i in range(len(units)):
                if i + 1 < len(units):
                    product(i + 1)
                pe.wait_ge(biased, i + 1)
                if i >= 4:
                    pe.wait_ge(sin_part, i - 3)
                nc.tensor.matmul(ps[:, 4 + i % 4, 0:BN], held["rot"][:, :], base[i % 2][:, :], start=True,
                                 stop=True).then_inc(rotated, 1)

        @block.scalar
        def _(act):
            for i, (w, g, b) in enumerate(units):
                act.wait_ge(done, i + 1)
                if i >= 2:
                    act.wait_ge(rotated, i - 1)
                    act.wait_ge(cos_part, i - 1)
                bias = V[("bq1", "bk1")[w]][:, g:g + 1]
                nc.scalar.activation(base[i % 2][:, :], ps[:, i % 4, 0:BN], ACT.Identity, bias=bias).then_inc(biased, 1)

        @block.vector
        def _(dve):
            for i, (w, g, b) in enumerate(units):
                cos, sin = (held["cosq"], held["sinq"]) if w == 0 else (held["cosk"], held["sink_"])
                dst = (QT, KT)[w][:, g, b * BN:(b + 1) * BN]
                dve.wait_ge(biased, i + 1)
                nc.vector.tensor_tensor(images(dst), images(base[i % 2][:, :]), spread(cos[:, :], 1, BIMG),
                                        ALU.mult).then_inc(cos_part, 1)
                dve.wait_ge(rotated, i + 1)
                nc.vector.tensor_tensor(images(turned[i % 2][:, :]), images(ps[:, 4 + i % 4, 0:BN]),
                                        spread(sin[:, :], 1, BIMG), ALU.mult).then_inc(sin_part, 1)
                dve.wait_ge(cos_part, i + 1)
                dve.wait_ge(sin_part, i + 1)
                nc.vector.tensor_tensor(dst, dst, turned[i % 2][:, :], ALU.add)


def project_out1(nc, sem, sb, ps, held, UT, scaled, hT, V):
    denominators(nc, sem, "a1", sb, ps, held, UT, UT)
    done, biased = sem("out1_product"), sem("out1_biased")
    units = [(b, m) for b in range(BL) for m in range(2)]
    with nc.Block() as block:
        @block.tensor
        def _(pe):
            for i, (b, m) in enumerate(units):
                for g in range(HG):
                    last = nc.tensor.matmul(ps[0:EC, i, 0:BN], held["wp1"][:, g, m * EC:(m + 1) * EC],
                                            UT[:, g, b * BN:(b + 1) * BN], start=g == 0, stop=g == HG - 1)
                last.then_inc(done, 1)

        @block.vector
        def _(dve):
            for i, (b, m) in enumerate(units):
                dve.wait_ge(done, i + 1)
                h = hT[:, m, b * BN:(b + 1) * BN]
                t = scaled[0:EC, m, b * BN:(b + 1) * BN]
                nc.vector.tensor_scalar(t, ps[0:EC, i, 0:BN], V["bp1"][:, m:m + 1], V["rezero"], ALU.add,
                                        ALU.mult).then_inc(biased, 1)
                dve.wait_ge(biased, i + 1)
                nc.vector.tensor_tensor(h, h, t, ALU.add)


def experts(nc, sem, gate, sb, allocator, ps, ins, held, load, await_pack, scratch, xnT, hT, w_stack, stacked_w, V):
    z_stack = sb("z_parts_by_row", [128, S_, NT], BF16)
    wt = sb("weights_by_expert", [128, S_ // 2, NT])
    g_stack = sb("weight_parts_by_row", [96, 2, 2, S_ // 2, NT], BF16)
    stacked_z, stacked_g, z_out = sem("z_parts_stacked"), sem("weight_parts_stacked"), sem("z_parts_out")
    w2_loaded = sem("loaded_W2")

    with ExitStack() as mem:
        s2 = allocator(mem)
        zT = s2("zT", [128, NT])
        mem2 = ExitStack()
        rest = allocator(mem2)("z_rest", [128, NT])
        z_part = [allocator(mem2)(f"z_part{n}", [128, NT], BF16) for n in range(3)]
        z_done, z_copied, z_split, cleared = sem("z_done"), sem("z_copied"), sem("z_split"), sem("z_stack_cleared")
        with nc.Block() as block:
            @block.gpsimd
            def _(pool):
                nc.gpsimd.memset(z_stack[64:128, :, :], 1.0).then_inc(cleared, 1)

            @block.tensor
            def _(pe):
                for b in range(BL):
                    for a in range(2):
                        last = nc.tensor.matmul(ps[:, b, 0:BN], held["P"][:, a, :], xnT[:, a, b * BN:(b + 1) * BN],
                                                start=a == 0, stop=a == 1)
                    last.then_inc(z_done, 1)

            @block.scalar
            def _(act):
                for b in range(BL):
                    act.wait_ge(z_done, b + 1)
                    nc.scalar.copy(zT[:, b * BN:(b + 1) * BN], ps[:, b, 0:BN]).then_inc(z_copied, 1)

            @block.vector
            def _(dve):
                dve.wait_ge(z_copied, BL)
                nc.vector.tensor_copy(z_part[0][:], zT[:]).then_inc(z_split, 1)
                for n in (1, 2):
                    dve.wait_ge(z_split, 2 * n - 1)
                    nc.vector.tensor_tensor(rest[:], (zT if n == 1 else rest)[:], z_part[n - 1][:],
                                            ALU.subtract).then_inc(z_split, 1)
                    dve.wait_ge(z_split, 2 * n)
                    nc.vector.tensor_copy(z_part[n][:], rest[:]).then_inc(z_split, 1)

            @block.sync
            def _(sp):
                load(sp, "attention1")
                for n in range(3):
                    sp.wait_ge(z_split, 2 * n + 1)
                    sp.dma_start(scratch["z"][n], z_part[n][:, :]).then_inc(z_out, 16)
                sp.wait_ge(cleared, 1)
                sp.wait_ge(z_out, 3 * 16)
                for row, part in Z_ROWS:
                    sp.dma_start(z_stack[row:row + R_, :, :],
                                 scratch["z"][part].rearrange("(s r) t -> r s t", r=R_)).then_inc(stacked_z, 16)
        mem2.close()

        choose_experts(nc, sem, gate, s2, ps, held, zT, wt, g_stack, stacked_g)
    comb = sb("combined", [128, 2, NT])
    held["W2"] = sb("in_W2", list(ins["W2"].shape))
    with nc.Block() as block:
        @block.sync
        def _(sp):
            sp.dma_start(held["W2"][:], ins["W2"]).then_inc(w2_loaded, 16)
            sp.wait_ge(stacked_z, 16 * len(Z_ROWS))
            await_pack(sp, "attention1")
            sp.wait_ge(w2_loaded, 16)
    with ExitStack() as mem:
        run_experts(nc, sem, gate, allocator(mem), ps, held, z_stack, g_stack, stacked_g, wt, w_stack, comb)

    gated = sb("gated", [G_, NT])
    g1_done, gated_ready, g2_done = sem("g1_done"), sem("gated_ready"), sem("g2_done")
    with nc.Block() as block:
        @block.tensor
        def _(pe):
            for b in range(BL):
                for j in range(2):
                    last = nc.tensor.matmul(ps[0:G_, b, 0:EB], held["G1"][:, j, :], comb[:, j, b * EB:(b + 1) * EB],
                                            start=j == 0, stop=j == 1)
                last.then_inc(g1_done, 1)
            for b in range(BL):
                pe.wait_ge(gated_ready, b + 1)
                if b == 2:
                    pe.wait_ge(gated_ready, 3)
                for m in range(2):
                    bank = 3 + (2 * b + m) if 2 * b + m < 5 else 0
                    nc.tensor.matmul(ps[0:EC, bank, 0:EB], held["G2"][:, m * EC:(m + 1) * EC],
                                     gated[:, b * EB:(b + 1) * EB], start=True, stop=True).then_inc(g2_done, 1)

        @block.scalar
        def _(act):
            for b in range(BL):
                act.wait_ge(g1_done, b + 1)
                nc.scalar.activation(gated[:, b * EB:(b + 1) * EB], ps[0:G_, b, 0:EB], ACT.Gelu_apprx_tanh,
                                     bias=V["g1b"]).then_inc(gated_ready, 1)

        @block.vector
        def _(dve):
            for i in range(2 * BL):
                b, m = divmod(i, 2)
                dve.wait_ge(g2_done, i + 1)
                h = hT[:, m, b * EB:(b + 1) * EB]
                nc.vector.scalar_tensor_tensor(h, ps[0:EC, 3 + i if i < 5 else 0, 0:EB], V["g2b"][:, m:m + 1], h,
                                               ALU.add, ALU.add)


G_TRANSFERS = 12


def choose_experts(nc, sem, gate, sb, ps, held, zT, wt, g_stack, stacked_g):
    W = M_ + TOPK
    zs = [sb(f"z_slice{p}", [128, GT]) for p in range(2)]
    sc = [sb(f"expert_scores{p}", [GT, S_, W]) for p in range(2)]
    marked = [sb(f"scores_marked{p}", [GT, S_, W]) for p in range(2)]
    best = sb("best", [GT, S_, 8])
    wanted = sb("wanted", [GT, S_, 8])
    ex = [sb(f"expert_exp{p}", [GT, S_, M_]) for p in range(2)]
    total = sb("exp_total", [GT, S_])
    left = [sb(f"weight_rest{p}", [128, S_ // 2, GT]) for p in range(2)]
    parts = sb("weight_parts", [128, 3, S_ // 2, NT], BF16)

    sentinels, sliced, scored, score_copied = (sem("sentinels"), sem("z_sliced"), sem("expert_scored"),
                                               sem("expert_score_copied"))
    best_ready, wanted_ready, marked_ready = sem("best_ready"), sem("wanted_ready"), sem("marked_ready")
    centred, exp_ready, picked, total_ready, inverted = (sem("escore_centred"), sem("eexp_ready"), sem("picked"),
                                                         sem("etotal_ready"), sem("etotal_inverted"))
    weighed, turned, first_ready, wt_ready = (sem("eweighed"), sem("eweight_turned"), sem("first_ready"),
                                              sem("wt_ready"))
    left_ready, second_ready, third_ready = sem("eleft_ready"), sem("second_ready"), sem("third_ready")

    def cols(i):
        return bass.ds(i * GT, GT)

    def wps(p):
        return ps[:, 2 + p, 0:4 * GT].rearrange("p (s t) -> p s t", s=4)

    with nc.Block() as block:
        @block.gpsimd
        def _(pool):
            for p in range(2):
                nc.gpsimd.memset(sc[p][:, :, M_:W], SENTINEL).then_inc(sentinels, 1)
            nc.gpsimd.memset(wanted[:, :, TOPK:8], SENTINEL).then_inc(sentinels, 1)

            def slice_z(i, p):
                if not is_early(i):
                    pool.wait_ge(scored, i - 1)
                pass_gate(pool, gate)
                nc.gpsimd.tensor_copy(zs[p][:, :], zT[:, cols(i)]).then_inc(sliced, 1)

            slice_z(0, 0)

            def step(k, p):
                if is_group(k + 1):
                    slice_z(k + 1, 1 - p)
                if is_group(k - 2):
                    pool.wait_ge(second_ready, k - 1)
                    pass_gate(pool, gate)
                    nc.gpsimd.tensor_tensor(parts[:, 2, :, cols(k - 2)], left[p][:, :, :], parts[:, 1, :, cols(k - 2)],
                                            ALU.subtract).then_inc(third_ready, 1)
                if is_group(k - 1):
                    pool.wait_ge(first_ready, k)
                    pool.wait_ge(wt_ready, k)
                    pass_gate(pool, gate)
                    nc.gpsimd.tensor_tensor(left[1 - p][:, :, :], wt[:, :, cols(k - 1)], parts[:, 0, :, cols(k - 1)],
                                            ALU.subtract).then_inc(left_ready, 1)
            pipeline(pool, step, GROUPS + 2)

        @block.tensor
        def _(pe):
            def score(i, p):
                pe.wait_ge(sliced, i + 1)
                if not is_early(i):
                    pe.wait_ge(score_copied, i - 1)
                nc.tensor.matmul(ps[0:GT, p, 0:S_ * M_], zs[p][:, :], held["C"][:, :], start=True,
                                 stop=True).then_inc(scored, 1)

            score(0, 0)

            def step(k, p):
                if is_group(k + 1):
                    score(k + 1, 1 - p)
                if is_group(k - 1):
                    pe.wait_ge(weighed, k)
                    if not is_early(k - 1):
                        pe.wait_ge(wt_ready, k - 2)
                    for q in range(4):
                        last = nc.tensor.transpose(ps[:, 3 - p, q * GT:(q + 1) * GT],
                                                   ex[1 - p][:, 2 * q:2 * q + 2, :], held["ident"][0:GT, 0:GT])
                    last.then_inc(turned, 1)
            pipeline(pe, step, GROUPS + 1)

        @block.scalar
        def _(act):
            act.wait_ge(sentinels, 3)

            def copy_scores(i, p):
                act.wait_ge(scored, i + 1)
                if not is_early(i):
                    act.wait_ge(marked_ready, i - 1)
                nc.scalar.copy(sc[p][:, :, 0:M_], ps[0:GT, p, :].rearrange("t (s m) -> t s m", s=S_)).then_inc(
                    score_copied, 1)

            copy_scores(0, 0)

            def step(k, p):
                if is_group(k + 1):
                    copy_scores(k + 1, 1 - p)
                if is_group(k):
                    act.wait_ge(centred, k + 1)
                    nc.scalar.activation(ex[p][:, :, :], ex[p][:, :, :], ACT.Exp).then_inc(exp_ready, 1)
                if is_group(k - 1):
                    act.wait_ge(turned, k)
                    pass_gate(act, gate)
                    nc.scalar.copy(parts[:, 0, :, cols(k - 1)], wps(1 - p)).then_inc(first_ready, 1)
                    nc.scalar.copy(wt[:, :, cols(k - 1)], wps(1 - p)).then_inc(wt_ready, 1)
                if is_group(k - 2):
                    act.wait_ge(left_ready, k - 1)
                    pass_gate(act, gate)
                    nc.scalar.copy(parts[:, 1, :, cols(k - 2)], left[p][:, :, :]).then_inc(second_ready, 1)
            pipeline(act, step, GROUPS + 2)

        @block.vector
        def _(dve):
            dve.wait_ge(sentinels, 3)

            def mark(i, p):
                if not (isinstance(i, int) and i == 0):
                    dve.wait_ge(marked_ready, i)
                    dve.wait_ge(centred, i)
                dve.wait_ge(score_copied, i + 1)
                pass_gate(dve, gate)
                for s in range(S_):
                    last = nc.vector.max(best[:, s, :], sc[p][:, s, 0:M_])
                last.then_inc(best_ready, 1)
                dve.wait_ge(best_ready, i + 1)
                nc.vector.tensor_copy(wanted[:, :, 0:TOPK], best[:, :, 0:TOPK]).then_inc(wanted_ready, 1)
                if not is_early(i):
                    dve.wait_ge(turned, i - 1)
                nc.vector.tensor_tensor(ex[p][:, :, :], sc[p][:, :, 0:M_],
                                        spread(best[:, :, 0], 2, M_), ALU.subtract).then_inc(centred, 1)
                dve.wait_ge(wanted_ready, i + 1)
                pass_gate(dve, gate)
                for s in range(S_):
                    last = nc.vector.match_replace(marked[p][:, s, :], wanted[:, s, :], sc[p][:, s, :], 2 * TAKEN)
                last.then_inc(marked_ready, 1)

            def weigh(i, p):
                dve.wait_ge(marked_ready, i + 1)
                dve.wait_ge(exp_ready, i + 1)
                nc.vector.scalar_tensor_tensor(ex[p][:, :, :], marked[p][:, :, 0:M_], TAKEN, ex[p][:, :, :], ALU.is_lt,
                                               ALU.mult).then_inc(picked, 1)
                dve.wait_ge(picked, i + 1)
                nc.vector.reduce_sum(total[:, :], ex[p][:, :, :], AX.X).then_inc(total_ready, 1)
                dve.wait_ge(total_ready, i + 1)
                nc.vector.reciprocal(total[:, :], total[:, :]).then_inc(inverted, 1)
                dve.wait_ge(inverted, i + 1)
                nc.vector.tensor_tensor(ex[p][:, :, :], ex[p][:, :, :],
                                        spread(total[:, :], 2, M_), ALU.mult).then_inc(weighed, 1)

            def step(k, p):
                if is_group(k):
                    mark(k, p)
                if is_group(k - 1):
                    weigh(k - 1, 1 - p)
            pipeline(dve, step, GROUPS + 1)

        @block.sync
        def _(sp):
            for b in range(BL):
                block_cols = slice(b * EB, (b + 1) * EB)
                sp.wait_ge(third_ready, -(-(b + 1) * EB // GT))
                if b:
                    sp.wait_ge(stacked_g, b * G_TRANSFERS * 16)
                for n in range(3):
                    for odd in range(2):
                        for half in range(2):
                            row = 64 * odd + 32 * half
                            sp.dma_start(g_stack[32 * n:32 * n + 32, odd, half, :, block_cols],
                                         parts[row:row + 32, n, :, block_cols]).then_inc(stacked_g, 16)
            sp.wait_ge(stacked_g, BL * G_TRANSFERS * 16)


def run_experts(nc, sem, gate, sb, ps, held, z_stack, g_stack, stacked_g, wt, w_stack, comb):
    act_out = [sb(f"hidden{j}", [128, EB]) for j in range(4)]
    weighted = [[sb(f"hidden_weighted{q}_{j}", [128, EB]) for j in range(4)] for q in range(2)]
    w2s = [sb(f"w2_chunk{q}", [128, 4, 32]) for q in range(2)]
    h_done, gelu_done, w_done, mult_done, y_done = (sem("hidden_product"), sem("hidden_gelu"), sem("weight_spread"),
                                                    sem("hidden_weighted"), sem("second_product"))
    w2_ready, comb_copied = sem("w2_chunk_ready"), sem("comb_copied")
    UNITS, CHUNKS = 8 * CH, 2 * CH

    def start(eng, *counted):
        for s in counted:
            eng.sem_inc(s, 1)

    def unit(b, sh, c, j):
        return b * UNITS + sh * (4 * CH) + c * 4 + j

    def chunk(b, sh, c):
        return b * CHUNKS + sh * CH + c

    def opens(sh, c, count):
        return sh == 0 and isinstance(c, int) and c < count

    def walk(eng, step):
        with eng.Fori(0, BL) as b:
            for sh in range(2):
                step(b, sh, 0, 0)
                step(b, sh, 1, 1)
                with eng.Fori(1, CH // 2 - 1) as pair:
                    step(b, sh, pair * 2, 0)
                    step(b, sh, pair * 2 + 1, 1)
                step(b, sh, CH - 2, 0)
                step(b, sh, CH - 1, 1)

    with nc.Block() as block:
        @block.tensor
        def _(pe):
            def first(b, sh, c, j):
                if opens(sh, c, 1):
                    pe.wait_ge(gelu_done, b * UNITS + 1)
                else:
                    pe.wait_ge(gelu_done, unit(b, sh, c, j) - 2)
                s = 4 * sh + j
                nc.tensor.matmul(ps[:, j, 0:EB], w_stack[:, s, bass.ds(c * 128, 128)],
                                 z_stack[:, s, bass.ds(b * EB, EB)], start=True, stop=True).then_inc(h_done, 1)

            def spread_weights(b, sh, c, j):
                if opens(sh, c, 1) and j < 2:
                    pe.wait_ge(mult_done, b * UNITS + 1)
                else:
                    pe.wait_ge(mult_done, unit(b, sh, c, j))
                s = 4 * sh + j
                rows = g_stack[:, s % 2, :, :, :].rearrange("p h s n -> p (h s n)")
                nc.tensor.matmul(ps[:, 4 + j % 2, 0:EB], held["sel"][:, bass.ds((c % 8) * 128, 128)],
                                 rows[:, bass.ds((c // 8) * (S_ // 2 * NT) + (s // 2) * NT + b * EB, EB)], start=True,
                                 stop=True).then_inc(w_done, 1)

            def second(b, sh, c, q):
                pe.wait_ge(mult_done, unit(b, sh, c, 3) + 2)
                pe.wait_ge(w2_ready, chunk(b, sh, c) + 1)
                for j in range(4):
                    last = nc.tensor.matmul(ps[32 * j:32 * j + 32, 6 + sh, 0:EB], w2s[q][:, j, :], weighted[q][j][:, :],
                                            start=False, stop=False, skip_group_check=True)
                last.then_inc(y_done, 1)

            def open_sums(b, sh):
                pe.wait_ge(comb_copied, b * 2 + 1)
                for jj in range(2):
                    nc.tensor.matmul(ps[:, 6 + sh, 0:EB], held["b2"][:, 2 * sh + jj, :],
                                     wt[:, 2 * sh + jj, bass.ds(b * EB, EB)], start=jj == 0, stop=False,
                                     skip_group_check=True)

            def step(b, sh, c, q):
                peeled = isinstance(c, int)
                if peeled and c == 0 and sh == 0:
                    pe.wait_ge(stacked_g, (b + 1) * (G_TRANSFERS * 16))
                    for j in range(3):
                        first(b, sh, c, j)
                for j in range(4):
                    spread_weights(b, sh, c, j)
                    if j == 1:
                        if not (peeled and c == 0):
                            second(b, sh, c - 1, 1 - q)
                        elif sh == 1:
                            second(b, 0, CH - 1, 1 - q)
                        if peeled and c == 0:
                            open_sums(b, sh)
                    if j == 0:
                        first(b, sh, c, 3)
                    elif not (peeled and c == CH - 1):
                        first(b, sh, c + 1, j - 1)
                    elif sh == 0:
                        first(b, 1, 0, j - 1)
                if peeled and c == CH - 1 and sh == 1:
                    second(b, sh, c, q)

            start(pe, y_done)
            walk(pe, step)

        @block.scalar
        def _(act):
            def step(b, sh, c, q):
                for j in range(4):
                    act.wait_ge(h_done, unit(b, sh, c, j) + 1)
                    if opens(sh, c, 1):
                        act.wait_ge(mult_done, b * UNITS + 1)
                    else:
                        act.wait_ge(mult_done, unit(b, sh, c, j) - 2)
                    nc.scalar.activation(act_out[j][:, :], ps[:, j, 0:EB], ACT.Gelu_apprx_tanh).then_inc(gelu_done, 1)
            start(act, gelu_done)
            walk(act, step)

        @block.vector
        def _(dve):
            def copy_sums(b, sh):
                dve.wait_ge(y_done, chunk(b, sh, CH - 1) + 2)
                nc.vector.tensor_scalar(comb[:, sh, bass.ds(b * EB, EB)], ps[:, 6 + sh, 0:EB], 0.0, None,
                                        ALU.add).then_inc(comb_copied, 1)

            def step(b, sh, c, q):
                for j in range(4):
                    dve.wait_ge(gelu_done, unit(b, sh, c, j) + 2)
                    dve.wait_ge(w_done, unit(b, sh, c, j) + 1)
                    if opens(sh, c, 2):
                        dve.wait_ge(y_done, b * CHUNKS + 1)
                    else:
                        dve.wait_ge(y_done, chunk(b, sh, c))
                    nc.vector.tensor_tensor(weighted[q][j][:, :], act_out[j][:, :], ps[:, 4 + j % 2, 0:EB],
                                            ALU.mult).then_inc(mult_done, 1)
                    if isinstance(c, int) and c == 0 and sh == 1 and j == 3:
                        copy_sums(b, 0)
                if isinstance(c, int) and c == CH - 1 and sh == 1:
                    copy_sums(b, 1)
            start(dve, mult_done, comb_copied)
            walk(dve, step)

        @block.gpsimd
        def _(pool):
            def step(b, sh, c, q):
                if opens(sh, c, 2):
                    pool.wait_ge(y_done, b * CHUNKS + 1)
                else:
                    pool.wait_ge(y_done, chunk(b, sh, c))
                pass_gate(pool, gate)
                nc.gpsimd.tensor_copy(w2s[q][:, :, :].rearrange("p k r -> p (k r)"),
                                      held["W2"][:, bass.ds((sh * CH + c) * 128, 128)]).then_inc(w2_ready, 1)
            walk(pool, step)


def quantised(nc, sem, gate, sb, ps, held, hT, out, V):
    win = sb("w_in_t", [EC, 2, 2 * FF], BF16)
    wout = sb("w_out_t", [128, 4, E], BF16)
    wsum = sb("w_sums", [128, 2])
    wscale = sb("w_scales", [128, 2])
    winv = sb("w_inv", [128, 2])

    prep, summed, inv_ready, rounded = sem("wq_sums"), sem("wq_summed"), sem("wq_inverted"), sem("wq_rounded")
    sizes = (E * 2 * FF, E * FF)
    with nc.Block() as block:
        @block.vector
        def _(dve):
            nc.vector.memset(wsum[:, :], 0.0).then_inc(prep, 1)
            dve.wait_ge(prep, 1)
            nc.vector.tensor_reduce(wsum[0:EC, 0:1], held["w_in"][:, :, :], AX.XY, ALU.add,
                                    apply_absolute_value=True).then_inc(prep, 1)
            nc.vector.tensor_reduce(wsum[:, 1:2], held["w_out"][:, :, :], AX.XY, ALU.add,
                                    apply_absolute_value=True).then_inc(prep, 1)
            for k in range(2):
                dve.wait_ge(summed, 1)
                nc.vector.tensor_scalar(wscale[:, k:k + 1], ps[:, 0, k:k + 1], 1.0 / sizes[k], Q_EPS, ALU.mult,
                                        ALU.max).then_inc(inv_ready, 1)
            dve.wait_ge(inv_ready, 2)
            nc.vector.reciprocal(winv[:, :], wscale[:, :]).then_inc(inv_ready, 1)
            dve.wait_ge(inv_ready, 3)
            n = 0
            for w, q, k in ((held["w_in"], win, 0), (held["w_out"], wout, 1)):
                rows = w.shape[0]
                nc.vector.tensor_scalar(w[:], w[:], winv[0:rows, k:k + 1], ROUND, ALU.mult,
                                        ALU.add).then_inc(rounded, 1)
                n += 1
                dve.wait_ge(rounded, n)
                nc.vector.tensor_scalar(w[:], w[:], ROUND, -1.0, ALU.subtract, ALU.max).then_inc(rounded, 1)
                n += 1
                dve.wait_ge(rounded, n)
                nc.vector.tensor_scalar(q[:], w[:], 1.0, None, ALU.min).then_inc(rounded, 1)
                n += 1

        @block.tensor
        def _(pe):
            pe.wait_ge(prep, 3)
            nc.tensor.matmul(ps[:, 0, 0:2], held["all_ones"][:, :], wsum[:, :], start=True, stop=True).then_inc(
                summed, 1)

    ht = sb("h_tokens", [GT, GROUPS, E])
    x = sb("x_centred", [GT, GROUPS, E])
    xg = sb("x_squares_then_gained", [GT, GROUPS, E])
    qb = sb("x_quantised", [GT, GROUPS * E], BF16)
    mean, ss, rstd, rms, amax, scale, dq = (sb(f"x_{n}", [GT, GROUPS]) for n in
                                            ("mean", "squares", "rstd", "rms", "max", "scale", "step"))
    ss2, rms2, amax2, scale2, dq2 = (sb(f"y_{n}", [GT, GROUPS]) for n in ("squares", "rms", "max", "scale", "step"))
    qt = [sb(f"x_quantised_t{p}", [EC, 2 * GT], BF16) for p in range(2)]
    sil = [sb(f"silu_gate{p}", [GT, FF]) for p in range(2)]
    y = [sb(f"y{p}", [GT, FF]) for p in range(2)]
    junk = sb("y_elementwise_squares", [GT, FF])
    yg = sb("y_gained", [GT, GROUPS * FF])
    yb = sb("y_quantised", [GT, GROUPS * FF], BF16)
    yt = [sb(f"y_quantised_t{p}", [128, 4 * GT], BF16) for p in range(2)]
    scaled = [sb(f"product_scaled{p}", [GT, E]) for p in range(2)]
    res = [sb(f"result{p}", [GT, E]) for p in range(2)]

    PAIRS = -(-GROUPS // 2)
    SEGMENTS = [(0, 4), (4, 8), (8, GROUPS)]
    turned, tokens, centred, squared = (sem("f1_turned"), sem("f1_tokens"), sem("f1_centred"), sem("f1_squared"))
    x_steps, summed_squares, std_ready = sem("f1_x_steps"), sem("f1_summed_squares"), sem("f1_std")
    mean_square, rms_ready, quantised_x = sem("f1_mean_square"), sem("f1_rms"), sem("f1_x_quantised")
    qt_ps, qt_sb, h_ps, silu_ready = sem("f1_qt_turned"), sem("f1_qt_copied"), sem("f1_h_product"), sem("f1_silu")
    y_ready, ss2_ready, gained, amax2_ready = sem("f1_y"), sem("f1_y_squares"), sem("f1_gained"), sem("f1_y_max")
    rms2_ready, y_steps, quantised_y = sem("f1_y_rms"), sem("f1_y_steps"), sem("f1_y_quantised")
    yt_ps, yt_sb, o_ps = sem("f1_yt_turned"), sem("f1_yt_copied"), sem("f1_o_product")
    scaled_ready, res_ready = sem("f1_scaled"), sem("f1_result")
    stored = [sem("stored_even"), sem("stored_odd")]

    def bank_bf16(rows, bank, width):
        return ps[0:rows, bank, :].bitcast(BF16)[:, 0:width]

    def column(t, i):
        return t[:, bass.ds(i, 1)]

    with nc.Block() as block:
        @block.tensor
        def _(pe):
            for j in range(PAIRS):
                for i in range(2 * j, min(2 * j + 2, GROUPS)):
                    for a in range(2):
                        at = (i % 2) * E + a * EC
                        last = nc.tensor.transpose(ps[0:GT, j, at:at + EC], hT[:, a, i * GT:(i + 1) * GT],
                                                   held["ident"][0:EC, 0:EC])
                last.then_inc(turned, 1)

            def turn_x(i, p):
                pe.wait_ge(quantised_x, i + 1)
                if not is_early(i):
                    pe.wait_ge(qt_sb, i - 1)
                for a in range(2):
                    last = nc.tensor.transpose(bank_bf16(EC, 6 + p, 2 * GT)[:, a * GT:(a + 1) * GT],
                                               qb[:, bass.ds(i * E + a * EC, EC)], held["identb"][0:GT, 0:GT])
                last.then_inc(qt_ps, 1)

            pe.wait_ge(tokens, PAIRS)
            pe.wait_ge(rounded, 6)
            turn_x(0, 0)

            def step(i, p):
                if not is_last(i):
                    turn_x(i + 1, 1 - p)
                pe.wait_ge(qt_sb, i + 1)
                if not is_early(i):
                    pe.wait_ge(y_ready, i - 1)
                for n in range(2):
                    for a in range(2):
                        last = nc.tensor.matmul(ps[0:GT, 2 * p + n, :], qt[p][:, a * GT:(a + 1) * GT],
                                                win[:, a, n * FF:(n + 1) * FF], start=a == 0, stop=a == 1)
                last.then_inc(h_ps, 1)
            over_groups(pe, step)

            def turn_y(i, p):
                pe.wait_ge(quantised_y, i + 1)
                if not is_early(i):
                    pe.wait_ge(yt_sb, i - 1)
                for a in range(4):
                    last = nc.tensor.transpose(bank_bf16(128, 4 + p, 4 * GT)[:, a * GT:(a + 1) * GT],
                                               yb[:, bass.ds(i * FF + a * 128, 128)], held["identb"][0:GT, 0:GT])
                last.then_inc(yt_ps, 1)

            turn_y(0, 0)

            def step(i, p):
                if not is_last(i):
                    turn_y(i + 1, 1 - p)
                pe.wait_ge(yt_sb, i + 1)
                if not is_early(i):
                    pe.wait_ge(scaled_ready, i - 1)
                for a in range(4):
                    last = nc.tensor.matmul(ps[0:GT, 6 + p, 0:E], yt[p][:, a * GT:(a + 1) * GT], wout[:, a, :],
                                            start=a == 0, stop=a == 3)
                last.then_inc(o_ps, 1)
            over_groups(pe, step)

        @block.scalar
        def _(act):
            for j in range(PAIRS):
                n = min(2, GROUPS - 2 * j)
                act.wait_ge(turned, j + 1)
                nc.scalar.copy(ht[:, 2 * j:2 * j + n, :].rearrange("t g e -> t (g e)"), ps[0:GT, j, 0:n * E]).then_inc(
                    tokens, 1)
            for k, (lo, hi) in enumerate(SEGMENTS):
                act.wait_ge(centred, k + 1)
                nc.scalar.activation(xg[:, lo:hi, :], x[:, lo:hi, :], ACT.Square).then_inc(squared, 1)
            act.wait_ge(summed_squares, 1)
            nc.scalar.activation(rstd[:, :], ss[:, :], ACT.Sqrt, bias=V["rms_ln"][0:GT], scale=1.0 / E).then_inc(
                std_ready, 1)
            act.wait_ge(mean_square, 1)
            nc.scalar.activation(rms[:, :], rms[:, :], ACT.Sqrt, bias=V["rms_eps"][0:GT]).then_inc(rms_ready, 1)

            def copy_x(i, p):
                act.wait_ge(qt_ps, i + 1)
                if not is_early(i):
                    act.wait_ge(h_ps, i - 1)
                nc.scalar.copy(qt[p][:, :], bank_bf16(EC, 6 + p, 2 * GT)).then_inc(qt_sb, 1)

            copy_x(0, 0)

            def step(k, p):
                if is_group(k + 1):
                    copy_x(k + 1, 1 - p)
                if is_group(k):
                    act.wait_ge(h_ps, k + 1)
                    if not is_early(k):
                        act.wait_ge(y_ready, k - 1)
                    pass_gate(act, gate)
                    nc.scalar.activation(sil[p][:, :], ps[0:GT, 2 * p + 1, :], ACT.Silu, scale=column(dq, k)).then_inc(
                        silu_ready, 1)
                if is_group(k - 1):
                    act.wait_ge(y_ready, k)
                    if not (isinstance(k, int) and k == 1):
                        act.wait_ge(ss2_ready, k - 1)
                    pass_gate(act, gate)
                    nc.scalar.activation(junk[:, :], y[1 - p][:, :], ACT.Square, accum_out=column(ss2, k - 1)).then_inc(
                        ss2_ready, 1)
            pipeline(act, step, GROUPS + 1)

            act.wait_ge(ss2_ready, GROUPS)
            nc.scalar.activation(rms2[:, :], ss2[:, :], ACT.Sqrt, bias=V["rms_eps"][0:GT], scale=1.0 / FF).then_inc(
                rms2_ready, 1)

            def copy_y(i, p):
                act.wait_ge(yt_ps, i + 1)
                if not is_early(i):
                    act.wait_ge(o_ps, i - 1)
                nc.scalar.copy(yt[p][:, :], bank_bf16(128, 4 + p, 4 * GT)).then_inc(yt_sb, 1)

            copy_y(0, 0)

            def step(i, p):
                if not is_last(i):
                    copy_y(i + 1, 1 - p)
                act.wait_ge(o_ps, i + 1)
                if not is_early(i):
                    act.wait_ge(res_ready, i - 1)
                pass_gate(act, gate)
                nc.scalar.activation(scaled[p][:, :], ps[0:GT, 6 + p, 0:E], ACT.Identity, scale=column(dq2, i)).then_inc(
                    scaled_ready, 1)
            over_groups(act, step)

        @block.vector
        def _(dve):
            def quantise(x, scale, q, steps, n, quantised):
                for lo, hi in SEGMENTS:
                    seg = x[:, lo:hi, :]
                    nc.vector.tensor_tensor(seg, seg, spread(scale[:, lo:hi], 2, x.shape[2]), ALU.mult).then_inc(
                        steps, 1)
                    n += 1
                    dve.wait_ge(steps, n)
                    nc.vector.tensor_scalar(seg, seg, ROUND, ROUND + 127.0, ALU.add, ALU.min).then_inc(steps, 1)
                    n += 1
                    dve.wait_ge(steps, n)
                    nc.vector.tensor_scalar(q[:, lo:hi, :], seg, ROUND - 128.0, ROUND, ALU.max,
                                            ALU.subtract).then_inc(quantised, hi - lo)

            n = 0
            for k, (lo, hi) in enumerate(SEGMENTS):
                dve.wait_ge(tokens, (hi + 1) // 2)
                nc.vector.reduce_sum(mean[:, lo:hi], ht[:, lo:hi, :], AX.X).then_inc(x_steps, 1)
                n += 1
                dve.wait_ge(x_steps, n)
                nc.vector.tensor_scalar(mean[:, lo:hi], mean[:, lo:hi], 1.0 / E, None, ALU.mult).then_inc(x_steps, 1)
                n += 1
                dve.wait_ge(x_steps, n)
                nc.vector.tensor_tensor(x[:, lo:hi, :], ht[:, lo:hi, :], spread(mean[:, lo:hi], 2, E),
                                        ALU.subtract).then_inc(centred, 1)
            for k, (lo, hi) in enumerate(SEGMENTS):
                dve.wait_ge(squared, k + 1)
                last = nc.vector.reduce_sum(ss[:, lo:hi], xg[:, lo:hi, :], AX.X)
            last.then_inc(summed_squares, 1)
            gain = held["gb_in"][0:GT, :]
            dve.wait_ge(summed_squares, 1)
            nc.vector.tensor_tensor(xg[:, :, :], x[:, :, :], spread(gain, 1, GROUPS), ALU.mult).then_inc(x_steps, 1)
            n += 1
            dve.wait_ge(x_steps, n)
            nc.vector.tensor_reduce(amax[:, :], xg[:, :, :], AX.X, ALU.max, apply_absolute_value=True).then_inc(
                x_steps, 1)
            n += 1
            dve.wait_ge(std_ready, 1)
            nc.vector.reciprocal(rstd[:, :], rstd[:, :]).then_inc(x_steps, 1)
            n += 1
            dve.wait_ge(x_steps, n)
            nc.vector.scalar_tensor_tensor(rms[:, :], ss[:, :], 1.0 / E, rstd[:, :], ALU.mult, ALU.mult).then_inc(
                x_steps, 1)
            n += 1
            dve.wait_ge(x_steps, n)
            nc.vector.tensor_tensor(rms[:, :], rms[:, :], rstd[:, :], ALU.mult).then_inc(mean_square, 1)
            dve.wait_ge(rms_ready, 1)
            nc.vector.reciprocal(rms[:, :], rms[:, :]).then_inc(x_steps, 1)
            n += 1
            dve.wait_ge(x_steps, n)
            nc.vector.tensor_tensor(rms[:, :], rms[:, :], rstd[:, :], ALU.mult).then_inc(x_steps, 1)
            n += 1

            def step_sizes(amax, norm, scale, dq, k, steps, n):
                dve.wait_ge(steps, n)
                nc.vector.tensor_tensor(amax[:, :], amax[:, :], norm[:, :], ALU.mult).then_inc(steps, 1)
                dve.wait_ge(steps, n + 1)
                nc.vector.tensor_scalar(amax[:, :], amax[:, :], Q_EPS, None, ALU.max).then_inc(steps, 1)
                dve.wait_ge(steps, n + 2)
                nc.vector.tensor_scalar(dq[:, :], amax[:, :], wscale[0:GT, k:k + 1], 1.0 / 127.0, ALU.mult,
                                        ALU.mult).then_inc(steps, 1)
                nc.vector.reciprocal(scale[:, :], amax[:, :]).then_inc(steps, 1)
                dve.wait_ge(steps, n + 4)
                nc.vector.scalar_tensor_tensor(scale[:, :], scale[:, :], 127.0, norm[:, :], ALU.mult,
                                               ALU.mult).then_inc(steps, 1)
                dve.wait_ge(steps, n + 5)
                return n + 5

            n = step_sizes(amax, rms, scale, dq, 0, x_steps, n)
            quantise(xg, scale, qb[:, :].rearrange("t (g e) -> t g e", e=E), x_steps, n, quantised_x)

            def step(k, p):
                if is_group(k):
                    dve.wait_ge(silu_ready, k + 1)
                    if not is_early(k):
                        dve.wait_ge(ss2_ready, k - 1)
                        dve.wait_ge(gained, k - 1)
                    nc.vector.scalar_tensor_tensor(y[p][:, :], ps[0:GT, 2 * p, :], column(dq, k), sil[p][:, :],
                                                   ALU.mult, ALU.mult).then_inc(y_ready, 1)
                if is_group(k - 2):
                    dve.wait_ge(gained, k - 1)
                    pass_gate(dve, gate)
                    nc.vector.tensor_reduce(column(amax2, k - 2), yg[:, bass.ds((k - 2) * FF, FF)], AX.X, ALU.max,
                                            apply_absolute_value=True).then_inc(amax2_ready, 1)
            pipeline(dve, step, GROUPS + 2)

            dve.wait_ge(rms2_ready, 1)
            nc.vector.reciprocal(rms2[:, :], rms2[:, :]).then_inc(y_steps, 1)
            dve.wait_ge(amax2_ready, GROUPS)
            n = step_sizes(amax2, rms2, scale2, dq2, 1, y_steps, 1)
            quantise(yg[:, :].rearrange("t (g f) -> t g f", f=FF), scale2,
                     yb[:, :].rearrange("t (g f) -> t g f", f=FF), y_steps, n, quantised_y)

        @block.gpsimd
        def _(pool):
            def step(i, p):
                pool.wait_ge(y_ready, i + 1)
                pass_gate(pool, gate)
                nc.gpsimd.tensor_tensor(yg[:, bass.ds(i * FF, FF)], y[p][:, :], held["gb_out"][0:GT, :],
                                        ALU.mult).then_inc(gained, 1)
            over_groups(pool, step)

            def step(i, p):
                pool.wait_ge(scaled_ready, i + 1)
                if not is_early(i):
                    pool.wait_ge(stored[p], (i - p) * 8)
                pass_gate(pool, gate)
                nc.gpsimd.tensor_tensor(res[p][:, :], scaled[p][:, :], ht[:, :, :].rearrange("t g e -> t (g e)")[
                    :, bass.ds(i * E, E)], ALU.add).then_inc(res_ready, 1)
            over_groups(pool, step)

        @block.sync
        def _(sp):
            def step(i, p):
                sp.wait_ge(res_ready, i + 1)
                rows = GT if not is_last(i) else IMAGES * TOK - (GROUPS - 1) * GT
                sp.dma_start(out[bass.ds(i * GT, rows), :], res[p][0:rows, :]).then_inc(stored[p], 16)
            over_groups(sp, step)
            sp.wait_ge(stored[0], 16 * ((GROUPS + 1) // 2))
            sp.wait_ge(stored[1], 16 * (GROUPS // 2))



def laid_out(x, np, bf16):
    f = np.float32
    a = {k: np.asarray(v) for k, v in x.items()}
    out = {}
    z = lambda *s: np.zeros(s, f)
    xt = z(PK * 128, NT)
    xt[:, :IMAGES * TOK] = a["x"].reshape(IMAGES, 3, GRID, PATCH, GRID, PATCH).transpose(1, 3, 5, 0, 2, 4).reshape(
        PK * 128, IMAGES * TOK)
    out["xt"] = xt.reshape(PK, 128, NT).transpose(1, 0, 2)
    out["tok_w"] = a["L0_tok_W"].reshape(E, PK, 128).transpose(2, 1, 0)

    def rows(w):
        return w.reshape(2, EC, -1).transpose(1, 0, 2)

    def by_head(w):
        p = z(w.shape[0], HEADS, 32)
        p[:, :, :HD] = w.reshape(w.shape[0], HEADS, HD)
        return rows(p.reshape(w.shape[0], -1)).reshape(EC, 2, HG, 128)

    def by_head_rows(w):
        p = z(HG, 4, 32, E)
        p[:, :, :HD] = w.reshape(HG, 4, HD, E)
        return p.transpose(1, 2, 0, 3).reshape(128, HG, E)

    qkv = a["L0_attn_w_qkv"]
    out["wq0"], out["wk0"], out["wv0"] = by_head(qkv[:, :E]), by_head(qkv[:, E:2 * E]), rows(qkv[:, 2 * E:])
    out["wp0"] = by_head_rows(a["L0_attn_w_proj"])
    R0, C0, ONE, MAXREL = HD, HD + ROWS + 1, 30, 14
    kc = z(4, 32, TOK)
    kc[:, R0 + ROWS, 0] = kc[:, C0 + COLS, 0] = 1
    for t in range(TOK - 1):
        kc[:, R0 + t // COLS, 1 + t] = kc[:, C0 + t % COLS, 1 + t] = 1
    out["kconst"] = kc.reshape(128, TOK)

    def classes(tab, n, base, value_side, identity):
        m = z(n + 1, 4, 32, 4, 32)
        for k in range(n + 1):
            idx = [0 if k == n or j == n else min(max(j - k, -MAXREL), MAXREL) + MAXREL + 1 for j in range(n + 1)]
            for h in range(4):
                blk = tab[idx]
                if value_side:
                    m[k, h, base:base + n + 1, h, :HD] = blk
                else:
                    m[k, h, :HD, h, base:base + n + 1] = blk.T
                if identity:
                    m[k, h, range(HD), h, range(HD)] = 1
        return m.reshape(n + 1, 128, 128).transpose(1, 0, 2)

    out["av"] = classes(a["L0_attn_tab_vk"], ROWS, R0, False, True)
    out["ah"] = classes(a["L0_attn_tab_hk"], COLS, C0, False, False)
    out["bv"] = classes(a["L0_attn_tab_vv"], ROWS, R0, True, True)
    out["bh"] = classes(a["L0_attn_tab_hv"], COLS, C0, True, False)
    den_rows, den_back = z(4, 32, HG, 32), z(BL, 32, HG, 4, 32)
    for g in range(HG):
        for h in range(4):
            den_rows[h, ONE, g, 4 * g + h] = 1
            den_back[:, 4 * g + h, g, h, :] = 1
    den_rows[0, ONE, 0, HEADS:] = 1
    out["den_rows"] = den_rows.reshape(128, HG, 32)
    out["den_back"] = den_back.reshape(BL * 32, HG, 128)
    out["blocks4"] = np.repeat(np.eye(4, dtype=f), 32, axis=0)
    img = np.arange(GT) // TOK
    same = img[:, None] == img[None, :]
    causal = same & (np.arange(GT)[None, :] <= np.arange(GT)[:, None])
    out["mask0"] = np.tile(np.where(same, 0, NEG).astype(f), (1, 4)).astype(bf16)
    m1 = np.where(causal, 0, NEG).astype(f)
    m1 = np.concatenate([m1, z(GT, 1)], axis=1)
    out["mask1"] = np.tile(m1, (1, 4)).astype(bf16)
    v0 = z(GT, HEADS, 32)
    for t in range(GT):
        p = t % TOK
        v0[t, :, R0 + (ROWS if p == 0 else (p - 1) // COLS)] = 1
        v0[t, :, C0 + (COLS if p == 0 else (p - 1) % COLS)] = 1
    v0[:, :, ONE] = 1
    out["v_start0"] = v0
    v1 = z(GT + 1, HEADS, 32)
    v1[:, :, ONE] = 1
    out["v_start1"] = v1
    out["ones"] = np.full((EC, EC), 1.0 / E, f)
    out["all_ones"] = np.ones((128, 128), f)
    out["ident"] = np.eye(128, dtype=f)
    out["identb"] = np.eye(128, dtype=f).astype(bf16)
    out["P"] = rows(a["L0_ffn_P"].transpose(1, 0, 2).reshape(E, S_ * R_))
    C = z(S_, R_, S_, M_)
    b2 = z(2, M_, S_ // 2, 4, 32)
    for s in range(S_):
        C[s, :, s, :] = a["L0_ffn_C"][s].T
        b2[s % 2, :, s // 2, s % 4, :R_] = a["L0_ffn_b2"][s]
    out["C"] = C.reshape(128, S_ * M_)
    out["b2"] = b2.reshape(128, S_ // 2, 128)
    out["W1"] = a["L0_ffn_W1"].transpose(0, 2, 1, 3).reshape(S_ * R_, M_ * H_)
    out["b1"] = a["L0_ffn_b1"].reshape(S_, M_ * H_)
    w2 = z(S_, CH, 128, 32)
    w2[..., :R_] = a["L0_ffn_W2"].reshape(S_, CH, 128, R_)
    out["W2"] = w2.reshape(2, 4, CH, 128, 32).transpose(3, 0, 2, 1, 4).reshape(128, -1)
    sel = z(3, 32, 8, 4, H_)
    for c in range(8):
        for m in range(4):
            sel[:, 4 * c + m, c, m, :] = 1
    out["sel"] = sel.reshape(96, 8 * 128).astype(bf16)
    g1 = z(4, 32, 2, G_)
    g1[:, :R_] = a["L0_ffn_G1"].reshape(2, 4, R_, G_).transpose(1, 2, 0, 3)
    out["G1"] = g1.reshape(128, 2, G_)
    out["G2"] = a["L0_ffn_G2"]
    w, bq = a["L1_attn_W_attn"], a["L1_attn_b_attn"]
    out["wq1"], out["wk1"], out["wv1"] = by_head(w[:, :E]), by_head(w[:, E:2 * E]), rows(w[:, 2 * E:])
    out["wp1"] = by_head_rows(a["L1_attn_W_proj"])
    out["vb1"] = np.broadcast_to(bq[2 * E:].reshape(1, HEADS, HD), (GT, HEADS, HD))
    rot = z(4, 32, 4, 32)
    cos, sin = z(4, 32, TOK), z(4, 32, TOK)
    freqs = (1.0 / np.float32(10000.0) ** (np.arange(0, HD, 2, dtype=f) / np.float32(HD))).astype(f)
    ang = np.outer(np.arange(TOK, dtype=f), freqs).astype(f)
    for d in range(HD):
        cos[:, d, :] = np.cos(ang[:, d // 2])
        sin[:, d, :] = np.sin(ang[:, d // 2])
    for h in range(4):
        for d in range(0, HD, 2):
            rot[h, d + 1, h, d] = -1
            rot[h, d, h, d + 1] = 1
    out["rot"] = rot.reshape(128, 128)
    cq = cos * f(HD ** -0.5)
    cq[:, 31] = 1
    out["cosq"], out["sinq"] = cq.reshape(128, TOK), (sin * f(HD ** -0.5)).reshape(128, TOK)
    out["cosk"], out["sink_"] = cos.reshape(128, TOK), sin.reshape(128, TOK)
    sk = z(4, 32, HG, 4)
    for h in range(4):
        sk[h, 31, :, h] = a["L1_attn_sinks"].reshape(HG, 4)[:, h]
    out["sinkcol"] = sk.reshape(128, HG, 4)
    out["gb_in"] = np.broadcast_to(a["L1_ffn_g_in"], (128, E))
    out["gb_out"] = np.broadcast_to(a["L1_ffn_g_out"], (128, FF))
    out["w_in"] = rows(a["L1_ffn_w_in"].T)
    out["w_out"] = a["L1_ffn_w_out"].T.reshape(4, 128, E).transpose(1, 0, 2)

    def by_head_vec(v, one=0):
        p = z(HG, 4, 32)
        p[..., :HD] = v.reshape(HG, 4, HD)
        p[..., 31] = one
        return p.reshape(HG, 128).T

    cols = {"tok_b": a["L0_tok_b"].reshape(2, EC).T, "ln_eps": np.full((128, 1), LN_EPS, f),
            "bp0": a["L0_attn_b_proj"].reshape(2, EC).T, "g2b": a["L0_ffn_g2b"].reshape(2, EC).T,
            "g1b": a["L0_ffn_g1b"].reshape(G_, 1), "norm_scale": a["L1_attn_norm_scale"].reshape(2, EC).T,
            "norm_bias": a["L1_attn_norm_bias"].reshape(2, EC).T, "bq1": by_head_vec(bq[:E], 1),
            "bk1": by_head_vec(bq[E:2 * E]), "bp1": a["L1_attn_b_proj"].reshape(2, EC).T,
            "rezero": np.broadcast_to(a["L1_attn_rezero"].reshape(1, 1), (128, 1)),
            "rms_eps": np.full((128, 1), RMS_EPS, f), "rms_ln": np.full((128, 1), LN_EPS, f)}
    vec = z(128, sum(k for _, k in VEC))
    at = 0
    for n, k in VEC:
        vec[:cols[n].shape[0], at:at + k] = cols[n]
        at += k
    out["vec"] = vec
    return out


def packed(arrays, np):
    out = {}
    for pack, names in PACKS.items():
        for tail, is_f32 in (("f", True), ("b", False)):
            chosen = [arrays[n] for n in names if (arrays[n].dtype == np.float32) == is_f32]
            if chosen:
                whole = np.zeros((128, sum(a[0].size for a in chosen)), chosen[0].dtype)
                at = 0
                for a in chosen:
                    whole[:a.shape[0], at:at + a[0].size] = a.reshape(a.shape[0], -1)
                    at += a[0].size
                out[f"pack_{pack}_{tail}"] = whole
    in_packs = {n for names in PACKS.values() for n in names}
    out.update({n: np.ascontiguousarray(a) for n, a in arrays.items() if n not in in_packs})
    return out



def kernel(**inputs):
    import numpy as _np
    import ml_dtypes as _ml
    import concourse.bacc as _bacc
    from concourse import mybir as _mybir
    from concourse.bass_utils import run_bass_kernel_spmd as _run

    nc = _bacc.Bacc("TRN2", target_bir_lowering=False, num_devices=1)
    views = laid_out(inputs, _np, _ml.bfloat16)
    shapes = {n: v.shape for n, v in views.items()}
    types = {n: _mybir.dt.from_np(v.dtype) for n, v in views.items()}
    arrays, args = {}, {}
    for name, a in packed(views, _np).items():
        arrays[f"in_{name}_dram"] = a
        args[name] = nc.dram_tensor(f"in_{name}_dram", a.shape, _mybir.dt.from_np(a.dtype), kind="ExternalInput").ap()
    out = nc.dram_tensor("out_0_dram", (IMAGES * TOK, E), F32, kind="ExternalOutput").ap()
    program(nc, args, shapes, types, out)
    r = _run(nc, [arrays], core_ids=[0])
    return r.results[0]["out_0_dram"].reshape(IMAGES, TOK, E)
```

```python
import concourse.bass as bass
from concourse import mybir
from contextlib import ExitStack

F32, BF16 = mybir.dt.float32, mybir.dt.bfloat16
ACT, ALU, AX = mybir.ActivationFunctionType, mybir.AluOpType, mybir.AxisListType

IMAGES, SIDE, PATCH = 32, 96, 16
GRID = SIDE // PATCH
TOK = GRID * GRID
E = 192
EC = E // 2
HEADS, HD = 12, 16
HG = HEADS // 4
PER = 3
GROUPS = -(-IMAGES // PER)
GT = PER * TOK
IMG_P = GROUPS * PER
NT = IMG_P * TOK
BL = 3
BN = NT // BL
BIMG = BN // TOK
EB = IMAGES * TOK // BL
PK = 3 * PATCH * PATCH // 128
ROWS, COLS = 7, 5
S_, R_, M_, H_, TOPK, G_ = 8, 16, 64, 32, 4, 64
CH = M_ * H_ // 128
W1_COLS = M_ * H_ + S_ * M_ * H_ // (S_ * R_)
FF = 512
LN_EPS, RMS_EPS, Q_EPS = 1e-5, 1e-6, 1e-5
NEG, TAKEN, SENTINEL = -1e30, -1e38, -3e38
ROUND = 1.5 * 2.0 ** 23


def spread(ap, axis, n):
    ap = ap.unsqueeze(axis)
    shape = list(ap.shape)
    shape[axis] = n
    return ap.to_broadcast(shape)


def over_groups(eng, step):
    step(0, 0)
    step(1, 1)
    with eng.Fori(1, GROUPS // 2) as pair:
        step(pair * 2, 0)
        step(pair * 2 + 1, 1)
    if GROUPS % 2:
        step(GROUPS - 1, 0)


def pipeline(eng, step, length, ahead=1, lead=4):
    full = lead + (GROUPS - ahead - lead) // 2 * 2
    for k in range(lead):
        step(k, k % 2)
    with eng.Fori(lead // 2, full // 2) as pair:
        step(pair * 2, 0)
        step(pair * 2 + 1, 1)
    for k in range(full, length):
        step(k, k % 2)


def is_group(i):
    return not isinstance(i, int) or 0 <= i < GROUPS


def is_early(i):
    return isinstance(i, int) and i < 2


def is_last(i):
    return isinstance(i, int) and i == GROUPS - 1


def pass_gate(eng, gate):
    eng.sem_inc(gate, 1)


class LayerNorm:

    def __init__(self, nc, tag, sem, ps, src, dst, centred, rstd, ones, eps, scale=None, bias=None):
        self.nc, self.ps, self.src, self.dst, self.centred, self.rstd = nc, ps, src, dst, centred, rstd
        self.squared = dst
        self.ones, self.eps, self.scale, self.bias = ones, eps, scale, bias
        self.mean_then_var, self.square_then_std = sem(f"{tag}_mean_then_var"), sem(f"{tag}_square_then_std")
        self.centred_ready, self.rstd_ready, self.normed = (sem(f"{tag}_centred"), sem(f"{tag}_rstd"),
                                                            sem(f"{tag}_normed"))
        self.scaled = sem(f"{tag}_scaled") if scale is not None else None
        self.blocks = [slice(b * BN, (b + 1) * BN) for b in range(BL)]

    def statistics(self, pe):
        for b, cols in enumerate(self.blocks):
            for a in range(2):
                last = self.nc.tensor.matmul(self.ps[0:EC, b, 0:BN], self.ones[:, :], self.src[:, a, cols],
                                             start=a == 0, stop=a == 1)
            last.then_inc(self.mean_then_var, 1)
        for b, cols in enumerate(self.blocks):
            pe.wait_ge(self.square_then_std, b + 1)
            for a in range(2):
                last = self.nc.tensor.matmul(self.ps[0:EC, BL + b, 0:BN], self.ones[:, :], self.squared[:, a, cols],
                                             start=a == 0, stop=a == 1)
            last.then_inc(self.mean_then_var, 1)

    def squares_and_roots(self, act):
        for b, cols in enumerate(self.blocks):
            act.wait_ge(self.centred_ready, b + 1)
            self.nc.scalar.activation(self.squared[:, :, cols], self.centred[:, :, cols], ACT.Square).then_inc(
                self.square_then_std, 1)
        for b, cols in enumerate(self.blocks):
            act.wait_ge(self.mean_then_var, BL + b + 1)
            self.nc.scalar.activation(self.rstd[:, cols], self.ps[0:EC, BL + b, 0:BN], ACT.Sqrt,
                                      bias=self.eps).then_inc(self.square_then_std, 1)

    def centre(self, dve):
        for b, cols in enumerate(self.blocks):
            dve.wait_ge(self.mean_then_var, b + 1)
            self.nc.vector.tensor_tensor(self.centred[:, :, cols], self.src[:, :, cols],
                                         spread(self.ps[0:EC, b, 0:BN], 1, 2), ALU.subtract).then_inc(
                                             self.centred_ready, 1)

    def divide(self, dve, b):
        cols = self.blocks[b]
        dve.wait_ge(self.square_then_std, BL + b + 1)
        self.nc.vector.reciprocal(self.rstd[:, cols], self.rstd[:, cols]).then_inc(self.rstd_ready, 1)
        dve.wait_ge(self.rstd_ready, b + 1)
        self.nc.vector.tensor_tensor(self.dst[:, :, cols], self.centred[:, :, cols], spread(self.rstd[:, cols], 1, 2),
                                     ALU.mult).then_inc(self.normed, 1)

    def scale_and_bias(self, act, b):
        act.wait_ge(self.normed, b + 1)
        for a in range(2):
            part = self.dst[:, a, self.blocks[b]]
            self.nc.scalar.activation(part, part, ACT.Identity, scale=self.scale[:, a:a + 1],
                                      bias=self.bias[:, a:a + 1]).then_inc(self.scaled, 1)

    def await_banks(self, eng):
        eng.wait_ge(self.centred_ready, BL)
        eng.wait_ge(self.square_then_std, 2 * BL)

    def await_block(self, eng, b):
        if self.scale is None:
            eng.wait_ge(self.normed, b + 1)
        else:
            eng.wait_ge(self.scaled, 2 * b + 2)


def attention(nc, tag, sem, sb, ps, QT, KT, UT, xnT, wv, v_bias, v_start, mask, blocks4, ident, identb, sink=None,
              meanwhile=None):
    KW = GT + (sink is not None)
    qs = [sb(f"{tag}_queries{p}", [128, HG, GT]) for p in range(2)]
    xs = [sb(f"{tag}_tokens{p}", [EC, 2, GT]) for p in range(2)]
    kd = [sb(f"{tag}_keys_by_head{p}", [128, HG, 4, KW]) for p in range(2)]
    va = [sb(f"{tag}_values{p}", [KW, HEADS, 32]) for p in range(2)]
    probs = [sb(f"{tag}_probs{p}", [GT, HEADS, KW]) for p in range(2)]
    pt = [sb(f"{tag}_probs_by_key{p}", [KW, HEADS, GT]) for p in range(2)]
    top = sb(f"{tag}_row_max", [GT, HEADS])
    scores = ps[0:GT, 0:HG, 0:4 * KW].rearrange("q g (h k) -> q g h k", h=4)
    probs_ps = ps[0:KW, HG:2 * HG, 0:4 * GT]
    v_ps = ps[0:GT, 6, 0:E]
    u_ps = ps[:, 7, 0:HG * GT]

    filled = sem(f"{tag}_constant_parts_filled")
    sliced, keys_ready, v_done = sem(f"{tag}_sliced"), sem(f"{tag}_keys"), sem(f"{tag}_v_product")
    values_ready, scored = sem(f"{tag}_values_ready"), sem(f"{tag}_scored")
    max_ready, shifted, exp_ready = sem(f"{tag}_max"), sem(f"{tag}_shifted"), sem(f"{tag}_exp")
    turned, turned_copied = sem(f"{tag}_turned"), sem(f"{tag}_turned_copied")
    summed, summed_copied = sem(f"{tag}_summed"), sem(f"{tag}_summed_copied")

    def cols(i):
        return bass.ds(i * GT, GT)

    with nc.Block() as block:
        @block.sync
        def _(sp):
            if meanwhile is not None:
                meanwhile(sp)

        @block.gpsimd
        def _(pool):
            for p in range(2):
                nc.gpsimd.tensor_copy(va[p][:, :, :], v_start[:, :, :]).then_inc(filled, 1)
            if sink is not None:
                for p in range(2):
                    nc.gpsimd.tensor_copy(kd[p][:, :, :, GT], sink[:, :, :]).then_inc(filled, 1)

            def step(i, p):
                if not is_early(i):
                    pool.wait_ge(scored, HG * i - HG)
                    pool.wait_ge(v_done, i - 1)
                pool.wait_ge(filled, 2)
                nc.gpsimd.tensor_copy(qs[p][:, :, :], QT[:, :, cols(i)]).then_inc(sliced, 1)
                nc.gpsimd.tensor_copy(xs[p][:, :, :], xnT[:, :, cols(i)]).then_inc(sliced, 1)
            over_groups(pool, step)

        @block.tensor
        def _(pe):
            def values_and_scores(i, p):
                pe.wait_ge(sliced, 2 * i + 2)
                pe.wait_ge(keys_ready, i + 1)
                for g in range(HG):
                    if not (isinstance(i, int) and i < 1):
                        pe.wait_ge(shifted, HG * i + g - 2)
                    out = ps[0:GT, g, 0:4 * KW]
                    nc.tensor.matmul(out, identb[0:GT, 0:GT], mask[:, :], start=True, stop=False)
                    nc.tensor.matmul(out, qs[p][:, g, :], kd[p][:, g, :, :].rearrange("p h k -> p (h k)"),
                                     start=False, stop=True).then_inc(scored, 1)
                if not (isinstance(i, int) and i < 1):
                    pe.wait_ge(values_ready, i)
                for a in range(2):
                    last = nc.tensor.matmul(v_ps, xs[p][:, a, :], wv[:, a, :], start=a == 0, stop=a == 1)
                last.then_inc(v_done, 1)

            def turn(i, p):
                for g in range(HG):
                    pe.wait_ge(exp_ready, HG * i + g + 1)
                    if not (isinstance(i, int) and i < 1):
                        pe.wait_ge(turned_copied, HG * i + g - 2)
                    for h in range(4):
                        last = nc.tensor.transpose(ps[0:KW, HG + g, h * GT:(h + 1) * GT], probs[p][:, 4 * g + h, :],
                                                   ident[0:GT, 0:GT])
                    last.then_inc(turned, 1)

            def weighted_sums(i, p):
                pe.wait_ge(values_ready, i + 1)
                if not (isinstance(i, int) and i < 1):
                    pe.wait_ge(summed_copied, i)
                for g in range(HG):
                    pe.wait_ge(turned_copied, HG * i + g + 1)
                    for h in range(4):
                        last = nc.tensor.matmul(ps[32 * h:32 * h + 32, 7, g * GT:(g + 1) * GT], va[p][:, 4 * g + h, :],
                                                pt[p][:, 4 * g + h, :], start=True, stop=True)
                last.then_inc(summed, 1)

            values_and_scores(0, 0)

            def step(i, p):
                if not is_last(i):
                    values_and_scores(i + 1, 1 - p)
                if not (isinstance(i, int) and i < 1):
                    weighted_sums(i - 1, 1 - p)
                turn(i, p)
            over_groups(pe, step)
            weighted_sums(GROUPS - 1, (GROUPS - 1) % 2)

        @block.vector
        def _(dve):
            def keys(i, p):
                if not is_early(i):
                    dve.wait_ge(scored, HG * i - HG)
                for g in range(HG):
                    last = nc.vector.tensor_tensor(kd[p][:, g, :, 0:GT], spread(KT[:, g, cols(i)], 1, 4),
                                                   spread(blocks4[:, :], 2, GT), ALU.mult)
                last.then_inc(keys_ready, 1)

            if sink is not None:
                dve.wait_ge(filled, 4)
            keys(0, 0)

            def step(i, p):
                if not is_last(i):
                    keys(i + 1, 1 - p)
                def row_max(g):
                    dve.wait_ge(scored, HG * i + g + 1)
                    nc.vector.reduce_max(top[:, 4 * g:4 * g + 4], scores[:, g], AX.X).then_inc(max_ready, 1)

                def shift(g):
                    dve.wait_ge(max_ready, HG * i + g + 1)
                    if not is_early(i):
                        dve.wait_ge(turned, HG * i + g - 5)
                    nc.vector.tensor_tensor(probs[p][:, 4 * g:4 * g + 4, :], scores[:, g],
                                            spread(top[:, 4 * g:4 * g + 4], 2, KW), ALU.subtract).then_inc(shifted, 1)

                row_max(0)
                for g in range(1, HG):
                    row_max(g)
                    shift(g - 1)
                shift(HG - 1)
                if not is_early(i):
                    dve.wait_ge(summed, i - 1)
                dve.wait_ge(filled, 2)
                dve.wait_ge(v_done, i + 1)
                out = va[p][0:GT, :, 0:HD]
                v = v_ps.rearrange("k (h d) -> k h d", h=HEADS)
                if v_bias is None:
                    nc.vector.tensor_copy(out, v).then_inc(values_ready, 1)
                else:
                    nc.vector.tensor_tensor(out, v, v_bias[:, :, :], ALU.add).then_inc(values_ready, 1)
            over_groups(dve, step)

        @block.scalar
        def _(act):
            def exponentials(i, p):
                for g in range(HG):
                    act.wait_ge(shifted, HG * i + g + 1)
                    part = probs[p][:, 4 * g:4 * g + 4, :]
                    nc.scalar.activation(part, part, ACT.Exp).then_inc(exp_ready, 1)

            def copy_sums(i):
                act.wait_ge(summed, i + 1)
                act.wait_ge(filled, 2)
                nc.scalar.copy(UT[:, :, cols(i)], u_ps.rearrange("p (g q) -> p g q", g=HG)).then_inc(summed_copied, 1)

            exponentials(0, 0)

            def step(i, p):
                if not (isinstance(i, int) and i < 1):
                    copy_sums(i - 1)
                for g in range(HG):
                    act.wait_ge(turned, HG * i + g + 1)
                    nc.scalar.copy(pt[p][:, 4 * g:4 * g + 4, :].rearrange("k h q -> k (h q)"),
                                   probs_ps[:, g, :]).then_inc(turned_copied, 1)
                if not is_last(i):
                    exponentials(i + 1, 1 - p)
            over_groups(act, step)
            copy_sums(GROUPS - 1)


def free_size(shape):
    n = 1
    for k in shape[1:]:
        n *= k
    return n


PACKS = {
    "first": ("vec", "ones"),
    "embedding": ("tok_w",),
    "kept": ("ident", "identb", "blocks4", "den_rows", "den_back", "P", "C", "sel", "b2", "G1", "G2"),
    "attention0": ("wq0", "wk0", "av", "ah", "kconst", "mask0", "wv0", "v_start0", "bv", "bh", "wp0"),
    "attention1": ("wq1", "wk1", "rot", "cosq", "sinq", "cosk", "sink_", "mask1", "wv1", "vb1", "v_start1", "sinkcol",
                   "wp1"),
    "feed_forward1": ("gb_in", "gb_out", "w_in", "w_out", "all_ones"),
}


def program(nc, ins, shapes, ins_types, out):
    with ExitStack() as ctx:
        def sem(name):
            return ctx.enter_context(nc.semaphore(name))

        def allocator(stack):
            return lambda name, shape, dt=F32: stack.enter_context(nc.sbuf_tensor(name, shape, dt))

        gate = sem("gate")
        sb = allocator(ctx)
        ps = ctx.enter_context(nc.psum_tensor("banks", [128, 8, 512], F32))

        held = {}
        def hold(stack, pack):
            for dt, tail in ((F32, "f"), (BF16, "b")):
                names = [n for n in PACKS[pack] if ins_types[n] == dt]
                if names:
                    width = sum(free_size(shapes[n]) for n in names)
                    tile = allocator(stack)(f"pack_{pack}_{tail}", [128, width], dt)
                    packs[pack].append((tile, ins[f"pack_{pack}_{tail}"]))
                    at = 0
                    for n in names:
                        shape, size = shapes[n], free_size(shapes[n])
                        view = tile[0:shape[0], at:at + size]
                        if len(shape) == 3:
                            view = view.rearrange("p (a n) -> p a n", a=shape[1])
                        elif len(shape) == 4:
                            view = view.rearrange("p (a b n) -> p a b n", a=shape[1], b=shape[2])
                        held[n] = view
                        at += size

        packs = {pack: [] for pack in PACKS}
        loaded = {pack: sem(f"loaded_{pack}") for pack in PACKS}

        def load(eng, pack):
            for tile, src in packs[pack]:
                eng.dma_start(tile[:], src).then_inc(loaded[pack], 16)

        def await_pack(eng, pack):
            eng.wait_ge(loaded[pack], 16 * len(packs[pack]))

        hold(ctx, "first")
        hold(ctx, "kept")
        hT = sb("hT", [EC, 2, NT])
        w_stack = sb("w1_parts_by_row", [128, S_, M_ * H_], BF16)
        w1_loaded = sem("loaded_W1")
        stacked_w = sem("w1_parts_stacked")
        vec = held["vec"]
        scratch = {"w1": nc.dram_tensor("scratch_w1", (3, S_ * R_, M_ * H_), BF16, kind="Internal").ap(),
                   "b1": nc.dram_tensor("scratch_b1", (3, 128, W1_COLS - M_ * H_), BF16, kind="Internal").ap(),
                   "z": nc.dram_tensor("scratch_z", (3, S_ * R_, NT), BF16, kind="Internal").ap()}
        V = {}
        for i, (n, k) in enumerate(VEC):
            V[n] = vec[0:VROWS[n], sum(k for _, k in VEC[:i]):sum(k for _, k in VEC[:i + 1])]

        with ExitStack() as mem:
            hold(mem, "embedding")
            hold(mem, "attention0")
            sb2 = allocator(mem)
            w1 = sb2("w1_and_b1", [S_ * R_, W1_COLS])
            w1_parts = [sb2(f"w1_part{n}", [S_ * R_, W1_COLS], BF16) for n in range(3)]
            embed(nc, sem, allocator, ps, ins, held, load, await_pack, hT, V, w_stack, w1, w1_loaded)
            s = allocator(mem)
            xnT = s("xnT0", [EC, 2, NT])
            QT, KT, UT = s("QT0", [128, HG, NT]), s("KT0", [128, HG, NT]), s("UT0", [128, HG, NT])
            with ExitStack() as mem2:
                s2 = allocator(mem2)
                norm = LayerNorm(nc, "ln0", sem, ps, hT, xnT, s2("centred0", [EC, 2, NT]), s2("rstd0", [EC, NT]),
                                 held["ones"], V["ln_eps"])
                project_qk0(nc, sem, ps, held, await_pack, norm, xnT, UT, QT, KT, w1, w1_loaded, w1_parts)
            with ExitStack() as mem2:
                attention(nc, "a0", sem, allocator(mem2), ps, QT, KT, UT, xnT, held["wv0"], None, held["v_start0"],
                          held["mask0"], held["blocks4"], held["ident"], held["identb"],
                          meanwhile=lambda sp: stack_w1(sp, w1_parts, scratch, sem("w1_parts_out"), w_stack,
                                                        stacked_w))
            class_pass(nc, sem, "u0_classes", ps, held["bv"], held["bh"], [UT[:, g, :] for g in range(HG)],
                       [QT[:, g, :] for g in range(HG)])
            project_out(nc, sem, "a0", s, ps, held, UT, QT, held["wp0"], hT, V["bp0"])

        with ExitStack() as mem:
            experts(nc, sem, gate, allocator(mem), allocator, ps, ins, held, scratch, hT, w_stack, V)

        hold(ctx, "attention1")
        hold(ctx, "feed_forward1")
        rounding = WeightRounding(nc, sem, sb, ps, held)
        with ExitStack() as mem:
            s = allocator(mem)
            xnT = s("xnT2", [EC, 2, NT])
            QT, KT, UT = s("QT1", [128, HG, NT]), s("KT1", [128, HG, NT]), s("UT1", [128, HG, NT])
            with ExitStack() as mem2:
                s2 = allocator(mem2)
                norm = LayerNorm(nc, "ln2", sem, ps, hT, xnT, s2("centred2", [EC, 2, NT]), s2("rstd2", [EC, NT]),
                                 held["ones"], V["ln_eps"], V["norm_scale"], V["norm_bias"])
                project_qk1(nc, sem, s2, ps, held, load, await_pack, norm, xnT, QT, KT, V)
            with ExitStack() as mem2:
                attention(nc, "a1", sem, allocator(mem2), ps, QT, KT, UT, xnT, held["wv1"], held["vb1"],
                          held["v_start1"], held["mask1"], held["blocks4"], held["ident"], held["identb"],
                          held["sinkcol"])
            project_out(nc, sem, "a1", s, ps, held, UT, UT, held["wp1"], hT, V["bp1"], V["rezero"], rounding)

        with ExitStack() as mem:
            quantised(nc, sem, gate, allocator(mem), ps, held, rounding, hT, out, V)


VEC = [("tok_b", 2), ("ln_eps", 1), ("bp0", 2), ("g2b", 2), ("g1b", 1), ("norm_scale", 2), ("norm_bias", 2),
       ("bq1", 3), ("bk1", 3), ("bp1", 2), ("rezero", 1), ("rms_eps", 1), ("rms_ln", 1)]
VROWS = {"tok_b": 96, "ln_eps": 96, "bp0": 96, "g2b": 96, "g1b": 64, "norm_scale": 96, "norm_bias": 96,
         "bq1": 128, "bk1": 128, "bp1": 96, "rezero": 96, "rms_eps": 128, "rms_ln": 128}


def embed(nc, sem, allocator, ps, ins, held, load, await_pack, hT, V, w_stack, w1, w1_loaded):
    with ExitStack() as mem:
        sb = allocator(mem)
        xt = sb("xt", [128, PK, NT])
        X_LOADS = [(0, 1), (1, 2), (2, 4), (4, PK)]
        x_loaded = [sem(f"loaded_x{k}") for k in range(len(X_LOADS))]
        tok_done, cleared = sem("tok_done"), sem("w_stack_cleared")

        with nc.Block() as block:
            @block.sync
            def _(sp):
                load(sp, "embedding")
                for k, (lo, hi) in enumerate(X_LOADS):
                    sp.dma_start(xt[:, lo:hi, :], ins["xt"][:, lo:hi, :]).then_inc(x_loaded[k], 16)
                load(sp, "first")
                load(sp, "attention0")
                load(sp, "kept")
                sp.dma_start(w1[:], ins["W1"]).then_inc(w1_loaded, 16)

            @block.gpsimd
            def _(pool):
                rows = w_stack[64:128, :, :].rearrange("p s n -> p (s n)").bitcast(F32)
                nc.gpsimd.memset(rows, 0.0).then_inc(cleared, 1)
                pool.wait_ge(cleared, 1)

            @block.tensor
            def _(pe):
                await_pack(pe, "embedding")
                for k in range(PK):
                    for n, (lo, hi) in enumerate(X_LOADS):
                        if lo == k:
                            pe.wait_ge(x_loaded[n], 16)
                    for b in range(BL):
                        for a in range(2):
                            last = nc.tensor.matmul(ps[0:EC, 2 * b + a, 0:BN], held["tok_w"][:, k, a * EC:(a + 1) * EC],
                                                    xt[:, k, b * BN:(b + 1) * BN], start=k == 0, stop=k == PK - 1)
                            if k == PK - 1:
                                last.then_inc(tok_done, 1)

            @block.scalar
            def _(act):
                await_pack(act, "first")
                for b in range(BL):
                    for a in range(2):
                        act.wait_ge(tok_done, 2 * b + a + 1)
                        nc.scalar.activation(hT[:, a, b * BN:(b + 1) * BN], ps[0:EC, 2 * b + a, 0:BN], ACT.Identity,
                                             bias=V["tok_b"][:, a:a + 1])


W_ROWS = [(0, 0), (16, 1), (32, 0), (48, 1), (64, 0), (96, 2)]
Z_ROWS = [(0, 0), (16, 0), (32, 1), (48, 1), (64, 2), (96, 0)]
BIAS_ROW = 112


def stack_w1(sp, w_part, scratch, parts_out, w_stack, stacked_w):
    for n in range(3):
        sp.dma_start(scratch["w1"][n], w_part[n][:, 0:M_ * H_]).then_inc(parts_out, 16)
        sp.dma_start(scratch["b1"][n], w_part[n][:, M_ * H_:W1_COLS]).then_inc(parts_out, 16)
    sp.wait_ge(parts_out, 6 * 16)
    for row, part in W_ROWS:
        sp.dma_start(w_stack[row:row + R_, :, :],
                     scratch["w1"][part].rearrange("(s r) n -> r s n", r=R_)).then_inc(stacked_w, 16)
    sp.dma_start(w_stack[BIAS_ROW:BIAS_ROW + 3, :, :].rearrange("n s c -> n (s c)"),
                 scratch["b1"].rearrange("n p c -> n (p c)")).then_inc(stacked_w, 16)
    sp.wait_ge(stacked_w, 16 * (len(W_ROWS) + 1))


def images(ap):
    return ap.rearrange("p (b t) -> p b t", t=TOK)


def class_units():
    rows = [(r, ("row", r)) for r in range(ROWS)] + [(ROWS, ("first", 0))]
    cols = [(c, ("col", c)) for c in range(COLS)] + [(COLS, ("first", 0))]
    return [(0, rows[0:3]), (0, rows[3:6]), (0, rows[6:7]), (0, rows[7:8]),
            (1, cols[0:2]), (1, cols[2:4]), (1, cols[4:5]), (1, cols[5:6])]


def positions(ap, kinds):
    v = images(ap)
    kind, first = kinds[0]
    if kind == "first":
        return v[:, :, 0:1]
    grid = v[:, :, 1:TOK].rearrange("p b (r c) -> p b r c", c=COLS)
    n = len(kinds)
    if kind == "row":
        t = grid[:, :, first:first + n, :].rearrange("p b r c -> p r b c")
    else:
        t = grid[:, :, :, first:first + n].rearrange("p b r c -> p c b r")
    return t if n > 1 else t[:, 0]


def class_pass(nc, sem, tag, ps, by_row, by_col, srcs, dsts):
    done, copied = sem(f"{tag}_product"), sem(f"{tag}_copied")
    units = [(n, u) for n in range(len(srcs)) for u in class_units()]

    def view(bank, kinds, size):
        n = len(kinds)
        flat = ps[:, bank, 0:n * size * IMG_P]
        if n > 1:
            return flat.rearrange("p (k b t) -> p k b t", k=n, b=IMG_P)
        return flat.rearrange("p (b t) -> p b t", b=IMG_P)

    def size(kinds):
        return {"first": 1, "row": COLS, "col": ROWS}[kinds[0][0]]

    with nc.Block() as block:
        @block.tensor
        def _(pe):
            for i, (n, (which, classes)) in enumerate(units):
                if i >= 8:
                    pe.wait_ge(copied, i - 7)
                m = (by_row, by_col)[which]
                for j, (c, kind) in enumerate(classes):
                    k = size([kind])
                    last = nc.tensor.matmul(ps[:, i % 8, j * k * IMG_P:(j + 1) * k * IMG_P].rearrange(
                        "p (b t) -> p b t", b=IMG_P), m[:, c, :], positions(srcs[n], [kind]), start=True, stop=True)
                last.then_inc(done, 1)

        @block.vector
        def _(dve):
            for i, (n, (which, classes)) in enumerate(units):
                dve.wait_ge(done, i + 1)
                kinds = [k for _, k in classes]
                got, dst = view(i % 8, kinds, size(kinds)), positions(dsts[n], kinds)
                if which == 0:
                    nc.vector.tensor_copy(dst, got).then_inc(copied, 1)
                else:
                    if i % 8 == 4:
                        dve.wait_ge(copied, i)
                    nc.vector.tensor_tensor(dst, dst, got, ALU.add).then_inc(copied, 1)


def project_qk0(nc, sem, ps, held, await_pack, norm, xnT, base, QT, KT, w1, w1_loaded, w1_parts):
    done, q_copied, k_copied = sem("qk0_product"), sem("q0_copied"), sem("k0_copied")
    rounded, left = sem("w1_part_rounded"), sem("w1_part_left")
    units = [(b, w, g) for b in range(BL) for w in ("wq0", "wk0") for g in range(HG)]

    def place(i):
        b, w, g = units[i]
        return (q_copied if w == "wq0" else k_copied), b * HG + g + 1

    with nc.Block() as block:
        @block.sync
        def _(sp):
            await_pack(sp, "kept")

        @block.tensor
        def _(pe):
            norm.statistics(pe)
            await_pack(pe, "attention0")
            norm.await_banks(pe)
            for i, (b, w, g) in enumerate(units):
                if i >= 8:
                    pe.wait_ge(*place(i - 8))
                norm.await_block(pe, b)
                for a in range(2):
                    last = nc.tensor.matmul(ps[:, i % 8, 0:BN], held[w][:, a, g, :], xnT[:, a, b * BN:(b + 1) * BN],
                                            start=a == 0, stop=a == 1)
                last.then_inc(done, 1)

        @block.scalar
        def _(act):
            norm.squares_and_roots(act)
            act.wait_ge(w1_loaded, 16)
            for b in range(BL):
                if b > 0:
                    act.wait_ge(left, b)
                nc.scalar.copy(w1_parts[b][:], w1[:]).then_inc(rounded, 1)
                for g in range(HG):
                    i = b * 2 * HG + g
                    act.wait_ge(done, i + 1)
                    nc.scalar.mul(base[:, g, b * BN:(b + 1) * BN], ps[:, i % 8, 0:BN], HD ** -0.5).then_inc(q_copied, 1)

        @block.vector
        def _(dve):
            def keys(b):
                for g in range(HG):
                    i = b * 2 * HG + HG + g
                    dve.wait_ge(done, i + 1)
                    nc.vector.tensor_tensor(images(KT[:, g, b * BN:(b + 1) * BN]), images(ps[:, i % 8, 0:BN]),
                                            spread(held["kconst"][:, :], 1, BIMG), ALU.add).then_inc(k_copied, 1)

            def rest_of_w1(n):
                dve.wait_ge(rounded, n + 1)
                nc.vector.tensor_tensor(w1[:], w1[:], w1_parts[n][:], ALU.subtract).then_inc(left, 1)

            norm.centre(dve)
            norm.divide(dve, 0)
            norm.divide(dve, 1)
            rest_of_w1(0)
            keys(0)
            norm.divide(dve, 2)
            rest_of_w1(1)
            keys(1)
            keys(2)

    class_pass(nc, sem, "q0_classes", ps, held["av"], held["ah"], [base[:, g, :] for g in range(HG)],
               [QT[:, g, :] for g in range(HG)])


def project_out(nc, sem, tag, sb, ps, held, UT, OT, wp, hT, bias, factor=None, rounding=None):
    gathered, inv = sem(f"{tag}_den"), sem(f"{tag}_inverted")
    back, divided = sem(f"{tag}_spread"), sem(f"{tag}_divided")
    done, biased, added = sem(f"{tag}_out_product"), sem(f"{tag}_out_biased"), sem(f"{tag}_out_added")
    inverse = sb(f"{tag}_inverse", [32 * BL, BN])
    scaled = sb(f"{tag}_out_scaled", [EC, BN])

    def back_bank(b, g):
        return 1 + HG * (b % 2) + g

    def cols(b):
        return slice(b * BN, (b + 1) * BN)

    with nc.Block() as block:
        @block.tensor
        def _(pe):
            for b in range(BL):
                for g in range(HG):
                    last = nc.tensor.matmul(ps[32 * b:32 * b + 32, 0, 0:BN], held["den_rows"][:, g, :],
                                            UT[:, g, cols(b)], start=g == 0, stop=g == HG - 1)
            last.then_inc(gathered, 1)
            if rounding is not None:
                rounding.total(pe)
            pe.wait_ge(inv, 1)

            def spread_back(b):
                if b >= 2:
                    pe.wait_ge(divided, HG * (b - 1))
                for g in range(HG):
                    nc.tensor.matmul(ps[:, back_bank(b, g), 0:BN], held["den_back"][32 * b:32 * b + 32, g, :],
                                     inverse[32 * b:32 * b + 32, :], start=True, stop=True).then_inc(back, 1)

            spread_back(0)
            for b in range(BL):
                if b + 1 < BL:
                    spread_back(b + 1)
                pe.wait_ge(divided, HG * (b + 1))
                for m in range(2):
                    if b > 0:
                        pe.wait_ge(added, 2 * b + m - 1)
                    for g in range(HG):
                        last = nc.tensor.matmul(ps[0:EC, (7, 0)[m], 0:BN], wp[:, g, m * EC:(m + 1) * EC],
                                                OT[:, g, cols(b)], start=g == 0, stop=g == HG - 1)
                    last.then_inc(done, 1)

        @block.vector
        def _(dve):
            def divide(b):
                for g in range(HG):
                    dve.wait_ge(back, HG * b + g + 1)
                    t = OT[:, g, cols(b)]
                    nc.vector.tensor_tensor(t, t, ps[:, back_bank(b, g), 0:BN], ALU.mult).then_inc(divided, 1)

            def add(b):
                for m in range(2):
                    i = 2 * b + m
                    product, h = ps[0:EC, (7, 0)[m], 0:BN], hT[:, m, cols(b)]
                    dve.wait_ge(done, i + 1)
                    if factor is None:
                        nc.vector.scalar_tensor_tensor(h, product, bias[:, m:m + 1], h, ALU.add, ALU.add).then_inc(
                            added, 1)
                    else:
                        if i > 0:
                            dve.wait_ge(added, i)
                        nc.vector.tensor_scalar(scaled[:, :], product, bias[:, m:m + 1], factor, ALU.add,
                                                ALU.mult).then_inc(biased, 1)
                        dve.wait_ge(biased, i + 1)
                        nc.vector.tensor_tensor(h, h, scaled[:, :], ALU.add).then_inc(added, 1)

            if rounding is not None:
                rounding.weight_sums(dve)
            dve.wait_ge(gathered, 1)
            nc.vector.reciprocal(inverse[:, :], ps[0:32 * BL, 0, 0:BN]).then_inc(inv, 1)
            if rounding is not None:
                rounding.scales(dve)
            divide(0)
            for b in range(BL):
                if b + 1 < BL:
                    divide(b + 1)
                    if rounding is not None:
                        rounding.round(dve, b)
                add(b)


def project_qk1(nc, sem, sb, ps, held, load, await_pack, norm, xnT, QT, KT, V):
    base = sb("qk1_base", [128, BN]), sb("qk1_base_b", [128, BN])
    turned = sb("qk1_sin", [128, BN]), sb("qk1_sin_b", [128, BN])
    done, biased, rotated = sem("qk1_product"), sem("qk1_biased"), sem("qk1_rotated")
    cos_part, sin_part = sem("qk1_cos_part"), sem("qk1_sin_part")
    units = [(b, w, g) for b in range(BL) for w in range(2) for g in range(HG)]
    per_block = 2 * HG

    def target(i):
        b, w, g = units[i]
        return (QT, KT)[w][:, g, b * BN:(b + 1) * BN]

    with nc.Block() as block:
        @block.sync
        def _(sp):
            load(sp, "attention1")
            load(sp, "feed_forward1")
            await_pack(sp, "attention1")
            await_pack(sp, "feed_forward1")

        @block.tensor
        def _(pe):
            def product(i):
                b, w, g = units[i]
                norm.await_block(pe, b)
                if i >= 4:
                    pe.wait_ge(biased, i - 3)
                for a in range(2):
                    last = nc.tensor.matmul(ps[:, i % 4, 0:BN], held[("wq1", "wk1")[w]][:, a, g, :],
                                            xnT[:, a, b * BN:(b + 1) * BN], start=a == 0, stop=a == 1)
                last.then_inc(done, 1)

            norm.statistics(pe)
            await_pack(pe, "attention1")
            norm.await_banks(pe)
            product(0)
            for i in range(len(units)):
                if i + 1 < len(units):
                    product(i + 1)
                pe.wait_ge(biased, i + 1)
                if i >= 4:
                    pe.wait_ge(sin_part, i - 3)
                nc.tensor.matmul(ps[:, 4 + i % 4, 0:BN], held["rot"][:, :], base[i % 2][:, :], start=True,
                                 stop=True).then_inc(rotated, 1)

        @block.scalar
        def _(act):
            norm.squares_and_roots(act)
            norm.scale_and_bias(act, 0)
            norm.scale_and_bias(act, 1)
            for i, (b, w, g) in enumerate(units):
                if i == per_block:
                    norm.scale_and_bias(act, 2)
                act.wait_ge(done, i + 1)
                if i >= 2:
                    act.wait_ge(rotated, i - 1)
                    act.wait_ge(cos_part, i - 1)
                bias = V[("bq1", "bk1")[w]][:, g:g + 1]
                nc.scalar.activation(base[i % 2][:, :], ps[:, i % 4, 0:BN], ACT.Identity, bias=bias).then_inc(biased, 1)

        @block.gpsimd
        def _(pool):
            await_pack(pool, "attention1")
            for i, (b, w, g) in enumerate(units):
                pool.wait_ge(biased, i + 1)
                cos = (held["cosq"], held["cosk"])[w]
                nc.gpsimd.tensor_tensor(images(target(i)), images(base[i % 2][:, :]), spread(cos[:, :], 1, BIMG),
                                        ALU.mult).then_inc(cos_part, 1)

        @block.vector
        def _(dve):
            norm.centre(dve)
            norm.divide(dve, 0)
            norm.divide(dve, 1)
            for i, (b, w, g) in enumerate(units):
                if i == per_block // 2:
                    norm.divide(dve, 2)
                sin = (held["sinq"], held["sink_"])[w]
                dve.wait_ge(rotated, i + 1)
                nc.vector.tensor_tensor(images(turned[i % 2][:, :]), images(ps[:, 4 + i % 4, 0:BN]),
                                        spread(sin[:, :], 1, BIMG), ALU.mult).then_inc(sin_part, 1)
                dve.wait_ge(cos_part, i + 1)
                dve.wait_ge(sin_part, i + 1)
                nc.vector.tensor_tensor(target(i), target(i), turned[i % 2][:, :], ALU.add)


class WeightRounding:

    def __init__(self, nc, sem, sb, ps, held):
        self.nc, self.ps, self.held = nc, ps, held
        self.w = [held["w_in"], held["w_out"]]
        self.rounded_w = [sb("w_in_rounded", [EC, 2, 2 * FF], BF16), sb("w_out_rounded", [128, 4, E], BF16)]
        self.sums, self.step, self.inverse = sb("w_sums", [128, 2]), sb("w_steps", [128, 2]), sb("w_inverse", [128, 2])
        self.measured, self.summed = sem("wq_measured"), sem("wq_summed")
        self.scaled, self.rounded = sem("wq_scales"), sem("wq_rounded")

    def weight_sums(self, dve):
        self.nc.vector.memset(self.sums[:, :], 0.0).then_inc(self.measured, 1)
        dve.wait_ge(self.measured, 1)
        for k, w in enumerate(self.w):
            self.nc.vector.tensor_reduce(self.sums[0:w.shape[0], k:k + 1], w, AX.XY, ALU.add,
                                         apply_absolute_value=True).then_inc(self.measured, 1)

    def total(self, pe):
        pe.wait_ge(self.measured, 3)
        self.nc.tensor.matmul(self.ps[:, 7, 0:2], self.held["all_ones"][:, :], self.sums[:, :], start=True,
                              stop=True).then_inc(self.summed, 1)

    def scales(self, dve):
        dve.wait_ge(self.summed, 1)
        for k, size in enumerate((E * 2 * FF, E * FF)):
            self.nc.vector.tensor_scalar(self.step[:, k:k + 1], self.ps[:, 7, k:k + 1], 1.0 / size, Q_EPS, ALU.mult,
                                         ALU.max).then_inc(self.scaled, 1)
        dve.wait_ge(self.scaled, 2)
        self.nc.vector.reciprocal(self.inverse[:, :], self.step[:, :]).then_inc(self.scaled, 1)

    def round(self, dve, k):
        w = self.w[k]
        dve.wait_ge(self.scaled, 3)
        self.nc.vector.tensor_scalar(w, w, self.inverse[0:w.shape[0], k:k + 1], ROUND, ALU.mult, ALU.add).then_inc(
            self.rounded, 1)
        dve.wait_ge(self.rounded, 2 * k + 1)
        self.nc.vector.tensor_scalar(w, w, ROUND, -1.0, ALU.subtract, ALU.max).then_inc(self.rounded, 1)
        dve.wait_ge(self.rounded, 2 * k + 2)
        self.nc.vector.tensor_scalar(self.rounded_w[k][:], w, 1.0, None, ALU.min)


def experts(nc, sem, gate, sb, allocator, ps, ins, held, scratch, hT, w_stack, V):
    z_stack = sb("z_parts_by_row", [128, S_, NT], BF16)
    wt = sb("weights_by_expert", [128, S_ // 2, NT])
    g_stack = sb("weight_parts_by_row", [96, 2, 2, S_ // 2, NT], BF16)
    stacked_z, stacked_g = sem("z_parts_stacked"), sem("weight_parts_stacked")
    w2_loaded = sem("loaded_W2")
    held["W2"] = sb("in_W2", list(ins["W2"].shape))
    parts = sb("weight_parts", [128, 3, S_ // 2, NT], BF16)

    choosing = ExitStack()
    zT = allocator(choosing)("zT", [128, NT])
    with ExitStack() as mem:
        s3 = allocator(mem)
        xnT = s3("xnT1", [EC, 2, NT])
        norm = LayerNorm(nc, "ln1", sem, ps, hT, xnT, s3("centred1", [EC, 2, NT]), s3("rstd1", [EC, NT]), held["ones"],
                         V["ln_eps"])
        z_done, cleared = sem("z_done"), sem("z_stack_cleared")
        with nc.Block() as block:
            @block.gpsimd
            def _(pool):
                nc.gpsimd.memset(z_stack[64:128, :, :], 1.0).then_inc(cleared, 1)

            @block.tensor
            def _(pe):
                norm.statistics(pe)
                norm.await_banks(pe)
                for b in range(BL):
                    norm.await_block(pe, b)
                    for a in range(2):
                        last = nc.tensor.matmul(ps[:, b, 0:BN], held["P"][:, a, :], xnT[:, a, b * BN:(b + 1) * BN],
                                                start=a == 0, stop=a == 1)
                    last.then_inc(z_done, 1)

            @block.scalar
            def _(act):
                norm.squares_and_roots(act)
                for b in range(BL):
                    act.wait_ge(z_done, b + 1)
                    nc.scalar.copy(zT[:, b * BN:(b + 1) * BN], ps[:, b, 0:BN])

            @block.vector
            def _(dve):
                norm.centre(dve)
                for b in range(BL):
                    norm.divide(dve, b)

    with choosing:
        choose_experts(nc, sem, gate, allocator(choosing), ps, held, ins, scratch, zT, z_stack, stacked_z, w2_loaded,
                       wt, parts, g_stack, stacked_g)
    comb = sb("combined", [128, 2, BL * EB])
    with ExitStack() as mem:
        run_experts(nc, sem, gate, allocator(mem), ps, held, z_stack, stacked_z, parts, g_stack, stacked_g,
                    wt, w_stack, w2_loaded, comb)

    gated = sb("gated", [G_, NT])
    g1_done, gated_ready, g2_done = sem("g1_done"), sem("gated_ready"), sem("g2_done")
    with nc.Block() as block:
        @block.tensor
        def _(pe):
            for b in range(BL):
                for j in range(2):
                    last = nc.tensor.matmul(ps[0:G_, b, 0:EB], held["G1"][:, j, :], comb[:, j, b * EB:(b + 1) * EB],
                                            start=j == 0, stop=j == 1)
                last.then_inc(g1_done, 1)
            for b in range(BL):
                pe.wait_ge(gated_ready, b + 1)
                if b == 2:
                    pe.wait_ge(gated_ready, 3)
                for m in range(2):
                    bank = 3 + (2 * b + m) if 2 * b + m < 5 else 0
                    nc.tensor.matmul(ps[0:EC, bank, 0:EB], held["G2"][:, m * EC:(m + 1) * EC],
                                     gated[:, b * EB:(b + 1) * EB], start=True, stop=True).then_inc(g2_done, 1)

        @block.scalar
        def _(act):
            for b in range(BL):
                act.wait_ge(g1_done, b + 1)
                nc.scalar.activation(gated[:, b * EB:(b + 1) * EB], ps[0:G_, b, 0:EB], ACT.Gelu_apprx_tanh,
                                     bias=V["g1b"]).then_inc(gated_ready, 1)

        @block.vector
        def _(dve):
            for i in range(2 * BL):
                b, m = divmod(i, 2)
                dve.wait_ge(g2_done, i + 1)
                h = hT[:, m, b * EB:(b + 1) * EB]
                nc.vector.scalar_tensor_tensor(h, ps[0:EC, 3 + i if i < 5 else 0, 0:EB], V["g2b"][:, m:m + 1], h,
                                               ALU.add, ALU.add)


G_TRANSFERS = 12


def choose_experts(nc, sem, gate, sb, ps, held, ins, scratch, zT, z_stack, stacked_z, w2_loaded, wt, parts, g_stack,
                   stacked_g):
    W = M_ + TOPK
    zs = [sb(f"z_slice{p}", [128, GT]) for p in range(2)]
    sc = [sb(f"expert_scores{p}", [GT, S_, W]) for p in range(2)]
    marked = [sb(f"scores_marked{p}", [GT, S_, W]) for p in range(2)]
    best = sb("best", [GT, S_, 8])
    wanted = sb("wanted", [GT, S_, 8])
    ex = [sb(f"expert_exp{p}", [GT, S_, M_]) for p in range(2)]
    best_exp = [sb(f"best_exp{p}", [GT, S_, TOPK]) for p in range(2)]
    total = sb("exp_total", [GT, S_])
    left = [sb(f"weight_rest{p}", [128, S_ // 2, GT]) for p in range(2)]

    z_rest = held["W2"][:, 0:NT]
    z_part = [held["W2"][:, (n + 2) * NT // 2:(n + 3) * NT // 2].bitcast(BF16) for n in range(3)]
    z_rounded, z_left, z_out = sem("z_part_rounded"), sem("z_part_left"), sem("z_parts_out")

    sentinels, sliced, scored, score_copied = (sem("sentinels"), sem("z_sliced"), sem("expert_scored"),
                                               sem("expert_score_copied"))
    best_ready, wanted_ready, marked_ready = sem("best_ready"), sem("wanted_ready"), sem("marked_ready")
    centred, exp_ready, picked, total_ready, inverted = (sem("escore_centred"), sem("eexp_ready"), sem("picked"),
                                                         sem("etotal_ready"), sem("etotal_inverted"))
    weighed, turned, first_ready, wt_ready = (sem("eweighed"), sem("eweight_turned"), sem("first_ready"),
                                              sem("wt_ready"))
    left_ready, second_ready, third_ready = sem("eleft_ready"), sem("second_ready"), sem("third_ready")

    def cols(i):
        return bass.ds(i * GT, GT)

    def wps(p):
        return ps[:, 2 + p, 0:4 * GT].rearrange("p (s t) -> p s t", s=4)

    with nc.Block() as block:
        @block.gpsimd
        def _(pool):
            for p in range(2):
                nc.gpsimd.memset(sc[p][:, :, M_:W], SENTINEL).then_inc(sentinels, 1)
            nc.gpsimd.memset(wanted[:, :, TOPK:8], SENTINEL).then_inc(sentinels, 1)

            def slice_z(i, p):
                if not is_early(i):
                    pool.wait_ge(scored, i - 1)
                pass_gate(pool, gate)
                nc.gpsimd.tensor_copy(zs[p][:, :], zT[:, cols(i)]).then_inc(sliced, 1)

            slice_z(0, 0)
            slice_z(1, 1)

            for n in range(2):
                pool.wait_ge(z_rounded, n + 1)
                nc.gpsimd.tensor_tensor(z_rest, zT[:, :] if n == 0 else z_rest, z_part[n],
                                        ALU.subtract).then_inc(z_left, 1)

            def step(k, p):
                if is_group(k + 2):
                    slice_z(k + 2, p)
                if is_group(k - 2):
                    pool.wait_ge(second_ready, k - 1)
                    pass_gate(pool, gate)
                    nc.gpsimd.tensor_tensor(parts[:, 2, :, cols(k - 2)], left[p][:, :, :], parts[:, 1, :, cols(k - 2)],
                                            ALU.subtract).then_inc(third_ready, 1)
                if is_group(k - 1):
                    pool.wait_ge(first_ready, k)
                    pool.wait_ge(wt_ready, k)
                    pass_gate(pool, gate)
                    nc.gpsimd.tensor_tensor(left[1 - p][:, :, :], wt[:, :, cols(k - 1)], parts[:, 0, :, cols(k - 1)],
                                            ALU.subtract).then_inc(left_ready, 1)
            pipeline(pool, step, GROUPS + 2, ahead=2)

        @block.tensor
        def _(pe):
            def score(i, p):
                pe.wait_ge(sliced, i + 1)
                if not is_early(i):
                    pe.wait_ge(score_copied, i - 1)
                nc.tensor.matmul(ps[0:GT, p, 0:S_ * M_], zs[p][:, :], held["C"][:, :], start=True,
                                 stop=True).then_inc(scored, 1)

            score(0, 0)

            def step(k, p):
                if is_group(k + 1):
                    score(k + 1, 1 - p)
                if is_group(k - 1):
                    pe.wait_ge(weighed, k)
                    if not is_early(k - 1):
                        pe.wait_ge(wt_ready, k - 2)
                    for q in range(4):
                        last = nc.tensor.transpose(ps[:, 3 - p, q * GT:(q + 1) * GT],
                                                   ex[1 - p][:, 2 * q:2 * q + 2, :], held["ident"][0:GT, 0:GT])
                    last.then_inc(turned, 1)
            pipeline(pe, step, GROUPS + 1)

        @block.scalar
        def _(act):
            act.wait_ge(sentinels, 3)

            def copy_scores(i, p):
                act.wait_ge(scored, i + 1)
                if not is_early(i):
                    act.wait_ge(marked_ready, i - 1)
                nc.scalar.copy(sc[p][:, :, 0:M_], ps[0:GT, p, :].rearrange("t (s m) -> t s m", s=S_)).then_inc(
                    score_copied, 1)

            def round_z(n):
                if n > 0:
                    act.wait_ge(z_left, n)
                nc.scalar.copy(z_part[n], zT[:, :] if n == 0 else z_rest).then_inc(z_rounded, 1)

            round_z(0)
            copy_scores(0, 0)

            def step(k, p):
                if is_group(k + 1):
                    copy_scores(k + 1, 1 - p)
                if isinstance(k, int) and k < 2:
                    round_z(k + 1)
                if is_group(k):
                    act.wait_ge(centred, k + 1)
                    nc.scalar.activation(best_exp[p][:, :, :], best_exp[p][:, :, :], ACT.Exp)
                    nc.scalar.activation(ex[p][:, :, :], ex[p][:, :, :], ACT.Exp).then_inc(exp_ready, 1)
                if is_group(k - 1):
                    act.wait_ge(turned, k)
                    pass_gate(act, gate)
                    nc.scalar.copy(parts[:, 0, :, cols(k - 1)], wps(1 - p)).then_inc(first_ready, 1)
                    nc.scalar.copy(wt[:, :, cols(k - 1)], wps(1 - p)).then_inc(wt_ready, 1)
                if is_group(k - 2):
                    act.wait_ge(left_ready, k - 1)
                    pass_gate(act, gate)
                    nc.scalar.copy(parts[:, 1, :, cols(k - 2)], left[p][:, :, :]).then_inc(second_ready, 1)
            pipeline(act, step, GROUPS + 2)

        @block.vector
        def _(dve):
            dve.wait_ge(sentinels, 3)

            def mark(i, p):
                if not (isinstance(i, int) and i == 0):
                    dve.wait_ge(marked_ready, i)
                    dve.wait_ge(centred, i)
                dve.wait_ge(score_copied, i + 1)
                pass_gate(dve, gate)
                for s in range(S_):
                    last = nc.vector.max(best[:, s, :], sc[p][:, s, 0:M_])
                last.then_inc(best_ready, 1)
                dve.wait_ge(best_ready, i + 1)
                nc.vector.tensor_copy(wanted[:, :, 0:TOPK], best[:, :, 0:TOPK]).then_inc(wanted_ready, 1)
                if not is_early(i):
                    dve.wait_ge(turned, i - 1)
                nc.vector.tensor_tensor(best_exp[p][:, :, :], best[:, :, 0:TOPK], spread(best[:, :, 0], 2, TOPK),
                                        ALU.subtract)
                nc.vector.tensor_tensor(ex[p][:, :, :], sc[p][:, :, 0:M_],
                                        spread(best[:, :, 0], 2, M_), ALU.subtract).then_inc(centred, 1)
                dve.wait_ge(wanted_ready, i + 1)
                pass_gate(dve, gate)
                for s in range(S_):
                    last = nc.vector.match_replace(marked[p][:, s, :], wanted[:, s, :], sc[p][:, s, :], 2 * TAKEN)
                last.then_inc(marked_ready, 1)

            def weigh(i, p):
                dve.wait_ge(exp_ready, i + 1)
                if not (isinstance(i, int) and i == 0):
                    dve.wait_ge(weighed, i)
                nc.vector.reduce_sum(total[:, :], best_exp[p][:, :, :], AX.X).then_inc(total_ready, 1)
                dve.wait_ge(marked_ready, i + 1)
                nc.vector.scalar_tensor_tensor(ex[p][:, :, :], marked[p][:, :, 0:M_], TAKEN, ex[p][:, :, :], ALU.is_lt,
                                               ALU.mult).then_inc(picked, 1)
                dve.wait_ge(total_ready, i + 1)
                nc.vector.reciprocal(total[:, :], total[:, :]).then_inc(inverted, 1)
                dve.wait_ge(picked, i + 1)
                dve.wait_ge(inverted, i + 1)
                nc.vector.tensor_tensor(ex[p][:, :, :], ex[p][:, :, :],
                                        spread(total[:, :], 2, M_), ALU.mult).then_inc(weighed, 1)

            def step(k, p):
                if is_group(k):
                    mark(k, p)
                if is_group(k - 1):
                    weigh(k - 1, 1 - p)
            pipeline(dve, step, GROUPS + 1)

        @block.sync
        def _(sp):
            for n in range(3):
                sp.wait_ge(z_rounded, n + 1)
                sp.dma_start(scratch["z"][n], z_part[n]).then_inc(z_out, 16)
            sp.wait_ge(z_out, 3 * 16)
            for row, part in Z_ROWS:
                sp.dma_start(z_stack[row:row + R_, :, :],
                             scratch["z"][part].rearrange("(s r) t -> r s t", r=R_)).then_inc(stacked_z, 16)
            sp.dma_start(held["W2"][:], ins["W2"]).then_inc(w2_loaded, 16)
            for b in range(BL - 1):
                sp.wait_ge(third_ready, -(-(b + 1) * EB // GT))
                stack_weights(sp, parts, g_stack, stacked_g, b)


def stack_weights(sp, parts, g_stack, stacked_g, b):
    block_cols = slice(b * EB, (b + 1) * EB)
    if b:
        sp.wait_ge(stacked_g, b * G_TRANSFERS * 16)
    for n in range(3):
        for odd in range(2):
            for half in range(2):
                row = 64 * odd + 32 * half
                sp.dma_start(g_stack[32 * n:32 * n + 32, odd, half, :, block_cols],
                             parts[row:row + 32, n, :, block_cols]).then_inc(stacked_g, 16)


def run_experts(nc, sem, gate, sb, ps, held, z_stack, stacked_z, parts, g_stack, stacked_g, wt, w_stack, w2_loaded,
                comb):
    act_out = [sb(f"hidden{j}", [128, EB]) for j in range(4)]
    weighted = [[sb(f"hidden_weighted{q}_{j}", [128, EB]) for j in range(4)] for q in range(3)]
    w2s = [sb(f"w2_chunk{q}", [128, 4, 32]) for q in range(3)]
    h_done, gelu_done, w_done, mult_done, y_done = (sem("hidden_product"), sem("hidden_gelu"), sem("weight_spread"),
                                                    sem("hidden_weighted"), sem("second_product"))
    w2_ready, comb_copied = sem("w2_chunk_ready"), sem("comb_copied")
    SUMS = 7

    UNIT_START, CHUNK_START = 4, 3

    HALVES = 2 * BL

    def unit(half, c, j):
        return half * (4 * CH) + c * 4 + j

    def unit_is(done, eng, n):
        eng.wait_ge(done, n + (UNIT_START + 1))

    def chunk(half, c):
        return half * CH + c

    def chunk_is_summed(eng, n):
        eng.wait_ge(y_done, n + (CHUNK_START + 1))

    def walk(eng, step, opening=1, ending=0):
        for half in range(HALVES):
            for c in range(opening):
                step(half, c, buffer(half, c))
            with eng.Fori(0, (CH - opening - ending) // 3) as third:
                for r in range(opening, opening + 3):
                    step(half, third * 3 + r, buffer(half, r))
            for c in range(CH - ending, CH):
                step(half, c, buffer(half, c))

    def buffer(half, c):
        return (half + c) % 3

    def w_bank(q, j):
        return 4 + (q + j) % 3

    def token_cols(half):
        return slice((half // 2) * EB, (half // 2 + 1) * EB)

    with nc.Block() as block:
        @block.sync
        def _(sp):
            stack_weights(sp, parts, g_stack, stacked_g, BL - 1)

        @block.tensor
        def _(pe):
            def first(half, c, j):
                s = 4 * (half % 2) + j
                nc.tensor.matmul(ps[:, j, 0:EB], w_stack[:, s, bass.ds(c * 128, 128)],
                                 z_stack[:, s, token_cols(half)], start=True, stop=True).then_inc(h_done, 1)

            def spread_weights(half, c, q, j):
                unit_is(mult_done, pe, unit(half, c, j) - 3)
                s = 4 * (half % 2) + j
                rows = g_stack[:, s % 2, :, :, :].rearrange("p h s n -> p (h s n)")
                at = (c // 8) * (S_ // 2 * NT) + ((s // 2) * NT + (half // 2) * EB)
                nc.tensor.matmul(ps[:, w_bank(q, j), 0:EB], held["sel"][:, bass.ds((c % 8) * 128, 128)],
                                 rows[:, bass.ds(at, EB)], start=True, stop=True).then_inc(w_done, 1)

            def second(half, c, q):
                if isinstance(c, int) and chunk(half, c) == HALVES * CH - 1:
                    unit_is(mult_done, pe, unit(half, c, 3))
                pe.wait_ge(w2_ready, chunk(half, c) + 1)
                for j in range(4):
                    last = nc.tensor.matmul(ps[32 * j:32 * j + 32, SUMS, 0:EB], w2s[q][:, j, :], weighted[q][j][:, :],
                                            start=False, stop=False, skip_group_check=True)
                last.then_inc(y_done, 1)

            def open_sums(half, jj):
                if jj == 0 and half > 0:
                    pe.wait_ge(comb_copied, half)
                nc.tensor.matmul(ps[:, SUMS, 0:EB], held["b2"][:, 2 * (half % 2) + jj, :],
                                 wt[:, 2 * (half % 2) + jj, token_cols(half)], start=jj == 0, stop=False,
                                 skip_group_check=True)

            def step(half, c, q):
                opening, ending = isinstance(c, int) and c == 0, isinstance(c, int) and c == CH - 1
                if opening and half % 2 == 0:
                    pe.wait_ge(stacked_g, (half // 2 + 1) * (G_TRANSFERS * 16))
                for j in range(4):
                    spread_weights(half, c, q, j)
                    if j < 3:
                        first(half, c, j + 1)
                    elif not ending:
                        first(half, c + 1, 0)
                    elif half + 1 < HALVES:
                        first(half + 1, 0, 0)
                    if isinstance(c, int) and c == 1 and j < 2:
                        open_sums(half, j)
                    if j == 2:
                        if not opening:
                            second(half, c - 1, (q - 1) % 3)
                        elif half > 0:
                            second(half - 1, CH - 1, buffer(half - 1, CH - 1))

            pe.sem_inc(y_done, CHUNK_START)
            pe.wait_ge(stacked_z, 16 * len(Z_ROWS))
            first(0, 0, 0)
            walk(pe, step, opening=2, ending=2)
            second(HALVES - 1, CH - 1, buffer(HALVES - 1, CH - 1))

        @block.scalar
        def _(act):
            def step(half, c, q):
                for j in range(4):
                    n = unit(half, c, j)
                    act.wait_ge(h_done, n + 1)
                    unit_is(mult_done, act, n - 4)
                    nc.scalar.activation(act_out[j][:, :], ps[:, j, 0:EB], ACT.Gelu_apprx_tanh).then_inc(gelu_done, 1)
            act.sem_inc(gelu_done, UNIT_START)
            walk(act, step)

        @block.vector
        def _(dve):
            def copy_sums(half):
                chunk_is_summed(dve, chunk(half, CH - 1))
                nc.vector.tensor_scalar(comb[:, half % 2, token_cols(half)], ps[:, SUMS, 0:EB], 0.0, None,
                                        ALU.add).then_inc(comb_copied, 1)

            def step(half, c, q):
                for j in range(4):
                    if isinstance(c, int) and c == 0 and half > 0 and j == 3:
                        copy_sums(half - 1)
                    n = unit(half, c, j)
                    unit_is(gelu_done, dve, n)
                    dve.wait_ge(w_done, n + 1)
                    chunk_is_summed(dve, chunk(half, c) - 3)
                    nc.vector.tensor_tensor(weighted[q][j][:, :], act_out[j][:, :], ps[:, w_bank(q, j), 0:EB],
                                            ALU.mult).then_inc(mult_done, 1)
            dve.sem_inc(mult_done, UNIT_START)
            walk(dve, step)
            copy_sums(HALVES - 1)

        @block.gpsimd
        def _(pool):
            def step(half, c, q):
                chunk_is_summed(pool, chunk(half, c) - 3)
                pass_gate(pool, gate)
                nc.gpsimd.tensor_copy(w2s[q][:, :, :].rearrange("p k r -> p (k r)"), held["W2"][
                    :, bass.ds(((half % 2) * CH + c) * 128, 128)]).then_inc(w2_ready, 1)
            pool.wait_ge(w2_loaded, 16)
            walk(pool, step)


def quantised(nc, sem, gate, sb, ps, held, rounding, hT, out, V):
    win, wout = rounding.rounded_w

    ht = sb("h_tokens", [GT, GROUPS, E])
    x = sb("x_centred", [GT, GROUPS, E])
    xg = sb("x_gained", [GT, GROUPS, E])
    qb = sb("x_quantised", [GT, GROUPS * E], BF16)
    mean, ss, rstd, rms, amax, scale, dq = (sb(f"x_{n}", [GT, GROUPS]) for n in
                                            ("mean", "squares", "rstd", "rms", "max", "scale", "step"))
    ss2, rms2, amax2, scale2, dq2 = (sb(f"y_{n}", [GT, GROUPS]) for n in ("squares", "rms", "max", "scale", "step"))
    qt = [sb(f"x_quantised_t{p}", [EC, 2 * GT], BF16) for p in range(2)]
    sil = [sb(f"silu_gate{p}", [GT, FF]) for p in range(2)]
    y = [sb(f"y{p}", [GT, FF]) for p in range(2)]
    junk = sb("y_elementwise_squares", [GT, FF])
    yg = sb("y_gained", [GT, GROUPS * FF])
    yb = sb("y_quantised", [GT, GROUPS * FF], BF16)
    yt = [sb(f"y_quantised_t{p}", [128, 4 * GT], BF16) for p in range(2)]
    scaled = [sb(f"product_scaled{p}", [GT, E]) for p in range(2)]
    res = [sb(f"result{p}", [GT, E]) for p in range(2)]

    PAIRS = -(-GROUPS // 2)
    SEGMENTS = [(0, 4), (4, 8), (8, GROUPS)]
    ROUND_SEGMENTS = [(0, 1), (1, 4), (4, 8), (8, GROUPS)]
    turned, tokens, centred, squared = (sem("f1_turned"), sem("f1_tokens"), sem("f1_centred"), sem("f1_squared"))
    x_steps, x_gained, std_ready = sem("f1_x_steps"), sem("f1_x_gained"), sem("f1_std")
    mean_square, rms_ready, quantised_x = sem("f1_mean_square"), sem("f1_rms"), sem("f1_x_quantised")
    qt_ps, qt_sb, h_ps, silu_ready = sem("f1_qt_turned"), sem("f1_qt_copied"), sem("f1_h_product"), sem("f1_silu")
    y_ready, ss2_ready, gained, amax2_ready = sem("f1_y"), sem("f1_y_squares"), sem("f1_gained"), sem("f1_y_max")
    rms2_ready, y_steps, quantised_y = sem("f1_y_rms"), sem("f1_y_steps"), sem("f1_y_quantised")
    yt_ps, yt_sb, o_ps = sem("f1_yt_turned"), sem("f1_yt_copied"), sem("f1_o_product")
    scaled_ready, res_ready = sem("f1_scaled"), sem("f1_result")
    stored = [sem("stored_even"), sem("stored_odd")]

    def bank_bf16(rows, bank, width):
        return ps[0:rows, bank, :].bitcast(BF16)[:, 0:width]

    def column(t, i):
        return t[:, bass.ds(i, 1)]

    with nc.Block() as block:
        @block.tensor
        def _(pe):
            for j in range(PAIRS):
                for i in range(2 * j, min(2 * j + 2, GROUPS)):
                    for a in range(2):
                        at = (i % 2) * E + a * EC
                        last = nc.tensor.transpose(ps[0:GT, j, at:at + EC], hT[:, a, i * GT:(i + 1) * GT],
                                                   held["ident"][0:EC, 0:EC])
                last.then_inc(turned, 1)

            def turn_x(i, p):
                pe.wait_ge(quantised_x, i + 1)
                if not is_early(i):
                    pe.wait_ge(qt_sb, i - 1)
                for a in range(2):
                    last = nc.tensor.transpose(bank_bf16(EC, 6 + p, 2 * GT)[:, a * GT:(a + 1) * GT],
                                               qb[:, bass.ds(i * E + a * EC, EC)], held["identb"][0:GT, 0:GT])
                last.then_inc(qt_ps, 1)

            pe.wait_ge(tokens, PAIRS)
            turn_x(0, 0)

            def step(i, p):
                if not is_last(i):
                    turn_x(i + 1, 1 - p)
                pe.wait_ge(qt_sb, i + 1)
                if not is_early(i):
                    pe.wait_ge(y_ready, i - 1)
                for n in range(2):
                    for a in range(2):
                        last = nc.tensor.matmul(ps[0:GT, 2 * p + n, :], qt[p][:, a * GT:(a + 1) * GT],
                                                win[:, a, n * FF:(n + 1) * FF], start=a == 0, stop=a == 1)
                last.then_inc(h_ps, 1)
            over_groups(pe, step)

            def turn_y(i, p):
                pe.wait_ge(quantised_y, i + 1)
                if not is_early(i):
                    pe.wait_ge(yt_sb, i - 1)
                for a in range(4):
                    last = nc.tensor.transpose(bank_bf16(128, 4 + p, 4 * GT)[:, a * GT:(a + 1) * GT],
                                               yb[:, bass.ds(i * FF + a * 128, 128)], held["identb"][0:GT, 0:GT])
                last.then_inc(yt_ps, 1)

            turn_y(0, 0)

            def step(i, p):
                if not is_last(i):
                    turn_y(i + 1, 1 - p)
                pe.wait_ge(yt_sb, i + 1)
                if not is_early(i):
                    pe.wait_ge(scaled_ready, i - 1)
                for a in range(4):
                    last = nc.tensor.matmul(ps[0:GT, 6 + p, 0:E], yt[p][:, a * GT:(a + 1) * GT], wout[:, a, :],
                                            start=a == 0, stop=a == 3)
                last.then_inc(o_ps, 1)
            over_groups(pe, step)

        @block.scalar
        def _(act):
            for j in range(PAIRS):
                n = min(2, GROUPS - 2 * j)
                act.wait_ge(turned, j + 1)
                nc.scalar.copy(ht[:, 2 * j:2 * j + n, :].rearrange("t g e -> t (g e)"), ps[0:GT, j, 0:n * E]).then_inc(
                    tokens, 1)
            for k, (lo, hi) in enumerate(SEGMENTS):
                act.wait_ge(centred, k + 1)
                for i in range(lo, hi):
                    if i > 0:
                        act.wait_ge(squared, i)
                    nc.scalar.activation(junk[:, 0:E], x[:, i, :], ACT.Square, accum_out=ss[:, i:i + 1]).then_inc(
                        squared, 1)
            act.wait_ge(squared, GROUPS)
            nc.scalar.activation(rstd[:, :], ss[:, :], ACT.Sqrt, bias=V["rms_ln"][0:GT], scale=1.0 / E).then_inc(
                std_ready, 1)
            act.wait_ge(mean_square, 1)
            nc.scalar.activation(rms[:, :], rms[:, :], ACT.Sqrt, bias=V["rms_eps"][0:GT]).then_inc(rms_ready, 1)

            def copy_x(i, p):
                act.wait_ge(qt_ps, i + 1)
                if not is_early(i):
                    act.wait_ge(h_ps, i - 1)
                nc.scalar.copy(qt[p][:, :], bank_bf16(EC, 6 + p, 2 * GT)).then_inc(qt_sb, 1)

            copy_x(0, 0)

            def step(k, p):
                if is_group(k + 1):
                    copy_x(k + 1, 1 - p)
                if is_group(k):
                    act.wait_ge(h_ps, k + 1)
                    if not is_early(k):
                        act.wait_ge(y_ready, k - 1)
                    pass_gate(act, gate)
                    nc.scalar.activation(sil[p][:, :], ps[0:GT, 2 * p + 1, :], ACT.Silu, scale=column(dq, k)).then_inc(
                        silu_ready, 1)
                if is_group(k - 1):
                    act.wait_ge(y_ready, k)
                    if not (isinstance(k, int) and k == 1):
                        act.wait_ge(ss2_ready, k - 1)
                    pass_gate(act, gate)
                    nc.scalar.activation(junk[:, :], y[1 - p][:, :], ACT.Square, accum_out=column(ss2, k - 1)).then_inc(
                        ss2_ready, 1)
            pipeline(act, step, GROUPS + 1)

            act.wait_ge(ss2_ready, GROUPS)
            nc.scalar.activation(rms2[:, :], ss2[:, :], ACT.Sqrt, bias=V["rms_eps"][0:GT], scale=1.0 / FF).then_inc(
                rms2_ready, 1)

            def copy_y(i, p):
                act.wait_ge(yt_ps, i + 1)
                if not is_early(i):
                    act.wait_ge(o_ps, i - 1)
                nc.scalar.copy(yt[p][:, :], bank_bf16(128, 4 + p, 4 * GT)).then_inc(yt_sb, 1)

            copy_y(0, 0)

            def step(i, p):
                if not is_last(i):
                    copy_y(i + 1, 1 - p)
                act.wait_ge(o_ps, i + 1)
                if not is_early(i):
                    act.wait_ge(res_ready, i - 1)
                pass_gate(act, gate)
                nc.scalar.activation(scaled[p][:, :], ps[0:GT, 6 + p, 0:E], ACT.Identity,
                                     scale=column(dq2, i)).then_inc(scaled_ready, 1)
            over_groups(act, step)

        @block.vector
        def _(dve):
            def quantise(x, scale, q, steps, n, quantised):
                for lo, hi in ROUND_SEGMENTS:
                    seg = x[:, lo:hi, :]
                    nc.vector.tensor_tensor(seg, seg, spread(scale[:, lo:hi], 2, x.shape[2]), ALU.mult).then_inc(
                        steps, 1)
                    n += 1
                    dve.wait_ge(steps, n)
                    nc.vector.tensor_scalar(seg, seg, ROUND, ROUND + 127.0, ALU.add, ALU.min).then_inc(steps, 1)
                    n += 1
                    dve.wait_ge(steps, n)
                    nc.vector.tensor_scalar(q[:, lo:hi, :], seg, ROUND - 128.0, ROUND, ALU.max,
                                            ALU.subtract).then_inc(quantised, hi - lo)

            n = 0
            for k, (lo, hi) in enumerate(SEGMENTS):
                dve.wait_ge(tokens, (hi + 1) // 2)
                nc.vector.reduce_sum(mean[:, lo:hi], ht[:, lo:hi, :], AX.X).then_inc(x_steps, 1)
                n += 1
                dve.wait_ge(x_steps, n)
                nc.vector.tensor_scalar(mean[:, lo:hi], mean[:, lo:hi], 1.0 / E, None, ALU.mult).then_inc(x_steps, 1)
                n += 1
                dve.wait_ge(x_steps, n)
                nc.vector.tensor_tensor(x[:, lo:hi, :], ht[:, lo:hi, :], spread(mean[:, lo:hi], 2, E),
                                        ALU.subtract).then_inc(centred, 1)
            for k, (lo, hi) in enumerate(SEGMENTS):
                dve.wait_ge(x_gained, k + 1)
                nc.vector.tensor_reduce(amax[:, lo:hi], xg[:, lo:hi, :], AX.X, ALU.max,
                                        apply_absolute_value=True).then_inc(x_steps, 1)
                n += 1
            dve.wait_ge(std_ready, 1)
            nc.vector.reciprocal(rstd[:, :], rstd[:, :]).then_inc(x_steps, 1)
            n += 1
            dve.wait_ge(x_steps, n)
            nc.vector.scalar_tensor_tensor(rms[:, :], ss[:, :], 1.0 / E, rstd[:, :], ALU.mult, ALU.mult).then_inc(
                x_steps, 1)
            n += 1
            dve.wait_ge(x_steps, n)
            nc.vector.tensor_tensor(rms[:, :], rms[:, :], rstd[:, :], ALU.mult).then_inc(mean_square, 1)
            dve.wait_ge(rms_ready, 1)
            nc.vector.reciprocal(rms[:, :], rms[:, :]).then_inc(x_steps, 1)
            n += 1
            dve.wait_ge(x_steps, n)
            nc.vector.tensor_tensor(rms[:, :], rms[:, :], rstd[:, :], ALU.mult).then_inc(x_steps, 1)
            n += 1

            def step_sizes(amax, norm, scale, dq, k, steps, n):
                dve.wait_ge(steps, n)
                nc.vector.tensor_tensor(amax[:, :], amax[:, :], norm[:, :], ALU.mult).then_inc(steps, 1)
                dve.wait_ge(steps, n + 1)
                nc.vector.tensor_scalar(amax[:, :], amax[:, :], Q_EPS, None, ALU.max).then_inc(steps, 1)
                dve.wait_ge(steps, n + 2)
                nc.vector.tensor_scalar(dq[:, :], amax[:, :], rounding.step[0:GT, k:k + 1], 1.0 / 127.0, ALU.mult,
                                        ALU.mult).then_inc(steps, 1)
                nc.vector.reciprocal(scale[:, :], amax[:, :]).then_inc(steps, 1)
                dve.wait_ge(steps, n + 4)
                nc.vector.scalar_tensor_tensor(scale[:, :], scale[:, :], 127.0, norm[:, :], ALU.mult,
                                               ALU.mult).then_inc(steps, 1)
                dve.wait_ge(steps, n + 5)
                return n + 5

            n = step_sizes(amax, rms, scale, dq, 0, x_steps, n)
            quantise(xg, scale, qb[:, :].rearrange("t (g e) -> t g e", e=E), x_steps, n, quantised_x)

            def step(k, p):
                if is_group(k):
                    dve.wait_ge(silu_ready, k + 1)
                    if not is_early(k):
                        dve.wait_ge(ss2_ready, k - 1)
                        dve.wait_ge(gained, k - 1)
                    nc.vector.scalar_tensor_tensor(y[p][:, :], ps[0:GT, 2 * p, :], column(dq, k), sil[p][:, :],
                                                   ALU.mult, ALU.mult).then_inc(y_ready, 1)
                if is_group(k - 2):
                    dve.wait_ge(gained, k - 1)
                    pass_gate(dve, gate)
                    nc.vector.tensor_reduce(column(amax2, k - 2), yg[:, bass.ds((k - 2) * FF, FF)], AX.X, ALU.max,
                                            apply_absolute_value=True).then_inc(amax2_ready, 1)
            pipeline(dve, step, GROUPS + 2)

            dve.wait_ge(rms2_ready, 1)
            nc.vector.reciprocal(rms2[:, :], rms2[:, :]).then_inc(y_steps, 1)
            dve.wait_ge(amax2_ready, GROUPS)
            n = step_sizes(amax2, rms2, scale2, dq2, 1, y_steps, 1)
            quantise(yg[:, :].rearrange("t (g f) -> t g f", f=FF), scale2,
                     yb[:, :].rearrange("t (g f) -> t g f", f=FF), y_steps, n, quantised_y)

        @block.gpsimd
        def _(pool):
            for k, (lo, hi) in enumerate(SEGMENTS):
                pool.wait_ge(centred, k + 1)
                nc.gpsimd.tensor_tensor(xg[:, lo:hi, :], x[:, lo:hi, :], spread(held["gb_in"][0:GT, :], 1, hi - lo),
                                        ALU.mult).then_inc(x_gained, 1)

            def step(i, p):
                pool.wait_ge(y_ready, i + 1)
                pass_gate(pool, gate)
                nc.gpsimd.tensor_tensor(yg[:, bass.ds(i * FF, FF)], y[p][:, :], held["gb_out"][0:GT, :],
                                        ALU.mult).then_inc(gained, 1)
            over_groups(pool, step)

            def step(i, p):
                pool.wait_ge(scaled_ready, i + 1)
                if not is_early(i):
                    pool.wait_ge(stored[p], (i - p) * 8)
                pass_gate(pool, gate)
                nc.gpsimd.tensor_tensor(res[p][:, :], scaled[p][:, :], ht[:, :, :].rearrange("t g e -> t (g e)")[
                    :, bass.ds(i * E, E)], ALU.add).then_inc(res_ready, 1)
            over_groups(pool, step)

        @block.sync
        def _(sp):
            def step(i, p):
                sp.wait_ge(res_ready, i + 1)
                rows = GT if not is_last(i) else IMAGES * TOK - (GROUPS - 1) * GT
                sp.dma_start(out[bass.ds(i * GT, rows), :], res[p][0:rows, :]).then_inc(stored[p], 16)
            over_groups(sp, step)
            sp.wait_ge(stored[0], 16 * ((GROUPS + 1) // 2))
            sp.wait_ge(stored[1], 16 * (GROUPS // 2))



def laid_out(x, np, bf16):
    f = np.float32
    a = {k: np.asarray(v) for k, v in x.items()}
    out = {}
    z = lambda *s: np.zeros(s, f)
    xt = z(PK * 128, NT)
    xt[:, :IMAGES * TOK] = a["x"].reshape(IMAGES, 3, GRID, PATCH, GRID, PATCH).transpose(1, 3, 5, 0, 2, 4).reshape(
        PK * 128, IMAGES * TOK)
    out["xt"] = xt.reshape(PK, 128, NT).transpose(1, 0, 2)
    out["tok_w"] = a["L0_tok_W"].reshape(E, PK, 128).transpose(2, 1, 0)

    def rows(w):
        return w.reshape(2, EC, -1).transpose(1, 0, 2)

    def by_head(w):
        p = z(w.shape[0], HEADS, 32)
        p[:, :, :HD] = w.reshape(w.shape[0], HEADS, HD)
        return rows(p.reshape(w.shape[0], -1)).reshape(EC, 2, HG, 128)

    def by_head_rows(w):
        p = z(HG, 4, 32, E)
        p[:, :, :HD] = w.reshape(HG, 4, HD, E)
        return p.transpose(1, 2, 0, 3).reshape(128, HG, E)

    qkv = a["L0_attn_w_qkv"]
    out["wq0"], out["wk0"], out["wv0"] = by_head(qkv[:, :E]), by_head(qkv[:, E:2 * E]), rows(qkv[:, 2 * E:])
    out["wp0"] = by_head_rows(a["L0_attn_w_proj"])
    R0, C0, ONE, MAXREL = HD, HD + ROWS + 1, 30, 14
    kc = z(4, 32, TOK)
    kc[:, R0 + ROWS, 0] = kc[:, C0 + COLS, 0] = 1
    for t in range(TOK - 1):
        kc[:, R0 + t // COLS, 1 + t] = kc[:, C0 + t % COLS, 1 + t] = 1
    out["kconst"] = kc.reshape(128, TOK)

    def classes(tab, n, base, value_side, identity):
        m = z(n + 1, 4, 32, 4, 32)
        for k in range(n + 1):
            idx = [0 if k == n or j == n else min(max(j - k, -MAXREL), MAXREL) + MAXREL + 1 for j in range(n + 1)]
            for h in range(4):
                blk = tab[idx]
                if value_side:
                    m[k, h, base:base + n + 1, h, :HD] = blk
                else:
                    m[k, h, :HD, h, base:base + n + 1] = blk.T
                if identity:
                    m[k, h, range(HD), h, range(HD)] = 1
        return m.reshape(n + 1, 128, 128).transpose(1, 0, 2)

    out["av"] = classes(a["L0_attn_tab_vk"], ROWS, R0, False, True)
    out["ah"] = classes(a["L0_attn_tab_hk"], COLS, C0, False, False)
    out["bv"] = classes(a["L0_attn_tab_vv"], ROWS, R0, True, True)
    out["bh"] = classes(a["L0_attn_tab_hv"], COLS, C0, True, False)
    den_rows, den_back = z(4, 32, HG, 32), z(BL, 32, HG, 4, 32)
    for g in range(HG):
        for h in range(4):
            den_rows[h, ONE, g, 4 * g + h] = 1
            den_back[:, 4 * g + h, g, h, :] = 1
    den_rows[0, ONE, 0, HEADS:] = 1
    out["den_rows"] = den_rows.reshape(128, HG, 32)
    out["den_back"] = den_back.reshape(BL * 32, HG, 128)
    out["blocks4"] = np.repeat(np.eye(4, dtype=f), 32, axis=0)
    img = np.arange(GT) // TOK
    same = img[:, None] == img[None, :]
    causal = same & (np.arange(GT)[None, :] <= np.arange(GT)[:, None])
    out["mask0"] = np.tile(np.where(same, 0, NEG).astype(f), (1, 4)).astype(bf16)
    m1 = np.where(causal, 0, NEG).astype(f)
    m1 = np.concatenate([m1, z(GT, 1)], axis=1)
    out["mask1"] = np.tile(m1, (1, 4)).astype(bf16)
    v0 = z(GT, HEADS, 32)
    for t in range(GT):
        p = t % TOK
        v0[t, :, R0 + (ROWS if p == 0 else (p - 1) // COLS)] = 1
        v0[t, :, C0 + (COLS if p == 0 else (p - 1) % COLS)] = 1
    v0[:, :, ONE] = 1
    out["v_start0"] = v0
    v1 = z(GT + 1, HEADS, 32)
    v1[:, :, ONE] = 1
    out["v_start1"] = v1
    out["ones"] = np.full((EC, EC), 1.0 / E, f)
    out["all_ones"] = np.ones((128, 128), f)
    out["ident"] = np.eye(128, dtype=f)
    out["identb"] = np.eye(128, dtype=f).astype(bf16)
    out["P"] = rows(a["L0_ffn_P"].transpose(1, 0, 2).reshape(E, S_ * R_))
    C = z(S_, R_, S_, M_)
    b2 = z(2, M_, S_ // 2, 4, 32)
    for s in range(S_):
        C[s, :, s, :] = a["L0_ffn_C"][s].T
        b2[s % 2, :, s // 2, s % 4, :R_] = a["L0_ffn_b2"][s]
    out["C"] = C.reshape(128, S_ * M_)
    out["b2"] = b2.reshape(128, S_ // 2, 128)
    out["W1"] = np.concatenate([a["L0_ffn_W1"].transpose(0, 2, 1, 3).reshape(S_ * R_, M_ * H_),
                                a["L0_ffn_b1"].reshape(S_ * R_, -1)], axis=1)
    w2 = z(S_, CH, 128, 32)
    w2[..., :R_] = a["L0_ffn_W2"].reshape(S_, CH, 128, R_)
    out["W2"] = w2.reshape(2, 4, CH, 128, 32).transpose(3, 0, 2, 1, 4).reshape(128, -1)
    sel = z(3, 32, 8, 4, H_)
    for c in range(8):
        for m in range(4):
            sel[:, 4 * c + m, c, m, :] = 1
    out["sel"] = sel.reshape(96, 8 * 128).astype(bf16)
    g1 = z(4, 32, 2, G_)
    g1[:, :R_] = a["L0_ffn_G1"].reshape(2, 4, R_, G_).transpose(1, 2, 0, 3)
    out["G1"] = g1.reshape(128, 2, G_)
    out["G2"] = a["L0_ffn_G2"]
    w, bq = a["L1_attn_W_attn"], a["L1_attn_b_attn"]
    out["wq1"], out["wk1"], out["wv1"] = by_head(w[:, :E]), by_head(w[:, E:2 * E]), rows(w[:, 2 * E:])
    out["wp1"] = by_head_rows(a["L1_attn_W_proj"])
    out["vb1"] = np.broadcast_to(bq[2 * E:].reshape(1, HEADS, HD), (GT, HEADS, HD))
    rot = z(4, 32, 4, 32)
    cos, sin = z(4, 32, TOK), z(4, 32, TOK)
    freqs = (1.0 / np.float32(10000.0) ** (np.arange(0, HD, 2, dtype=f) / np.float32(HD))).astype(f)
    ang = np.outer(np.arange(TOK, dtype=f), freqs).astype(f)
    for d in range(HD):
        cos[:, d, :] = np.cos(ang[:, d // 2])
        sin[:, d, :] = np.sin(ang[:, d // 2])
    for h in range(4):
        for d in range(0, HD, 2):
            rot[h, d + 1, h, d] = -1
            rot[h, d, h, d + 1] = 1
    out["rot"] = rot.reshape(128, 128)
    cq = cos * f(HD ** -0.5)
    cq[:, 31] = 1
    out["cosq"], out["sinq"] = cq.reshape(128, TOK), (sin * f(HD ** -0.5)).reshape(128, TOK)
    out["cosk"], out["sink_"] = cos.reshape(128, TOK), sin.reshape(128, TOK)
    sk = z(4, 32, HG, 4)
    for h in range(4):
        sk[h, 31, :, h] = a["L1_attn_sinks"].reshape(HG, 4)[:, h]
    out["sinkcol"] = sk.reshape(128, HG, 4)
    out["gb_in"] = np.broadcast_to(a["L1_ffn_g_in"], (128, E))
    out["gb_out"] = np.broadcast_to(a["L1_ffn_g_out"], (128, FF))
    out["w_in"] = rows(a["L1_ffn_w_in"].T)
    out["w_out"] = a["L1_ffn_w_out"].T.reshape(4, 128, E).transpose(1, 0, 2)

    def by_head_vec(v, one=0):
        p = z(HG, 4, 32)
        p[..., :HD] = v.reshape(HG, 4, HD)
        p[..., 31] = one
        return p.reshape(HG, 128).T

    cols = {"tok_b": a["L0_tok_b"].reshape(2, EC).T, "ln_eps": np.full((128, 1), LN_EPS, f),
            "bp0": a["L0_attn_b_proj"].reshape(2, EC).T, "g2b": a["L0_ffn_g2b"].reshape(2, EC).T,
            "g1b": a["L0_ffn_g1b"].reshape(G_, 1), "norm_scale": a["L1_attn_norm_scale"].reshape(2, EC).T,
            "norm_bias": a["L1_attn_norm_bias"].reshape(2, EC).T, "bq1": by_head_vec(bq[:E], 1),
            "bk1": by_head_vec(bq[E:2 * E]), "bp1": a["L1_attn_b_proj"].reshape(2, EC).T,
            "rezero": np.broadcast_to(a["L1_attn_rezero"].reshape(1, 1), (128, 1)),
            "rms_eps": np.full((128, 1), RMS_EPS, f), "rms_ln": np.full((128, 1), LN_EPS, f)}
    vec = z(128, sum(k for _, k in VEC))
    at = 0
    for n, k in VEC:
        vec[:cols[n].shape[0], at:at + k] = cols[n]
        at += k
    out["vec"] = vec
    return out


def packed(arrays, np):
    out = {}
    for pack, names in PACKS.items():
        for tail, is_f32 in (("f", True), ("b", False)):
            chosen = [arrays[n] for n in names if (arrays[n].dtype == np.float32) == is_f32]
            if chosen:
                whole = np.zeros((128, sum(a[0].size for a in chosen)), chosen[0].dtype)
                at = 0
                for a in chosen:
                    whole[:a.shape[0], at:at + a[0].size] = a.reshape(a.shape[0], -1)
                    at += a[0].size
                out[f"pack_{pack}_{tail}"] = whole
    in_packs = {n for names in PACKS.values() for n in names}
    out.update({n: np.ascontiguousarray(a) for n, a in arrays.items() if n not in in_packs})
    return out



def kernel(**inputs):
    import numpy as _np
    import ml_dtypes as _ml
    import concourse.bacc as _bacc
    from concourse import mybir as _mybir
    from concourse.bass_utils import run_bass_kernel_spmd as _run

    nc = _bacc.Bacc("TRN2", target_bir_lowering=False, num_devices=1)
    views = laid_out(inputs, _np, _ml.bfloat16)
    shapes = {n: v.shape for n, v in views.items()}
    types = {n: _mybir.dt.from_np(v.dtype) for n, v in views.items()}
    arrays, args = {}, {}
    for name, a in packed(views, _np).items():
        arrays[f"in_{name}_dram"] = a
        args[name] = nc.dram_tensor(f"in_{name}_dram", a.shape, _mybir.dt.from_np(a.dtype), kind="ExternalInput").ap()
    out = nc.dram_tensor("out_0_dram", (IMAGES * TOK, E), F32, kind="ExternalOutput").ap()
    program(nc, args, shapes, types, out)
    r = _run(nc, [arrays], core_ids=[0])
    return r.results[0]["out_0_dram"].reshape(IMAGES, TOK, E)
```
